# Optimizing a Trainium2 kernel written in Bass

```python
import numpy as np
import jax
import jax.numpy as jnp

def _softmax(x, axis=-1):
    return jax.nn.softmax(x, axis=axis)

def _gelu(x):
    return jax.nn.gelu(x, approximate=True)

def _silu(x):
    return jax.nn.silu(x)

def _sigmoid(x):
    return jax.nn.sigmoid(x)

def _layernorm(x, axis=-1, eps=1e-05):
    m = jnp.mean(x, axis=axis, keepdims=True)
    v = jnp.var(x, axis=axis, keepdims=True)
    return (x - m) / jnp.sqrt(v + eps)

def _scatter_add(tgt, idx, src, axis=0):
    return tgt.at[idx].add(src)

def _segment_sum(src, seg, n):
    return jax.ops.segment_sum(src, seg, n)
kernel_name = 'mk_flamingo_gated_d4_seqx_r8_bdb028'

def setup_inputs(seed: int=0):
    np.random.seed(seed)
    _w = jnp.asarray

    def _rec_inputs():
        import jax
        import jax.numpy as jnp
        _rk = jax.random.key(seed)
        x = 7.22e-05 + 1 * jax.random.normal(jax.random.fold_in(_rk, 1), (128, 64, 128), jnp.float32)
        _lenS = 64 - jax.random.randint(jax.random.fold_in(_rk, 7), (128,), 0, max(1, 64 // 4) + 1, jnp.int32)
        _lenS2 = 64 - jax.random.randint(jax.random.fold_in(_rk, 8), (128,), 0, max(1, 64 // 4) + 1, jnp.int32)
        _ctx_1024P = jax.random.normal(jax.random.fold_in(_rk, 11), (128, 16, 128), jnp.float32)
        _ctx_1024c = jax.random.dirichlet(jax.random.fold_in(_rk, 511), 0.3 * jnp.ones((16,), jnp.float32), (128, 64))
        _ctx_1024t = jnp.einsum('bsk,bkd->bsd', _ctx_1024c, _ctx_1024P)
        _ctx_1024t = _ctx_1024t * jax.lax.rsqrt(jnp.mean(jnp.square(_ctx_1024t)) + 1e-12) * 0.953939
        ctx_1024 = 4.13588e-05 + 0.999923 * (_ctx_1024t + 0.3 * jax.random.normal(jax.random.fold_in(_rk, 611), (128, 64, 128), jnp.float32))
        _validS = jnp.arange(64)[None, :] < _lenS[:, None]
        _validS2 = jnp.arange(64)[None, :] < _lenS2[:, None]
        _causal = jnp.tril(jnp.ones((64, 64), dtype=bool))
        mask_BxSxS2_bf1 = jnp.ones((128, 64, 64), dtype=bool)
        _g = jax.random.normal(jax.random.fold_in(_rk, 9001), (2, 4), jnp.float32)
        _g = jnp.sign(_g) * jnp.maximum(jnp.abs(_g), 1.0) + (_g == 0) * 1.0
        g_xattn = _g[0]
        g_ffn = _g[1]
        return (x, ctx_1024, mask_BxSxS2_bf1, g_xattn, g_ffn)
    x, ctx_1024, mask_BxSxS2_bf1, g_xattn, g_ffn = _rec_inputs()

    def _L0_xattn_setup():
        import jax, jax.numpy as jnp
        import numpy as np
        DIM_IN, DIM_KEY, HEADS = (128, 64, 16)
        B, S = (4, 256)
        key = jax.random.key(seed)
        ks = jax.random.split(key, 7)
        scale_in = 1.0 / np.sqrt(DIM_IN)
        scale_hd = 1.0 / np.sqrt(HEADS * DIM_KEY)
        return {'q_in': jax.random.normal(ks[0], (B, S, DIM_IN), dtype=jnp.float32), 'k_in': jax.random.normal(ks[1], (B, S, DIM_IN), dtype=jnp.float32), 'v_in': jax.random.normal(ks[2], (B, S, DIM_IN), dtype=jnp.float32), 'Wq': jax.random.normal(ks[3], (DIM_IN, HEADS * DIM_KEY), dtype=jnp.float32) * scale_in, 'Wk': jax.random.normal(ks[4], (DIM_IN, HEADS * DIM_KEY), dtype=jnp.float32) * scale_in, 'Wv': jax.random.normal(ks[5], (DIM_IN, HEADS * DIM_KEY), dtype=jnp.float32) * scale_in, 'Wo': jax.random.normal(ks[6], (HEADS * DIM_KEY, DIM_IN), dtype=jnp.float32) * scale_hd}
    _L0_xattn_all = _L0_xattn_setup()
    _L0_xattn_in = {k: v for k, v in _L0_xattn_all.items() if k in ('Wq', 'Wk', 'Wv', 'Wo')}
    del _L0_xattn_all

    def _L0_ffn_setup():
        import jax, jax.numpy as jnp
        import numpy as np
        HIDDEN = 128
        FF = 512
        N_EXPERTS = 8
        CAP_FACTOR = 1.0
        B, S = (4, 256)
        STD = 0.02

        def _gelu(x):
            return x * 0.5 * (1.0 + jax.lax.erf(x / 1.41421))
        key = jax.random.key(seed)
        ks = jax.random.split(key, 6)
        x = jax.random.normal(ks[0], (B, S, HIDDEN), dtype=jnp.float32)
        W_sw = jax.random.normal(ks[1], (HIDDEN, N_EXPERTS), dtype=jnp.float32) * STD
        b_sw = jnp.zeros((N_EXPERTS,), dtype=jnp.float32)
        W1 = jax.random.normal(ks[2], (N_EXPERTS, HIDDEN, FF), dtype=jnp.float32) * STD
        b1 = jnp.zeros((N_EXPERTS, FF), dtype=jnp.float32)
        W2 = jax.random.normal(ks[3], (N_EXPERTS, FF, HIDDEN), dtype=jnp.float32) * STD
        b2 = jnp.zeros((N_EXPERTS, HIDDEN), dtype=jnp.float32)
        return {'x': x, 'W_sw': W_sw, 'b_sw': b_sw, 'W1': W1, 'b1': b1, 'W2': W2, 'b2': b2}
    _L0_ffn_all = _L0_ffn_setup()
    _L0_ffn_in = {k: v for k, v in _L0_ffn_all.items() if k in ('W_sw', 'b_sw', 'W1', 'b1', 'W2', 'b2')}
    del _L0_ffn_all

    def _L1_xattn_setup():
        import jax, jax.numpy as jnp
        import numpy as np
        N_HEAD = 16
        D_MODEL = 128

        def _split_heads(x, n_head):
            b, s, d = x.shape
            return x.reshape(b, s, n_head, d // n_head).transpose(0, 2, 1, 3)
        key = jax.random.key(seed)
        ks = jax.random.split(key, 11)
        B, S, D = (4, 256, D_MODEL)
        scale = 1.0 / np.sqrt(D)
        inp = {'q': jax.random.normal(ks[0], (B, S, D), jnp.float32), 'k': jax.random.normal(ks[1], (B, S, D), jnp.float32), 'v': jax.random.normal(ks[2], (B, S, D), jnp.float32), 'wq': jax.random.normal(ks[3], (D, D), jnp.float32) * scale, 'bq': jax.random.normal(ks[4], (D,), jnp.float32) * scale, 'wk': jax.random.normal(ks[5], (D, D), jnp.float32) * scale, 'bk': jax.random.normal(ks[6], (D,), jnp.float32) * scale, 'wv': jax.random.normal(ks[7], (D, D), jnp.float32) * scale, 'bv': jax.random.normal(ks[8], (D,), jnp.float32) * scale, 'wo': jax.random.normal(ks[9], (D, D), jnp.float32) * scale, 'bo': jax.random.normal(ks[10], (D,), jnp.float32) * scale}
        return inp
    _L1_xattn_all = _L1_xattn_setup()
    _L1_xattn_in = {k: v for k, v in _L1_xattn_all.items() if k in ('wq', 'bq', 'wk', 'bk', 'wv', 'bv', 'wo', 'bo')}
    del _L1_xattn_all

    def _L1_ffn_setup():
        import jax, jax.numpy as jnp
        import numpy as np
        EPS = 1e-05

        def rmsnorm(x):
            return x * jax.lax.rsqrt(jnp.mean(x * x, axis=-1, keepdims=True) + EPS)

        def act_quant(x):
            scale = 127.0 / jnp.clip(jnp.max(jnp.abs(x), axis=-1, keepdims=True), 1e-05)
            q = jnp.clip(jnp.round(x * scale), -128.0, 127.0) / scale
            return x + jax.lax.stop_gradient(q - x)

        def weight_quant(w):
            scale = 1.0 / jnp.clip(jnp.mean(jnp.abs(w)), 1e-05)
            q = jnp.clip(jnp.round(w * scale), -1.0, 1.0) / scale
            return w + jax.lax.stop_gradient(q - w)

        def bitlinear(x, w, b):
            xq = act_quant(rmsnorm(x))
            wq = weight_quant(w)
            return jnp.einsum('bsd,fd->bsf', xq, wq) + b
        key = jax.random.key(seed)
        k0, k1, k2 = jax.random.split(key, 3)
        B, S, D, F = (2, 1024, 128, 512)
        x = jax.random.normal(k0, (B, S, D), dtype=jnp.float32)
        w1 = jax.random.normal(k1, (F, D), dtype=jnp.float32) * (1.0 / np.sqrt(D))
        b1 = jnp.zeros((F,), dtype=jnp.float32)
        w2 = jax.random.normal(k2, (D, F), dtype=jnp.float32) * (1.0 / np.sqrt(F))
        b2 = jnp.zeros((D,), dtype=jnp.float32)
        return {'x': x, 'w1': w1, 'b1': b1, 'w2': w2, 'b2': b2}
    _L1_ffn_all = _L1_ffn_setup()
    _L1_ffn_in = {k: v for k, v in _L1_ffn_all.items() if k in ('w1', 'b1', 'w2', 'b2')}
    del _L1_ffn_all

    def _L2_xattn_setup():
        import jax, jax.numpy as jnp
        import numpy as np
        D_MODEL = 128
        KEY_DIM = 128
        VALUE_DIM = 128
        N_HEADS = 16
        key = jax.random.key(seed)
        ks = jax.random.split(key, 12)
        B, S = (4, 256)
        s = 0.02
        return {'queries': jax.random.normal(ks[0], (B, S, D_MODEL), jnp.float32), 'keys': jax.random.normal(ks[1], (B, S, D_MODEL), jnp.float32), 'values': jax.random.normal(ks[2], (B, S, D_MODEL), jnp.float32), 'masks': jnp.ones((B, S, S), dtype=bool), 'Wq': jax.random.normal(ks[3], (D_MODEL, KEY_DIM), jnp.float32) * s, 'bq': jnp.zeros((KEY_DIM,), jnp.float32), 'Wk': jax.random.normal(ks[4], (D_MODEL, KEY_DIM), jnp.float32) * s, 'bk': jnp.zeros((KEY_DIM,), jnp.float32), 'Wv': jax.random.normal(ks[5], (D_MODEL, VALUE_DIM), jnp.float32) * s, 'bv': jnp.zeros((VALUE_DIM,), jnp.float32), 'Wo': jax.random.normal(ks[6], (VALUE_DIM, D_MODEL), jnp.float32) * s, 'bo': jnp.zeros((D_MODEL,), jnp.float32)}
    _L2_xattn_all = _L2_xattn_setup()
    _L2_xattn_in = {k: v for k, v in _L2_xattn_all.items() if k in ('Wq', 'bq', 'Wk', 'bk', 'Wv', 'bv', 'Wo', 'bo')}
    del _L2_xattn_all

    def _L2_ffn_setup():
        import jax, jax.numpy as jnp
        import numpy as np
        TOP_K = 2
        key = jax.random.key(seed)
        k1, k2, k3, k4, k5 = jax.random.split(key, 5)
        B, S, D, F, E = (2, 128, 128, 256, 8)
        return {'x': jax.random.normal(k1, (B, S, D), dtype=jnp.float32), 'router_kernel_DE': jax.random.normal(k2, (D, E), dtype=jnp.float32) * 0.02, 'kernel_gating_EDF': jax.random.normal(k3, (E, D, F), dtype=jnp.float32) * 0.02, 'kernel_up_EDF': jax.random.normal(k4, (E, D, F), dtype=jnp.float32) * 0.02, 'kernel_down_EFD': jax.random.normal(k5, (E, F, D), dtype=jnp.float32) * 0.02}
    _L2_ffn_all = _L2_ffn_setup()
    _L2_ffn_in = {k: v for k, v in _L2_ffn_all.items() if k in ('router_kernel_DE', 'kernel_gating_EDF', 'kernel_up_EDF', 'kernel_down_EFD')}
    del _L2_ffn_all

    def _L3_xattn_setup():
        import jax, jax.numpy as jnp
        import numpy as np
        B, SQ, SKV, E, H = (4, 256, 256, 128, 16)
        HD = E // H

        def stablemax(x):
            s = jnp.where(x >= 0, x + 1.0, 1.0 / (1.0 - x))
            return s / jnp.sum(s, axis=-1, keepdims=True)
        key = jax.random.key(seed)
        ks = jax.random.split(key, 6)
        scale = 1.0 / np.sqrt(E)
        return {'query': jax.random.normal(ks[0], (B, SQ, E), jnp.float32), 'key_value': jax.random.normal(ks[1], (B, SKV, E), jnp.float32), 'Wq': jax.random.normal(ks[2], (E, E), jnp.float32) * scale, 'bq': jnp.zeros((E,), jnp.float32), 'Wk': jax.random.normal(ks[3], (E, E), jnp.float32) * scale, 'bk': jnp.zeros((E,), jnp.float32), 'Wv': jax.random.normal(ks[4], (E, E), jnp.float32) * scale, 'bv': jnp.zeros((E,), jnp.float32), 'Wo': jax.random.normal(ks[5], (E, E), jnp.float32) * scale, 'bo': jnp.zeros((E,), jnp.float32)}
    _L3_xattn_all = _L3_xattn_setup()
    _L3_xattn_in = {k: v for k, v in _L3_xattn_all.items() if k in ('Wq', 'bq', 'Wk', 'bk', 'Wv', 'bv', 'Wo', 'bo')}
    del _L3_xattn_all

    def _L3_ffn_setup():
        import jax, jax.numpy as jnp
        import numpy as np

        def _moe_forward(x, Wg, W1, b1, W2, b2):
            B, S, H = x.shape
            E = Wg.shape[1]
            tokens = x.reshape(-1, H)
            T = tokens.shape[0]
            C = -(-T // E)
            logits = tokens @ Wg
            gates = jax.nn.softmax(logits, axis=-1)
            idx = jnp.argmax(gates, axis=1)
            mask1 = jax.nn.one_hot(idx, E, dtype=gates.dtype)
            locations1 = jnp.cumsum(mask1, axis=0) - 1.0
            mask1 = mask1 * (locations1 < C).astype(gates.dtype)
            loc_s = jnp.sum(locations1 * mask1, axis=1).astype(jnp.int32)
            gates1 = jnp.sum(gates * mask1, axis=1)
            loc_oh = jax.nn.one_hot(loc_s, C, dtype=gates.dtype)
            dispatch = mask1[:, :, None] * loc_oh[:, None, :]
            combine = gates1[:, None, None] * dispatch
            expert_in = jnp.einsum('tec,th->ech', dispatch, tokens)
            hidden = jax.nn.relu(jnp.einsum('ech,ehf->ecf', expert_in, W1) + b1[:, None, :])
            expert_out = jnp.einsum('ecf,efh->ech', hidden, W2) + b2[:, None, :]
            out = jnp.einsum('tec,ech->th', combine, expert_out)
            return out.reshape(B, S, H)
        key = jax.random.key(seed)
        ks = jax.random.split(key, 6)
        B, S, H, F, E = (4, 256, 128, 512, 8)
        x = jax.random.normal(ks[0], (B, S, H), dtype=jnp.float32)
        Wg = jax.random.normal(ks[1], (H, E), dtype=jnp.float32) * (1.0 / np.sqrt(H))
        W1 = jax.random.normal(ks[2], (E, H, F), dtype=jnp.float32) * (1.0 / np.sqrt(H))
        b1 = jnp.zeros((E, F), dtype=jnp.float32)
        W2 = jax.random.normal(ks[3], (E, F, H), dtype=jnp.float32) * (1.0 / np.sqrt(F))
        b2 = jnp.zeros((E, H), dtype=jnp.float32)
        return {'x': x, 'Wg': Wg, 'W1': W1, 'b1': b1, 'W2': W2, 'b2': b2}
    _L3_ffn_all = _L3_ffn_setup()
    _L3_ffn_in = {k: v for k, v in _L3_ffn_all.items() if k in ('Wg', 'W1', 'b1', 'W2', 'b2')}
    del _L3_ffn_all
    return {'x': x, 'ctx_1024': ctx_1024, 'mask_BxSxS2_bf1': mask_BxSxS2_bf1, 'g_xattn': g_xattn, 'g_ffn': g_ffn, 'L0_xattn_Wq': _L0_xattn_in['Wq'], 'L0_xattn_Wk': _L0_xattn_in['Wk'], 'L0_xattn_Wv': _L0_xattn_in['Wv'], 'L0_xattn_Wo': _L0_xattn_in['Wo'], 'L0_ffn_W_sw': _L0_ffn_in['W_sw'], 'L0_ffn_b_sw': _L0_ffn_in['b_sw'], 'L0_ffn_W1': _L0_ffn_in['W1'], 'L0_ffn_b1': _L0_ffn_in['b1'], 'L0_ffn_W2': _L0_ffn_in['W2'], 'L0_ffn_b2': _L0_ffn_in['b2'], 'L1_xattn_wq': _L1_xattn_in['wq'], 'L1_xattn_bq': _L1_xattn_in['bq'], 'L1_xattn_wk': _L1_xattn_in['wk'], 'L1_xattn_bk': _L1_xattn_in['bk'], 'L1_xattn_wv': _L1_xattn_in['wv'], 'L1_xattn_bv': _L1_xattn_in['bv'], 'L1_xattn_wo': _L1_xattn_in['wo'], 'L1_xattn_bo': _L1_xattn_in['bo'], 'L1_ffn_w1': _L1_ffn_in['w1'], 'L1_ffn_b1': _L1_ffn_in['b1'], 'L1_ffn_w2': _L1_ffn_in['w2'], 'L1_ffn_b2': _L1_ffn_in['b2'], 'L2_xattn_Wq': _L2_xattn_in['Wq'], 'L2_xattn_bq': _L2_xattn_in['bq'], 'L2_xattn_Wk': _L2_xattn_in['Wk'], 'L2_xattn_bk': _L2_xattn_in['bk'], 'L2_xattn_Wv': _L2_xattn_in['Wv'], 'L2_xattn_bv': _L2_xattn_in['bv'], 'L2_xattn_Wo': _L2_xattn_in['Wo'], 'L2_xattn_bo': _L2_xattn_in['bo'], 'L2_ffn_router_kernel_DE': _L2_ffn_in['router_kernel_DE'], 'L2_ffn_kernel_gating_EDF': _L2_ffn_in['kernel_gating_EDF'], 'L2_ffn_kernel_up_EDF': _L2_ffn_in['kernel_up_EDF'], 'L2_ffn_kernel_down_EFD': _L2_ffn_in['kernel_down_EFD'], 'L3_xattn_Wq': _L3_xattn_in['Wq'], 'L3_xattn_bq': _L3_xattn_in['bq'], 'L3_xattn_Wk': _L3_xattn_in['Wk'], 'L3_xattn_bk': _L3_xattn_in['bk'], 'L3_xattn_Wv': _L3_xattn_in['Wv'], 'L3_xattn_bv': _L3_xattn_in['bv'], 'L3_xattn_Wo': _L3_xattn_in['Wo'], 'L3_xattn_bo': _L3_xattn_in['bo'], 'L3_ffn_Wg': _L3_ffn_in['Wg'], 'L3_ffn_W1': _L3_ffn_in['W1'], 'L3_ffn_b1': _L3_ffn_in['b1'], 'L3_ffn_W2': _L3_ffn_in['W2'], 'L3_ffn_b2': _L3_ffn_in['b2']}

def reference(x, ctx_1024, mask_BxSxS2_bf1, g_xattn, g_ffn, L0_xattn_Wq, L0_xattn_Wk, L0_xattn_Wv, L0_xattn_Wo, L0_ffn_W_sw, L0_ffn_b_sw, L0_ffn_W1, L0_ffn_b1, L0_ffn_W2, L0_ffn_b2, L1_xattn_wq, L1_xattn_bq, L1_xattn_wk, L1_xattn_bk, L1_xattn_wv, L1_xattn_bv, L1_xattn_wo, L1_xattn_bo, L1_ffn_w1, L1_ffn_b1, L1_ffn_w2, L1_ffn_b2, L2_xattn_Wq, L2_xattn_bq, L2_xattn_Wk, L2_xattn_bk, L2_xattn_Wv, L2_xattn_bv, L2_xattn_Wo, L2_xattn_bo, L2_ffn_router_kernel_DE, L2_ffn_kernel_gating_EDF, L2_ffn_kernel_up_EDF, L2_ffn_kernel_down_EFD, L3_xattn_Wq, L3_xattn_bq, L3_xattn_Wk, L3_xattn_bk, L3_xattn_Wv, L3_xattn_bv, L3_xattn_Wo, L3_xattn_bo, L3_ffn_Wg, L3_ffn_W1, L3_ffn_b1, L3_ffn_W2, L3_ffn_b2):
    import jax
    import jax.numpy as jnp

    def _L0_xattn_ref(q_in, k_in, v_in, Wq, Wk, Wv, Wo):
        import jax, jax.numpy as jnp
        import numpy as np
        DIM_IN, DIM_KEY, HEADS = (128, 64, 16)
        B, S = (4, 256)
        b, s, _ = q_in.shape

        def proj(x, W):
            return (x @ W).reshape(b, s, HEADS, DIM_KEY).transpose(0, 2, 1, 3)
        q, k, v = (proj(q_in, Wq), proj(k_in, Wk), proj(v_in, Wv))
        score = jnp.einsum('bhqd,bhkd->bhqk', q, k) / jnp.sqrt(jnp.float32(DIM_KEY))
        p = jax.nn.softmax(score, axis=-1)
        out = jnp.einsum('bhqk,bhkd->bhqd', p, v)
        out = out.transpose(0, 2, 1, 3).reshape(b, s, HEADS * DIM_KEY)
        return out @ Wo

    def _L0_ffn_ref(x, W_sw, b_sw, W1, b1, W2, b2):
        import jax, jax.numpy as jnp
        import numpy as np
        HIDDEN = 128
        FF = 512
        N_EXPERTS = 8
        CAP_FACTOR = 1.0
        B, S = (4, 256)
        STD = 0.02

        def _gelu(x):
            return x * 0.5 * (1.0 + jax.lax.erf(x / 1.41421))
        Bb, Ss, D = x.shape
        T = Bb * Ss
        E = W1.shape[0]
        capacity = int(CAP_FACTOR * T / E)
        xf = x.reshape(T, D)
        logits = xf @ W_sw + b_sw
        probs = jax.nn.softmax(logits, axis=-1)
        pmax = jnp.max(probs, axis=-1)
        routes = jnp.argmax(probs, axis=-1)
        factor = pmax / jax.lax.stop_gradient(pmax)
        xs = xf * factor[:, None]
        onehot = jax.nn.one_hot(routes, E, dtype=jnp.int32)
        pos = jnp.cumsum(onehot, axis=0) - 1
        pos_tok = jnp.take_along_axis(pos, routes[:, None], axis=1)[:, 0]
        keep = pos_tok < capacity
        pos_safe = jnp.where(keep, pos_tok, capacity)
        buf = jnp.zeros((E, capacity + 1, D), dtype=xs.dtype)
        buf = buf.at[routes, pos_safe].set(xs)
        buf = buf[:, :capacity]
        h = _gelu(jnp.einsum('ecd,edf->ecf', buf, W1) + b1[:, None, :])
        expert_out = jnp.einsum('ecf,efd->ecd', h, W2) + b2[:, None, :]
        gathered = expert_out[routes, jnp.minimum(pos_tok, capacity - 1)]
        final = jnp.where(keep[:, None], gathered, xs)
        return final.reshape(Bb, Ss, D)

    def _L1_xattn_ref(q, k, v, wq, bq, wk, bk, wv, bv, wo, bo):
        import jax, jax.numpy as jnp
        import numpy as np
        N_HEAD = 16
        D_MODEL = 128

        def _split_heads(x, n_head):
            b, s, d = x.shape
            return x.reshape(b, s, n_head, d // n_head).transpose(0, 2, 1, 3)
        qp = q @ wq.T + bq
        kp = k @ wk.T + bk
        vp = v @ wv.T + bv
        qh = _split_heads(qp, N_HEAD)
        kh = _split_heads(kp, N_HEAD)
        vh = _split_heads(vp, N_HEAD)
        dh = qh.shape[-1]
        score = jnp.einsum('bhqd,bhkd->bhqk', qh, kh) / jnp.sqrt(jnp.float32(dh))
        attn = jax.nn.softmax(score, axis=-1)
        out = jnp.einsum('bhqk,bhkd->bhqd', attn, vh)
        b, h, s, _ = out.shape
        out = out.transpose(0, 2, 1, 3).reshape(b, s, h * dh)
        return out @ wo.T + bo

    def _L1_ffn_ref(x, w1, b1, w2, b2):
        import jax, jax.numpy as jnp
        import numpy as np
        EPS = 1e-05

        def rmsnorm(x):
            return x * jax.lax.rsqrt(jnp.mean(x * x, axis=-1, keepdims=True) + EPS)

        def act_quant(x):
            scale = 127.0 / jnp.clip(jnp.max(jnp.abs(x), axis=-1, keepdims=True), 1e-05)
            q = jnp.clip(jnp.round(x * scale), -128.0, 127.0) / scale
            return x + jax.lax.stop_gradient(q - x)

        def weight_quant(w):
            scale = 1.0 / jnp.clip(jnp.mean(jnp.abs(w)), 1e-05)
            q = jnp.clip(jnp.round(w * scale), -1.0, 1.0) / scale
            return w + jax.lax.stop_gradient(q - w)

        def bitlinear(x, w, b):
            xq = act_quant(rmsnorm(x))
            wq = weight_quant(w)
            return jnp.einsum('bsd,fd->bsf', xq, wq) + b
        h = bitlinear(x, w1, b1)
        h = jax.nn.gelu(h, approximate=False)
        return bitlinear(h, w2, b2)

    def _L2_xattn_ref(queries, keys, values, masks, Wq, bq, Wk, bk, Wv, bv, Wo, bo):
        import jax, jax.numpy as jnp
        import numpy as np
        D_MODEL = 128
        KEY_DIM = 128
        VALUE_DIM = 128
        N_HEADS = 16
        B, S, _ = queries.shape
        H = N_HEADS
        dk = KEY_DIM // H
        dv = VALUE_DIM // H
        q = (queries @ Wq + bq).reshape(B, S, H, dk).transpose(0, 2, 1, 3)
        k = (keys @ Wk + bk).reshape(B, S, H, dk).transpose(0, 2, 1, 3)
        v = (values @ Wv + bv).reshape(B, S, H, dv).transpose(0, 2, 1, 3)
        scores = jnp.einsum('bhqd,bhkd->bhqk', q, k) / jnp.sqrt(jnp.float32(dk))
        scores = jnp.where(masks[:, None, :, :], scores, jnp.float32(-1000000000.0))
        attn = jax.nn.softmax(scores, axis=-1)
        out = jnp.einsum('bhqk,bhkd->bhqd', attn, v)
        cat = out.transpose(0, 2, 1, 3).reshape(B, S, VALUE_DIM)
        cat = cat.transpose(0, 2, 1).reshape(B, S, VALUE_DIM)
        return cat @ Wo + bo

    def _L2_ffn_ref(x, router_kernel_DE, kernel_gating_EDF, kernel_up_EDF, kernel_down_EFD):
        import jax, jax.numpy as jnp
        import numpy as np
        TOP_K = 2
        E = router_kernel_DE.shape[-1]
        x = x.astype(jnp.float32)
        logits_BSE = jnp.einsum('BSD,DE->BSE', x, router_kernel_DE)
        probs_BSE = jax.nn.softmax(logits_BSE.astype(jnp.float32), axis=-1)
        weights_BSK, indices_BSK = jax.lax.top_k(probs_BSE, TOP_K)
        norm_weights_BSK = jax.nn.softmax(weights_BSK, axis=-1)
        one_hot_BSKE = jax.nn.one_hot(indices_BSK, num_classes=E, dtype=x.dtype)
        full_weights_BSE = jnp.sum(one_hot_BSKE * norm_weights_BSK[..., None], axis=2)
        gating_BSEF = jnp.einsum('BSD,EDF->BSEF', x, kernel_gating_EDF)
        act_BSEF = jax.nn.silu(gating_BSEF)
        up_BSEF = jnp.einsum('BSD,EDF->BSEF', x, kernel_up_EDF)
        fuse_BSEF = act_BSEF * up_BSEF
        down_BSED = jnp.einsum('BSEF,EFD->BSED', fuse_BSEF, kernel_down_EFD)
        out_BSD = jnp.einsum('BSED,BSE->BSD', down_BSED, full_weights_BSE)
        return out_BSD.astype(jnp.float32)

    def _L3_xattn_ref(query, key_value, Wq, bq, Wk, bk, Wv, bv, Wo, bo):
        import jax, jax.numpy as jnp
        import numpy as np
        B, SQ, SKV, E, H = (4, 256, 256, 128, 16)
        HD = E // H

        def stablemax(x):
            s = jnp.where(x >= 0, x + 1.0, 1.0 / (1.0 - x))
            return s / jnp.sum(s, axis=-1, keepdims=True)
        b = query.shape[0]
        q = query @ Wq.T + bq
        k = key_value @ Wk.T + bk
        v = key_value @ Wv.T + bv
        q = q.reshape(b, -1, H, HD).transpose(0, 2, 1, 3)
        k = k.reshape(b, -1, H, HD).transpose(0, 2, 1, 3)
        v = v.reshape(b, -1, H, HD).transpose(0, 2, 1, 3)
        scores = jnp.einsum('bhqd,bhkd->bhqk', q, k) / np.sqrt(HD).astype(np.float32)
        attn = stablemax(scores)
        context = jnp.einsum('bhqk,bhkd->bhqd', attn, v)
        context = context.transpose(0, 2, 1, 3).reshape(b, -1, E)
        return context @ Wo.T + bo

    def _L3_ffn_ref(x, Wg, W1, b1, W2, b2):
        import jax, jax.numpy as jnp
        import numpy as np

        def _moe_forward(x, Wg, W1, b1, W2, b2):
            B, S, H = x.shape
            E = Wg.shape[1]
            tokens = x.reshape(-1, H)
            T = tokens.shape[0]
            C = -(-T // E)
            logits = tokens @ Wg
            gates = jax.nn.softmax(logits, axis=-1)
            idx = jnp.argmax(gates, axis=1)
            mask1 = jax.nn.one_hot(idx, E, dtype=gates.dtype)
            locations1 = jnp.cumsum(mask1, axis=0) - 1.0
            mask1 = mask1 * (locations1 < C).astype(gates.dtype)
            loc_s = jnp.sum(locations1 * mask1, axis=1).astype(jnp.int32)
            gates1 = jnp.sum(gates * mask1, axis=1)
            loc_oh = jax.nn.one_hot(loc_s, C, dtype=gates.dtype)
            dispatch = mask1[:, :, None] * loc_oh[:, None, :]
            combine = gates1[:, None, None] * dispatch
            expert_in = jnp.einsum('tec,th->ech', dispatch, tokens)
            hidden = jax.nn.relu(jnp.einsum('ech,ehf->ecf', expert_in, W1) + b1[:, None, :])
            expert_out = jnp.einsum('ecf,efh->ech', hidden, W2) + b2[:, None, :]
            out = jnp.einsum('tec,ech->th', combine, expert_out)
            return out.reshape(B, S, H)
        return _moe_forward(x, Wg, W1, b1, W2, b2)
    x = x + jnp.tanh(g_xattn[0]) * _L0_xattn_ref(_layernorm(x, axis=-1), ctx_1024, ctx_1024, L0_xattn_Wq, L0_xattn_Wk, L0_xattn_Wv, L0_xattn_Wo)
    x = x + jnp.tanh(g_ffn[0]) * _L0_ffn_ref(_layernorm(x, axis=-1), L0_ffn_W_sw, L0_ffn_b_sw, L0_ffn_W1, L0_ffn_b1, L0_ffn_W2, L0_ffn_b2)
    x = x + jnp.tanh(g_xattn[1]) * _L1_xattn_ref(_layernorm(x, axis=-1), ctx_1024, ctx_1024, L1_xattn_wq, L1_xattn_bq, L1_xattn_wk, L1_xattn_bk, L1_xattn_wv, L1_xattn_bv, L1_xattn_wo, L1_xattn_bo)
    x = x + jnp.tanh(g_ffn[1]) * _L1_ffn_ref(_layernorm(x, axis=-1), L1_ffn_w1, L1_ffn_b1, L1_ffn_w2, L1_ffn_b2)
    x = x + jnp.tanh(g_xattn[2]) * _L2_xattn_ref(_layernorm(x, axis=-1), ctx_1024, ctx_1024, mask_BxSxS2_bf1, L2_xattn_Wq, L2_xattn_bq, L2_xattn_Wk, L2_xattn_bk, L2_xattn_Wv, L2_xattn_bv, L2_xattn_Wo, L2_xattn_bo)
    x = x + jnp.tanh(g_ffn[2]) * _L2_ffn_ref(_layernorm(x, axis=-1), L2_ffn_router_kernel_DE, L2_ffn_kernel_gating_EDF, L2_ffn_kernel_up_EDF, L2_ffn_kernel_down_EFD)
    x = x + jnp.tanh(g_xattn[3]) * _L3_xattn_ref(_layernorm(x, axis=-1), ctx_1024, L3_xattn_Wq, L3_xattn_bq, L3_xattn_Wk, L3_xattn_bk, L3_xattn_Wv, L3_xattn_bv, L3_xattn_Wo, L3_xattn_bo)
    x = x + jnp.tanh(g_ffn[3]) * _L3_ffn_ref(_layernorm(x, axis=-1), L3_ffn_Wg, L3_ffn_W1, L3_ffn_b1, L3_ffn_W2, L3_ffn_b2)
    return x

_drawn_inputs = setup_inputs


def setup_inputs(seed=0):
    import zlib

    import numpy as np

    out = dict(_drawn_inputs(seed))
    spreads = {'L0_ffn_b_sw': (0.0, 0.1),
     'L0_ffn_b1': (0.0, 0.377),
     'L0_ffn_b2': (0.0, 0.1),
     'L1_ffn_b1': (0.0, 0.1),
     'L1_ffn_b2': (0.0, 0.1),
     'L2_xattn_bq': (0.0, 0.8),
     'L2_xattn_bk': (0.0, 2.0),
     'L2_xattn_bv': (0.0, 0.332),
     'L2_xattn_bo': (0.0, 0.1),
     'L3_xattn_bq': (0.0, 1.627),
     'L3_xattn_bk': (0.0, 2.0),
     'L3_xattn_bv': (0.0, 0.1),
     'L3_xattn_bo': (0.0, 0.1),
     'L3_ffn_b1': (0.0, 0.477),
     'L3_ffn_b2': (0.0, 0.344)}
    factors = {'L1_xattn_bk': 64.0,
     'L2_xattn_Wq': 8.0,
     'L2_xattn_Wk': 8.0,
     'L2_ffn_router_kernel_DE': 6.667,
     'L2_ffn_kernel_gating_EDF': 7.484,
     'L2_ffn_kernel_up_EDF': 7.24,
     'L2_ffn_kernel_down_EFD': 6.288}
    for name, (base, spread) in spreads.items():
        noise = np.random.default_rng([zlib.crc32(name.encode()), seed]).standard_normal(out[name].shape)
        drawn = base * np.exp(spread * noise) if base else spread * noise
        out[name] = jnp.asarray(drawn.astype(out[name].dtype))
    for name, factor in factors.items():
        out[name] = (out[name] * factor).astype(out[name].dtype)
    return out
```

```python
from contextlib import ExitStack

import numpy as np
import concourse.bass as bass
from concourse import mybir

P = 128
ALU = mybir.AluOpType
ACT = mybir.ActivationFunctionType
F32 = mybir.dt.float32
BF16 = mybir.dt.bfloat16
U8 = mybir.dt.uint8
I32 = mybir.dt.int32
U32 = mybir.dt.uint32
AX = mybir.AxisListType

BATCH, SEQ, D = 128, 64, 128
TOKENS = BATCH * SEQ
TILES = TOKENS // P
HEADS = 16
EXPERTS = 8
CAP = TOKENS // EXPERTS
FF = 512
FF2 = 256
SLOTS = 512
SUB = SLOTS // P
SLOT_TILES = TOKENS // SLOTS
TOP2_TILES = 2 * TOKENS // SLOTS + EXPERTS
LN_EPS = 1e-5
ERF_C = float(np.sqrt(2.0) / 1.41421)
MAGIC = 1.5 * 2.0 ** 23
BIG = 3.0e38

C_IDENT, C_TRI, C_ONES, C_JMASK, C_ECOL, C_BLK, C_ITEM = 0, 128, 256, 384, 388, 396, 412
C_COLS = C_ITEM + TOP2_TILES


def constants():
    c = np.zeros((P, C_COLS), np.float32)
    c[:, C_IDENT:C_IDENT + P] = np.eye(P)
    c[:, C_TRI:C_TRI + P] = np.triu(np.ones((P, P)))
    c[:, C_ONES:C_ONES + P] = 1.0
    for j in range(4):
        c[:, C_JMASK + j] = (np.arange(P) % 32) // 8 == j
    c[:, C_ECOL:C_ECOL + EXPERTS] = np.arange(EXPERTS)
    c[:, C_BLK:C_BLK + 16] = np.arange(16) * SLOTS
    c[:, C_ITEM:] = np.arange(TOP2_TILES)
    return c


class Step:

    def __init__(self, eng, items, t, i=None, unroll=2):
        self.eng, self.items, self.t, self.i, self.unroll = eng, items, t, i, unroll
        self.counts = {}

    def live(self, s):
        return self.i is not None or 0 <= self.t - s < self.items

    def par(self, s, buffers=2):
        return (self.t - s) % buffers

    def item(self, s):
        return self.t - s if self.i is None else self.i * self.unroll + (self.t - s)

    def done(self, s):
        if self.i is None:
            return max(0, min(self.t - s + 1, self.items))
        if s not in self.counts:
            self.counts[s] = self.eng.to_reg(self.i * self.unroll + (self.t - s + 1))
        return self.counts[s]

    def landed(self, s, dmas=1):
        if self.i is None:
            return 16 * dmas * ((self.t - s) // 2 + 1) if self.t >= s else 0
        return self.eng.to_reg(self.i * (8 * dmas * self.unroll) + 16 * dmas * ((self.t - s) // 2 + 1))


def pipeline(eng, items, depth, emit, unroll=2):
    first = -(-depth // unroll) * unroll
    for t in range(first):
        emit(Step(eng, items, t))
    with eng.Fori(0, (items - first) // unroll) as i:
        for k in range(unroll):
            emit(Step(eng, items, first + k, i, unroll))
    for t in range(items, items + depth - 1):
        emit(Step(eng, items, t))


def wait(eng, sem, count):
    if not (isinstance(count, int) and count <= 0):
        eng.wait_ge(sem, count)


class Phase:

    def __init__(self, nc, ctx, name):
        self.nc, self.ctx, self.name = nc, ctx, name
        self.held = []
        ctx.callback(self.clear)

    def clear(self):
        self.nc.clear_and_free_semaphores(self.held)
        self.nc.all_engine_barrier()

    def sb(self, name, shape, dt=F32):
        return self.ctx.enter_context(self.nc.sbuf_tensor(f"{self.name}_{name}", shape, dt))

    def ps(self, name, shape, dt=F32):
        return self.ctx.enter_context(self.nc.psum_tensor(f"{self.name}_{name}", shape, dt))

    def sem(self, name):
        self.held.append(self.nc.alloc_semaphore(f"{self.name}_{name}"))
        return self.held[-1]

    def sems(self, names):
        return [self.sem(n) for n in names.split()]



def load_inputs(nc, g, t):
    with ExitStack() as ctx:
        ph = Phase(nc, ctx, "setup")
        gates_raw = ph.sb("gates_raw", [P, 8])
        zeros = ph.sb("zeros", [P, 8 * D])
        loaded, zeroed, tanh_done, rows_zeroed, gates_in = ph.sems("loaded zeroed tanh_done rows_zeroed gates_in")
        block = ctx.enter_context(nc.Block())
        fills = [(g.slots0, TOKENS), (g.slots3, TOKENS), (g.slots2, TOP2_TILES * SLOTS)]

        @block.sync
        def _(sp):
            sp.dma_start(gates_raw[:, 0:4], t["g_xattn"].partition_broadcast(P)).then_inc(gates_in, 16)
            sp.dma_start(gates_raw[:, 4:8], t["g_ffn"].partition_broadcast(P)).then_inc(gates_in, 16)
            sp.dma_start(g.const[:, :], t["consts"]).then_inc(loaded, 16)
            sp.dma_start(g.x[:, :, :], t["x"].rearrange("(t p) d -> p t d", p=P)).then_inc(loaded, 16)
            sp.wait_ge(zeroed, 1)
            n = 0
            for rows, count in fills:
                view = rows.rearrange("(n p a) d -> n p (a d)", p=P, a=8)
                for k in range(count // (8 * P)):
                    sp.dma_start(view[k], zeros[:, :]).then_inc(rows_zeroed, 16)
                    n += 1
            sp.wait_ge(loaded, 32)
            sp.wait_ge(rows_zeroed, 16 * n)

        @block.scalar
        def _(act):
            act.wait_ge(gates_in, 32)
            nc.scalar.activation(g.gate[:, :], gates_raw[:, :], ACT.Tanh).then_inc(tanh_done, 1)

        @block.vector
        def _(dve):
            nc.vector.memset(zeros[:, :], 0.0).then_inc(zeroed, 1)
            nc.vector.memset(g.neg_half[:, :], -0.5).then_inc(tanh_done, 1)
            nc.vector.memset(g.eps[:, :], LN_EPS).then_inc(tanh_done, 1)
            dve.wait_ge(loaded, 32)
            nc.vector.tensor_copy(g.const_bf[:, :], g.const[:, 0:384]).then_inc(tanh_done, 1)



def attention_narrow(nc, g, name, gate_col, wq, bq, wk, bk, wv, bv, wo, bo, kind, mask=None):
    ITEMS, TPI = TILES // 2, 2
    SCALE = float(1.0 / np.sqrt(np.float32(8)))
    folded = kind == "masked"
    with ExitStack() as ctx:
        ph = Phase(nc, ctx, name)
        wq_s, wk_s, wv_s = ph.sb("wq", [P, D]), ph.sb("wk", [P, D]), ph.sb("wv", [P, 2, 64])
        wo_s = ph.sb("wo", [P, 2, 2, D]) if folded else ph.sb("wo", [P, D])
        bq_s, bk_s = ph.sb("bq", [P, 1]), ph.sb("bk", [P, 1])
        bv_s, bo_s = ph.sb("bv", [P, 64]), ph.sb("bo", [1, D])
        bq_scaled, bk_masked = ph.sb("bq_scaled", [P, 1]), ph.sb("bk_masked", [P, 4])
        ctx_t = ph.sb("ctx_t", [P, 2, 256])
        st, mv = ph.sb("st", [P, 2, TPI, 6]), ph.sb("mv", [P, 2, TPI, 2])
        var_eps, rstd = ph.sb("var_eps", [P, 2, TPI]), ph.sb("rstd", [P, 2, TPI])
        xn, xn_t = ph.sb("xn", [P, 2, TPI, D]), ph.sb("xn_t", [P, 2, 256])
        q_t, k_t = ph.sb("q_t", [P, 2, 256]), ph.sb("k_t", [P, 2, 4, 256])
        val = ph.sb("val", [P, 2, 4, 8, 18])
        prob = ph.sb("prob", [P, 2, 4, TPI, 4, 64])
        top = ph.sb("top", [P, 4, TPI, 4])
        prob_t = ph.sb("prob_t", [P, 16, P])
        recip = ph.sb("recip", [P, TPI, 8, 2])
        ctx_out, ctx_out_t = ph.sb("ctx_out", [P, TPI, D]), ph.sb("ctx_out_t", [P, TPI, P])
        soft = ph.sb("soft", [P, 4, TPI, 4, 64]) if kind == "stable" else None
        if mask is not None:
            mask_raw, limit = ph.sb("mask_raw", [P, TILES, 64], U8), ph.sb("limit", [P, TILES, 64])
        S = ph.ps("S", [P, 4, TPI, 4, 64])
        PT = ph.ps("PT", [P, 2, 512])
        A, B = ph.ps("A", [P, 512]), ph.ps("B", [P, 512])

        weights_in, ready = ph.sem("weights_in"), ph.sem("ready")
        ctx_in = [ph.sem(f"ctx_in{k}") for k in range(2)]
        (stats_part, stats_done, eps_done, rstd_done, xn_done, xt_filled, xt_drained, qk_filled, qk_drained,
         v_filled, v_drained, s_filled, s_drained, s_limited, top_done, shifted, prob_ready, relu_done, log_done, soft_done,
         o_filled, recip_done, o_drained, ot_filled, ot_drained, wo_filled, wo_drained) = ph.sems(
            "stats_part stats_done eps_done rstd_done xn_done xt_filled xt_drained qk_filled qk_drained "
            "v_filled v_drained s_filled s_drained s_limited top_done shifted prob_ready relu_done log_done soft_done "
            "o_filled recip_done o_drained ot_filled ot_drained wo_filled wo_drained")
        pt_filled = [ph.sem(f"pt_filled{k}") for k in range(4)]
        pt_drained = [ph.sem(f"pt_drained{k}") for k in range(4)]
        block = ctx.enter_context(nc.Block())
        LOADED = 16 * (11 + (mask is not None) + folded)
        READY = 5 + (mask is not None)
        DEPTH = 8
        ident = g.const[:, C_IDENT:C_IDENT + P]

        @block.sync
        def _(sp):
            sp.dma_start(wq_s[:, :], wq).then_inc(weights_in, 16)
            sp.dma_start(wk_s[:, :], wk).then_inc(weights_in, 16)
            sp.dma_start(wv_s[:, :, :], wv).then_inc(weights_in, 16)
            sp.dma_start(bq_s[:, :], bq).then_inc(weights_in, 16)
            sp.dma_start(bk_s[:, :], bk).then_inc(weights_in, 16)
            for h in range(2):
                sp.dma_start(bv_s[64 * h:64 * h + 64, :], bv[h].partition_broadcast(64)).then_inc(weights_in, 16)
            sp.dma_start(bo_s[:, :], bo).then_inc(weights_in, 16)
            if folded:
                sp.wait_ge(ready, 1)
                for b in range(2):
                    sp.dma_start(wo_s[64 * b:64 * b + 64, b, :, :], wo).then_inc(weights_in, 16)
                sp.dma_start(mask_raw[:, :, :], mask).then_inc(weights_in, 16)
            else:
                sp.dma_start(wo_s[:, :], wo).then_inc(weights_in, 16)
            for h in range(2):
                sp.dma_start(ctx_t[:, h, :], g.ctx_t[:, 256 * h:256 * h + 256]).then_inc(ctx_in[h], 16)
                sp.dma_start(g.scrap[h:h + 1, :], g.const[h:h + 1, 0:8]).then_inc(weights_in, 16)

            def step(t):
                done_v = t.done(4)
                if t.live(2):
                    wait(sp, v_filled, done_v)
                    sp.dma_start(ctx_t[:, t.par(2), :], g.ctx_t[:, bass.ds(t.item(2) * 256, 256)]).then_inc(
                        ctx_in[t.par(2)], 16)

            for t in range(4, DEPTH):
                step(Step(sp, ITEMS, t))
            with sp.Fori(0, (ITEMS - DEPTH) // 2) as i:
                for k in range(2):
                    step(Step(sp, ITEMS, DEPTH + k, i))
            for t in range(ITEMS, ITEMS + 2):
                step(Step(sp, ITEMS, t))

        @block.gpsimd
        def _(pool):
            def step(t):
                n0 = t.done(0)
                if t.live(0):
                    pool.wait_ge(ready, READY)
                    wait(pool, stats_done, n0)
                    nc.gpsimd.tensor_tensor(var_eps[:, t.par(0), :], mv[:, t.par(0), :, 1], g.eps[:, 0:TPI],
                                            ALU.add).then_inc(eps_done, 1)
                    pool.wait_ge(ready, READY)
                    wait(pool, eps_done, n0)
                    nc.gpsimd.tensor_tensor(rstd[:, t.par(0), :], var_eps[:, t.par(0), :], g.neg_half[:, 0:TPI],
                                            ALU.pow).then_inc(rstd_done, 1)

            pipeline(pool, ITEMS, 1, step)

        @block.vector
        def _(dve):
            n = nc.vector.memset(wo_s[:, :, :, :] if folded else bk_masked[:, :], 0.0).then_inc(ready, 1)
            nc.vector.memset(val[:, :, :, :, :], 0.0).then_inc(ready, 1)
            dve.wait_ge(ready, 2)
            for h in range(2):
                nc.vector.memset(val[64 * h:64 * h + 64, :, :, :, 16 + h:17 + h], 1.0).then_inc(s_limited, 1)
            dve.wait_ge(s_limited, 2)
            dve.wait_ge(weights_in, LOADED)
            nc.vector.tensor_scalar(bq_scaled[:, :], bq_s[:, :], SCALE, None, ALU.mult).then_inc(ready, 1)
            nc.vector.tensor_tensor(bk_masked[:, :], g.const[:, C_JMASK:C_JMASK + 4], bk_s[:, :].broadcast_to([P, 4]),
                                    ALU.mult).then_inc(ready, 1)
            if mask is not None:
                nc.vector.tensor_scalar(limit[:, :, :], mask_raw[:, :, :], BIG, -1.0e9, ALU.mult, ALU.add).then_inc(ready, 1)
            nc.vector.tensor_copy(recip[:, 0, 0, :], g.const[:, 0:2]).then_inc(ready, 1)

            def flat_all(s, t):
                return prob[:, t.par(s), :, :, :, :].rearrange("p r t j k -> p (r t j k)")

            def step(t):
                n0, n1, n3, n4, n6, n7 = (t.done(s) for s in (0, 1, 3, 4, 6, 7))

                def add_to_stream():
                    dve.wait_ge(ready, READY)
                    wait(dve, wo_filled, n7)
                    src = (A if folded else B)[:, 0:256]
                    xs = g.x[:, bass.ds(t.item(7) * 2, 2), :]
                    nc.vector.scalar_tensor_tensor(xs, src.rearrange("p (t d) -> p t d", t=2), g.gate[:, gate_col:gate_col + 1],
                                                   xs, ALU.mult, ALU.add).then_inc(wo_drained, 1)

                def copy_values():
                    dve.wait_ge(ready, READY)
                    wait(dve, v_filled, n4)
                    for h in range(2):
                        rows = slice(64 * h, 64 * h + 64)
                        last = nc.vector.tensor_tensor(
                            val[rows, t.par(4), :, :, 8 * h:8 * h + 8],
                            A[rows, 0:256].rearrange("p (b h c) -> p b h c", b=4, h=8),
                            bv_s[rows, :].rearrange("p (h c) -> p h c", h=8).unsqueeze(1).broadcast_to([64, 4, 8, 8]),
                            ALU.add)
                    last.then_inc(v_drained, 1)

                if folded and t.live(7):
                    add_to_stream()
                if t.live(6):
                    o = B[:, 0:288].rearrange("p (t h c) -> p t h c", t=2, h=8)
                    dve.wait_ge(ready, READY)
                    wait(dve, o_filled, n6)
                    nc.vector.reciprocal(recip[:, :, :, :], o[:, :, :, 16:18]).then_inc(recip_done, 1)
                    dve.wait_ge(ready, READY)
                    wait(dve, recip_done, n6)
                    for tile in range(2):
                        last = nc.vector.tensor_tensor(
                            ctx_out[:, tile, :].rearrange("p (h two c) -> p h two c", h=8, two=2),
                            o[:, tile, :, 0:16].rearrange("p h (two c) -> p h two c", two=2),
                            recip[:, tile, :, :].unsqueeze(3).broadcast_to([P, 8, 2, 8]), ALU.mult)
                    last.then_inc(o_drained, 1)
                if t.live(4):
                    pr = prob[:, t.par(4), :, :, :, :]
                    flat = pr.rearrange("p r t j k -> p (r t j) k")
                    src = S[:, :, :, :, :].rearrange("p r t j k -> p (r t j) k")
                    topf = top[:, :, :, :].rearrange("p r t j -> p (r t j)")
                    if kind == "stable":
                        dve.wait_ge(ready, READY)
                        wait(dve, relu_done, n4)
                        nc.vector.tensor_scalar(pr.rearrange("p r t j k -> p (r t j k)"),
                                                S[:, :, :, :, :].rearrange("p r t j k -> p (r t j k)"),
                                                0.0, None, ALU.max).then_inc(s_drained, 1)
                    else:
                        dve.wait_ge(ready, READY)
                        wait(dve, s_filled, n4)
                        if mask is not None:
                            for tile in range(2):
                                last = nc.vector.tensor_tensor(
                                    pr[:, :, tile, :, :], S[:, :, tile, :, :],
                                    limit[:, bass.ds(t.item(4) * 2 + tile, 1), :].unsqueeze(1).broadcast_to([P, 4, 4, 64]),
                                    ALU.min)
                            last.then_inc(s_drained, 1)
                            copy_values()
                            src = flat
                            dve.wait_ge(ready, READY)
                            wait(dve, s_drained, n4)
                        nc.vector.tensor_reduce(topf, src, AX.X, ALU.max).then_inc(top_done, 1)
                        dve.wait_ge(ready, READY)
                        wait(dve, top_done, n4)
                        last = nc.vector.tensor_tensor(flat, src, topf.unsqueeze(2).broadcast_to([P, 32, 64]), ALU.subtract)
                        last.then_inc(shifted if mask is not None else s_drained, 1)
                if t.live(4) and mask is None:
                    copy_values()
                if not folded and t.live(7):
                    add_to_stream()
                if t.live(1):
                    dve.wait_ge(ready, READY)
                    wait(dve, rstd_done, n1)
                    wait(dve, xt_filled, n3)
                    for tile in range(2):
                        last = nc.vector.tensor_scalar(
                            xn[:, t.par(1), tile, :].unsqueeze(1), g.x[:, bass.ds(t.item(1) * 2 + tile, 1), :],
                            mv[:, t.par(1), tile, 0:1], rstd[:, t.par(1), tile:tile + 1], ALU.subtract, ALU.mult)
                    last.then_inc(xn_done, 1)
                if t.live(0):
                    for tile in range(2):
                        last = nc.vector.bn_stats(st[:, t.par(0), tile, :], g.x[:, bass.ds(t.item(0) * 2 + tile, 1), :])
                    last.then_inc(stats_part, 1)
                    dve.wait_ge(ready, READY)
                    wait(dve, stats_part, n0)
                    for tile in range(2):
                        last = nc.vector.bn_aggr(mv[:, t.par(0), tile, :], st[:, t.par(0), tile, :])
                    last.then_inc(stats_done, 1)
                if t.live(4) and kind == "stable":
                    dve.wait_ge(ready, READY)
                    wait(dve, soft_done, n4)
                    nc.vector.tensor_tensor(flat_all(4, t), flat_all(4, t), soft[:, :, :, :, :].rearrange("p r t j k -> p (r t j k)"),
                                            ALU.add).then_inc(prob_ready, 1)

            pipeline(dve, ITEMS, DEPTH, step)

        @block.scalar
        def _(act):
            if kind == "stable":
                nc.scalar.preload_act_table_set("natural_log_exp_and_others")
            def step(t):
                n2, n3, n4, n5, n6 = t.done(2), t.done(3), t.done(4), t.done(5), t.done(6)
                if kind == "stable" and t.live(4):
                    act.wait_ge(ready, READY)
                    wait(act, s_filled, n4)
                    wait(act, prob_ready, n5)
                    nc.scalar.activation(soft[:, :, :, :, :].rearrange("p r t j k -> p (r t j k)"),
                                         S[:, :, :, :, :].rearrange("p r t j k -> p (r t j k)"), ACT.Relu,
                                         scale=-1.0).then_inc(relu_done, 1)
                if t.live(2):
                    act.wait_ge(ready, READY)
                    wait(act, xt_filled, n2)
                    nc.scalar.copy(xn_t[:, t.par(2), :], A[:, 0:256]).then_inc(xt_drained, 1)
                if t.live(3):
                    act.wait_ge(ready, READY)
                    wait(act, qk_filled, n3)
                    nc.scalar.activation(q_t[:, t.par(3), :], B[:, 0:256], ACT.Identity, bias=bq_scaled[:, :], scale=SCALE)
                    for j in range(4):
                        last = nc.scalar.activation(k_t[:, t.par(3), j, :], B[:, 256:512], ACT.Identity,
                                                    bias=bk_masked[:, j:j + 1], scale=g.const[:, C_JMASK + j:C_JMASK + j + 1])
                    last.then_inc(qk_drained, 1)
                if t.live(5):
                    for c in range(4):
                        act.wait_ge(ready, READY)
                        wait(act, pt_filled[c], n5)
                        nc.scalar.copy(prob_t[:, 4 * c:4 * c + 4, :], PT[:, c % 2, :].rearrange("p (a q) -> p a q", a=4)).then_inc(
                            pt_drained[c], 1)
                if t.live(6) and not folded:
                    act.wait_ge(ready, READY)
                    wait(act, ot_filled, n6)
                    nc.scalar.copy(ctx_out_t[:, :, :], A[:, 0:256].rearrange("p (t q) -> p t q", t=2)).then_inc(ot_drained, 1)
                if t.live(4):
                    flat = prob[:, t.par(4), :, :, :, :].rearrange("p r t j k -> p (r t j k)")
                    if kind == "stable":
                        sf = soft[:, :, :, :, :].rearrange("p r t j k -> p (r t j k)")
                        act.wait_ge(ready, READY)
                        wait(act, relu_done, n4)
                        nc.scalar.activation(sf, sf, ACT.Ln, bias=g.const[:, C_ONES:C_ONES + 1]).then_inc(log_done, 1)
                        act.wait_ge(ready, READY)
                        wait(act, log_done, n4)
                        nc.scalar.activation(sf, sf, ACT.Exp, scale=-1.0).then_inc(soft_done, 1)
                    else:
                        act.wait_ge(ready, READY)
                        wait(act, shifted if mask is not None else s_drained, n4)
                        nc.scalar.activation(flat, flat, ACT.Exp).then_inc(prob_ready, 1)

            pipeline(act, ITEMS, DEPTH, step)

        @block.tensor
        def _(pe):
            def step(t):
                n2, n3, n4, n5, n6, n7 = (t.done(s) for s in range(2, 8))
                n8 = t.done(8) if t.i is None else None
                context_landed = t.landed(3)
                def bank_read(*reads):
                    if t.i is None:
                        for sem, count in reads:
                            wait(pe, sem, count)

                if t.live(4):
                    pe.wait_ge(ready, READY)
                    wait(pe, qk_drained, n4)
                    wait(pe, s_drained, n5)
                    for tile in range(2):
                        for r in range(4):
                            for b in range(2):
                                rows = slice(32 * r, 32 * r + 32)
                                seq = slice(128 * tile + 64 * b, 128 * tile + 64 * b + 64)
                                last = nc.tensor.matmul(S[64 * b:64 * b + 64, r, tile, :, :], q_t[rows, t.par(4), seq],
                                                        k_t[rows, t.par(4), :, seq], start=True, stop=True)
                    last.then_inc(s_filled, 1)
                if t.live(2):
                    pe.wait_ge(ready, READY)
                    wait(pe, xn_done, n2)
                    wait(pe, wo_drained if folded else ot_drained, n7)
                    bank_read((xt_drained, n3), (v_drained, n5))
                    for tile in range(2):
                        last = nc.tensor.transpose(A[:, P * tile:P * tile + P], xn[:, t.par(2), tile, :], ident)
                    last.then_inc(xt_filled, 1)
                if t.live(3):
                    pe.wait_ge(ready, READY)
                    wait(pe, xt_drained, n3)
                    wait(pe, ctx_in[t.par(3)], context_landed)
                    wait(pe, o_drained, n6)
                    bank_read((qk_drained, n4), (wo_drained, n8))
                    nc.tensor.matmul(B[:, 0:256], wq_s[:, :], xn_t[:, t.par(3), :], start=True, stop=True)
                    nc.tensor.matmul(B[:, 256:512], wk_s[:, :], ctx_t[:, t.par(3), :], start=True, stop=True).then_inc(
                        qk_filled, 1)

                def transpose_probabilities(c):
                    pe.wait_ge(ready, READY)
                    wait(pe, prob_ready, n5)
                    wait(pe, pt_drained[(c + 2) % 4], n6 if c < 2 else n5)
                    for a in range(4):
                        last = nc.tensor.transpose(
                            PT[:, c % 2, P * a:P * a + P],
                            prob[:, t.par(5), c, a // 2, 2 * (a % 2):2 * (a % 2) + 2, :].rearrange("p j k -> p (j k)"), ident)
                    last.then_inc(pt_filled[c], 1)

                if t.live(5):
                    transpose_probabilities(0)
                    transpose_probabilities(1)
                if t.live(4):
                    pe.wait_ge(ready, READY)
                    wait(pe, xt_drained, n2)
                    bank_read((v_drained, n5), (wo_drained if folded else ot_drained, n7))
                    for b in range(4):
                        for h in range(2):
                            last = nc.tensor.matmul(A[64 * h:64 * h + 64, 64 * b:64 * b + 64],
                                                    ctx_t[:, t.par(4), 64 * b:64 * b + 64], wv_s[:, h, :],
                                                    start=True, stop=True)
                    last.then_inc(v_filled, 1)
                if t.live(7) and not folded:
                    pe.wait_ge(ready, READY)
                    wait(pe, ot_drained, n7)
                    wait(pe, qk_drained, n3)
                    bank_read((o_drained, n6), (wo_drained, n8))
                    nc.tensor.matmul(B[:, 0:256], g.const[0:1, C_ONES:C_ONES + P], bo_s[:, :].unsqueeze(1).broadcast_to([1, 2, D]),
                                     start=True, stop=False)
                    for tile in range(2):
                        last = nc.tensor.matmul(B[:, P * tile:P * tile + P], ctx_out_t[:, tile, :], wo_s[:, :],
                                                start=False, stop=tile == 1)
                    last.then_inc(wo_filled, 1)
                if t.live(5):
                    transpose_probabilities(2)
                    transpose_probabilities(3)
                if t.live(6):
                    pe.wait_ge(ready, READY)
                    wait(pe, o_drained, n6)
                    wait(pe, v_drained, n4)
                    bank_read((xt_drained, n2), (wo_drained if folded else ot_drained, n7))
                    if folded:
                        for b in range(2):
                            out = A[64 * b:64 * b + 64, 0:256]
                            nc.tensor.matmul(out, g.const[0:1, C_ONES:C_ONES + 64], bo_s[:, :].unsqueeze(1).broadcast_to([1, 2, D]),
                                             start=True, stop=False)
                            for tile in range(2):
                                for c in range(2):
                                    last = nc.tensor.matmul(out[:, P * tile:P * tile + P], ctx_out[:, tile, c:P:2],
                                                            wo_s[:, b, c, :], start=False, stop=(tile, c) == (1, 1))
                        last.then_inc(wo_filled, 1)
                    else:
                        for tile in range(2):
                            last = nc.tensor.transpose(A[:, P * tile:P * tile + P], ctx_out[:, tile, :], ident)
                        last.then_inc(ot_filled, 1)
                if t.live(5):
                    pe.wait_ge(ready, READY)
                    wait(pe, pt_drained[2], n5)
                    wait(pe, pt_drained[3], n5)
                    wait(pe, v_drained, n5)
                    if folded:
                        wait(pe, qk_drained, n3)
                    else:
                        wait(pe, wo_drained, n7)
                    bank_read((qk_drained, n3), (o_drained, n6))
                    for tile in range(2):
                        for b in range(2):
                            for hp in range(8):
                                col = 144 * tile + 18 * hp
                                last = nc.tensor.matmul(
                                    B[64 * b:64 * b + 64, col:col + 18],
                                    prob_t[:, 4 * (hp // 2) + 2 * tile + hp % 2, 64 * b:64 * b + 64],
                                    val[:, t.par(5), 2 * tile + b, hp, :], start=True, stop=True)
                    last.then_inc(o_filled, 1)

            pipeline(pe, ITEMS, DEPTH, step)



def attention_wide(nc, g, t_in):
    ITEMS, DEPTH = TILES, 8
    SCALE = 1.0 / 8.0
    with ExitStack() as ctx:
        ph = Phase(nc, ctx, "l0")
        wq_s, wk_s = ph.sb("wq", [P, 8, P]), ph.sb("wk", [P, 8, P])
        wv_s, wo_s = ph.sb("wv", [P, 2, 512]), ph.sb("wo", [P, 8, D])
        ctx_t = ph.sb("ctx_t", [P, 2, P])
        st, mv = ph.sb("st", [P, 2, 6]), ph.sb("mv", [P, 2, 2])
        var_eps, rstd = ph.sb("var_eps", [P, 2]), ph.sb("rstd", [P, 2])
        xn, xn_t = ph.sb("xn", [P, 2, D]), ph.sb("xn_t", [P, 2, P])
        q_t, k_t = ph.sb("q_t", [P, 2, 8, P]), ph.sb("k_t", [P, 2, 8, P])
        val = ph.sb("val", [P, 2, 2, 8, 64])
        prob = ph.sb("prob", [P, 2, 8, 2, 64])
        top, total, recip = ph.sb("top", [P, 2, 8]), ph.sb("total", [P, 2, 8, 2]), ph.sb("recip", [P, 8, 2])
        prob_t = ph.sb("prob_t", [P, 8, P])
        ctx_out, ctx_out_t = ph.sb("ctx_out", [P, 8, 2, 64]), ph.sb("ctx_out_t", [P, 8, P])
        S, O = ph.ps("S", [P, 2, 8, 64]), ph.ps("O", [P, 2, 8, 64])
        R = ph.ps("R", [P, 4, 512])
        weights_in, ready = ph.sem("weights_in"), ph.sem("ready")
        ctx_in = [ph.sem(f"ctx_in{k}") for k in range(2)]
        (stats_part, stats_done, eps_done, rstd_done, xn_done, s_filled, s_drained, top_done, prob_ready,
         total_done, o_filled, recip_done, o_drained) = ph.sems(
            "stats_part stats_done eps_done rstd_done xn_done s_filled s_drained top_done prob_ready "
            "total_done o_filled recip_done o_drained")
        BANKS = [[("q0", 3), ("v0", 4), ("pt1", 5)], [("q1", 3), ("v1", 4), ("wo", 7)],
                 [("k0", 3), ("xt", 2), ("ot0", 6)], [("k1", 3), ("pt0", 5), ("ot1", 6)]]
        filled = {n: ph.sem(n + "_filled") for uses in BANKS for n, _ in uses}
        drained = {n: ph.sem(n + "_drained") for uses in BANKS for n, _ in uses}
        where = {n: b for b, uses in enumerate(BANKS) for n, _ in uses}
        ident = g.const[:, C_IDENT:C_IDENT + P]
        block = ctx.enter_context(nc.Block())

        @block.sync
        def _(sp):
            sp.dma_start(wq_s[:, :, :], t_in["L0_wq"].rearrange("d (c n) -> d c n", c=8)).then_inc(weights_in, 16)
            sp.dma_start(wk_s[:, :, :], t_in["L0_wk"].rearrange("d (c n) -> d c n", c=8)).then_inc(weights_in, 16)
            sp.dma_start(wv_s[:, :, :], t_in["L0_wv"]).then_inc(weights_in, 16)
            sp.dma_start(wo_s[:, :, :], t_in["L0_wo"].rearrange("(c p) d -> p c d", p=P)).then_inc(weights_in, 16)

            def step(t):
                values = t.done(4)
                if t.live(2):
                    wait(sp, filled["v1"], values)
                    sp.dma_start(ctx_t[:, t.par(2), :], g.ctx_t[:, bass.ds(t.item(2) * P, P)]).then_inc(ctx_in[t.par(2)], 16)

            pipeline(sp, ITEMS, DEPTH, step)

        @block.gpsimd
        def _(pool):
            def step(t):
                n0 = t.done(0)
                if t.live(0):
                    pool.wait_ge(ready, 1)
                    wait(pool, stats_done, n0)
                    nc.gpsimd.tensor_tensor(var_eps[:, t.par(0):t.par(0) + 1], mv[:, t.par(0), 1:2], g.eps[:, 0:1],
                                            ALU.add).then_inc(eps_done, 1)
                    pool.wait_ge(ready, 1)
                    wait(pool, eps_done, n0)
                    nc.gpsimd.tensor_tensor(rstd[:, t.par(0):t.par(0) + 1], var_eps[:, t.par(0):t.par(0) + 1],
                                            g.neg_half[:, 0:1], ALU.pow).then_inc(rstd_done, 1)

            pipeline(pool, ITEMS, 1, step)

        @block.vector
        def _(dve):
            dve.wait_ge(weights_in, 64)
            nc.vector.tensor_copy(recip[:, 0, :], g.const[:, 0:2]).then_inc(ready, 1)

            def step(t):
                n0, n1, n2, n3, n4, n5, n6, n7 = (t.done(s) for s in range(8))

                def copy_out(name, count, out):
                    dve.wait_ge(ready, 1)
                    wait(dve, filled[name], count)
                    nc.vector.tensor_copy(out, R[:, where[name], :].rearrange("p (c n) -> p c n", c=4)).then_inc(drained[name], 1)

                if t.live(6):
                    dve.wait_ge(ready, 1)
                    wait(dve, total_done, n6)
                    nc.vector.reciprocal(recip[:, :, :], total[:, t.par(6), :, :]).then_inc(recip_done, 1)
                    dve.wait_ge(ready, 1)
                    wait(dve, recip_done, n6)
                    wait(dve, o_filled, n6)
                    nc.vector.tensor_tensor(ctx_out[:, :, :, :], O[:, :, :, :].rearrange("p a h c -> p h a c"),
                                            recip[:, :, :].unsqueeze(3).broadcast_to([P, 8, 2, 64]), ALU.mult).then_inc(o_drained, 1)
                if t.live(1):
                    dve.wait_ge(ready, 1)
                    wait(dve, rstd_done, n1)
                    wait(dve, filled["xt"], n3)
                    nc.vector.tensor_scalar(xn[:, t.par(1), :].unsqueeze(1), g.x[:, bass.ds(t.item(1), 1), :],
                                            mv[:, t.par(1), 0:1], rstd[:, t.par(1):t.par(1) + 1],
                                            ALU.subtract, ALU.mult).then_inc(xn_done, 1)
                if t.live(0):
                    nc.vector.bn_stats(st[:, t.par(0), :], g.x[:, bass.ds(t.item(0), 1), :]).then_inc(stats_part, 1)
                    dve.wait_ge(ready, 1)
                    wait(dve, stats_part, n0)
                    nc.vector.bn_aggr(mv[:, t.par(0), :], st[:, t.par(0), :]).then_inc(stats_done, 1)
                if t.live(3):
                    copy_out("k1", n3, k_t[:, t.par(3), 4:8, :])
                if t.live(2):
                    dve.wait_ge(ready, 1)
                    wait(dve, filled["xt"], n2)
                    nc.vector.tensor_copy(xn_t[:, t.par(2), :], R[:, where["xt"], 0:P]).then_inc(drained["xt"], 1)
                if t.live(5):
                    dve.wait_ge(ready, 1)
                    wait(dve, prob_ready, n5)
                    nc.vector.tensor_reduce(total[:, t.par(5), :, :], prob[:, t.par(5), :, :, :], AX.X, ALU.add).then_inc(total_done, 1)
                if t.live(7):
                    dve.wait_ge(ready, 1)
                    wait(dve, filled["wo"], n7)
                    xs = g.x[:, bass.ds(t.item(7), 1), :]
                    nc.vector.scalar_tensor_tensor(xs, R[:, where["wo"], 0:D].unsqueeze(1), g.gate[:, 0:1], xs,
                                                   ALU.mult, ALU.add).then_inc(drained["wo"], 1)
                if t.live(4):
                    dve.wait_ge(ready, 1)
                    wait(dve, s_filled, n4)
                    nc.vector.tensor_reduce(top[:, :, :], S[:, :, :, :], AX.X, ALU.max).then_inc(top_done, 1)
                    dve.wait_ge(ready, 1)
                    wait(dve, top_done, n4)
                    nc.vector.tensor_tensor(prob[:, t.par(4), :, :, :].rearrange("p h a k -> p a h k"), S[:, :, :, :],
                                            top[:, :, :].unsqueeze(3).broadcast_to([P, 2, 8, 64]), ALU.subtract).then_inc(s_drained, 1)
                if t.live(6):
                    copy_out("ot1", n6, ctx_out_t[:, 4:8, :])

            pipeline(dve, ITEMS, DEPTH, step)

        @block.scalar
        def _(act):
            def step(t):
                n3, n4, n5, n6 = (t.done(s) for s in range(3, 7))

                def copy_out(name, count, out, scale=1.0):
                    act.wait_ge(ready, 1)
                    wait(act, filled[name], count)
                    nc.scalar.activation(out, R[:, where[name], :].rearrange("p (c n) -> p c n", c=out.shape[1]), ACT.Copy,
                                         scale=scale).then_inc(drained[name], 1)

                if t.live(3):
                    copy_out("q0", n3, q_t[:, t.par(3), 0:4, :], SCALE)
                    copy_out("q1", n3, q_t[:, t.par(3), 4:8, :], SCALE)
                    copy_out("k0", n3, k_t[:, t.par(3), 0:4, :])
                if t.live(4):
                    copy_out("v0", n4, val[:, t.par(4), 0, :, :])
                    copy_out("v1", n4, val[:, t.par(4), 1, :, :])
                if t.live(5):
                    copy_out("pt0", n5, prob_t[:, 0:4, :])
                    copy_out("pt1", n5, prob_t[:, 4:8, :])
                if t.live(6):
                    copy_out("ot0", n6, ctx_out_t[:, 0:4, :])
                if t.live(4):
                    flat = prob[:, t.par(4), :, :, :].rearrange("p h a k -> p (h a k)")
                    act.wait_ge(ready, 1)
                    wait(act, s_drained, n4)
                    nc.scalar.activation(flat, flat, ACT.Exp).then_inc(prob_ready, 1)

            pipeline(act, ITEMS, DEPTH, step)

        @block.tensor
        def _(pe):
            def step(t):
                n2, n3, n4, n5, n6, n7, n8 = (t.done(s) for s in range(2, 9))
                context_landed = t.landed(3)

                def claim(name):
                    uses = BANKS[where[name]]
                    at = [n for n, _ in uses].index(name)
                    before = uses[at - 1:at] if at else uses[-1:]
                    for n, s in (before if t.i is not None else uses):
                        wait(pe, drained[n], t.done(s) if n in [m for m, _ in uses[:at]] else t.done(s + 1))
                    return R[:, where[name], :]

                if t.live(3):
                    for c, (name, w, src) in enumerate((("q0", wq_s, xn_t), ("q1", wq_s, xn_t), ("k0", wk_s, ctx_t), ("k1", wk_s, ctx_t))):
                        pe.wait_ge(ready, 1)
                        if c == 0:
                            wait(pe, drained["xt"], n3)
                        if c == 2:
                            wait(pe, ctx_in[t.par(3)], context_landed)
                        bank = claim(name)
                        for k in range(4):
                            last = nc.tensor.matmul(bank[:, P * k:P * k + P], w[:, 4 * (c % 2) + k, :], src[:, t.par(3), :],
                                                    start=True, stop=True)
                        last.then_inc(filled[name], 1)
                if t.live(4):
                    for b in range(2):
                        pe.wait_ge(ready, 1)
                        bank = claim(f"v{b}")
                        for h in range(2):
                            last = nc.tensor.matmul(bank[64 * h:64 * h + 64, :], ctx_t[:, t.par(4), 64 * b:64 * b + 64],
                                                    wv_s[:, h, :], start=True, stop=True)
                        last.then_inc(filled[f"v{b}"], 1)
                if t.live(2):
                    pe.wait_ge(ready, 1)
                    wait(pe, xn_done, n2)
                    bank = claim("xt")
                    nc.tensor.transpose(bank[:, 0:P], xn[:, t.par(2), :], ident).then_inc(filled["xt"], 1)
                if t.live(5):
                    for c in range(2):
                        pe.wait_ge(ready, 1)
                        wait(pe, prob_ready, n5)
                        bank = claim(f"pt{c}")
                        for k in range(4):
                            last = nc.tensor.transpose(bank[:, P * k:P * k + P],
                                                       prob[:, t.par(5), 4 * c + k, :, :].rearrange("p a k -> p (a k)"), ident)
                        last.then_inc(filled[f"pt{c}"], 1)
                if t.live(7):
                    pe.wait_ge(ready, 1)
                    wait(pe, drained["ot1"], n7)
                    wait(pe, drained["ot0"], n7)
                    bank = claim("wo")
                    for k in range(8):
                        last = nc.tensor.matmul(bank[:, 0:D], ctx_out_t[:, k, :], wo_s[:, k, :], start=k == 0, stop=k == 7)
                    last.then_inc(filled["wo"], 1)
                if t.live(4):
                    pe.wait_ge(ready, 1)
                    wait(pe, drained["q1"], n4)
                    wait(pe, drained["k0"], n4)
                    wait(pe, drained["k1"], n4)
                    wait(pe, s_drained, n5)
                    for k in range(8):
                        for b in range(2):
                            for h in range(2):
                                rows = slice(64 * h, 64 * h + 64)
                                last = nc.tensor.matmul(S[64 * b:64 * b + 64, h, k, :], q_t[rows, t.par(4), k, 64 * b:64 * b + 64],
                                                        k_t[rows, t.par(4), k, 64 * b:64 * b + 64], start=True, stop=True)
                    last.then_inc(s_filled, 1)
                if t.live(6):
                    for c in range(2):
                        pe.wait_ge(ready, 1)
                        wait(pe, o_drained, n6)
                        bank = claim(f"ot{c}")
                        for k in range(4):
                            last = nc.tensor.transpose(bank[:, P * k:P * k + P],
                                                       ctx_out[:, 4 * c + k, :, :].rearrange("p a c -> p (a c)"), ident)
                        last.then_inc(filled[f"ot{c}"], 1)
                if t.live(5):
                    pe.wait_ge(ready, 1)
                    wait(pe, drained["pt0"], n5)
                    wait(pe, drained["pt1"], n5)
                    wait(pe, drained["v1"], n5)
                    wait(pe, o_drained, n6)
                    for k in range(8):
                        for b in range(2):
                            for h in range(2):
                                rows = slice(64 * h, 64 * h + 64)
                                last = nc.tensor.matmul(O[64 * b:64 * b + 64, h, k, :], prob_t[rows, k, 64 * b:64 * b + 64],
                                                        val[rows, t.par(5), b, k, :], start=True, stop=True)
                    last.then_inc(o_filled, 1)

            pipeline(pe, ITEMS, DEPTH, step)



def route(nc, g, name, w, b):
    ITEMS, DEPTH = TILES // 2, 5
    with ExitStack() as ctx:
        ph = Phase(nc, ctx, name)
        w_s, b_s = ph.sb("w", [P, EXPERTS]), ph.sb("b", [1, EXPERTS])
        st, mv = ph.sb("st", [P, 2, 2, 6]), ph.sb("mv", [P, 2, 2, 2])
        var_eps, rstd = ph.sb("var_eps", [P, 2, 2]), ph.sb("rstd", [P, 2, 2])
        xn, xn_t = ph.sb("xn", [P, 2, 2, D]), ph.sb("xn_t", [P, 2, 256])
        X, L = ph.ps("X", [P, 2, 512]), ph.ps("L", [P, 2, 512])
        weights_in = ph.sem("weights_in")
        stats_part, stats_done, eps_done, rstd_done, xn_done, xt_filled, xt_drained, l_filled, l_drained = ph.sems(
            "stats_part stats_done eps_done rstd_done xn_done xt_filled xt_drained l_filled l_drained")
        block = ctx.enter_context(nc.Block())
        LOADED = 16 if b is None else 32

        @block.sync
        def _(sp):
            sp.dma_start(w_s[:, :], w).then_inc(weights_in, 16)
            if b is not None:
                sp.dma_start(b_s[:, :], b).then_inc(weights_in, 16)

        @block.gpsimd
        def _(pool):
            def step(t):
                n0 = t.done(0)
                if t.live(0):
                    pool.wait_ge(weights_in, LOADED)
                    wait(pool, stats_done, n0)
                    nc.gpsimd.tensor_tensor(var_eps[:, t.par(0), :], mv[:, t.par(0), :, 1], g.eps[:, 0:2], ALU.add).then_inc(eps_done, 1)
                    pool.wait_ge(weights_in, LOADED)
                    wait(pool, eps_done, n0)
                    nc.gpsimd.tensor_tensor(rstd[:, t.par(0), :], var_eps[:, t.par(0), :], g.neg_half[:, 0:2],
                                            ALU.pow).then_inc(rstd_done, 1)

            pipeline(pool, ITEMS, 1, step)

        @block.vector
        def _(dve):
            def step(t):
                n0, n1, n3, n4 = t.done(0), t.done(1), t.done(3), t.done(4)
                if t.live(0):
                    for k in range(2):
                        last = nc.vector.bn_stats(st[:, t.par(0), k, :], g.x[:, bass.ds(t.item(0) * 2 + k, 1), :])
                    last.then_inc(stats_part, 1)
                    dve.wait_ge(weights_in, LOADED)
                    wait(dve, stats_part, n0)
                    for k in range(2):
                        last = nc.vector.bn_aggr(mv[:, t.par(0), k, :], st[:, t.par(0), k, :])
                    last.then_inc(stats_done, 1)
                if t.live(1):
                    dve.wait_ge(weights_in, LOADED)
                    wait(dve, rstd_done, n1)
                    wait(dve, xt_filled, n3)
                    for k in range(2):
                        for out in (g.xn[:, bass.ds(t.item(1) * 2 + k, 1), :], xn[:, t.par(1), k, :].unsqueeze(1)):
                            last = nc.vector.tensor_scalar(out, g.x[:, bass.ds(t.item(1) * 2 + k, 1), :],
                                                           mv[:, t.par(1), k, 0:1], rstd[:, t.par(1), k:k + 1],
                                                           ALU.subtract, ALU.mult)
                    last.then_inc(xn_done, 1)
                if t.live(4):
                    dve.wait_ge(weights_in, LOADED)
                    wait(dve, l_filled, n4)
                    nc.vector.tensor_copy(g.logits[:, bass.ds(t.item(4) * 2, 2), :],
                                          L[:, t.par(4), 0:16].rearrange("p (t e) -> p t e", t=2)).then_inc(l_drained, 1)

            pipeline(dve, ITEMS, DEPTH, step)

        @block.scalar
        def _(act):
            def step(t):
                n2 = t.done(2)
                if t.live(2):
                    act.wait_ge(weights_in, LOADED)
                    wait(act, xt_filled, n2)
                    nc.scalar.copy(xn_t[:, t.par(2), :], X[:, t.par(2), 0:256]).then_inc(xt_drained, 1)

            pipeline(act, ITEMS, DEPTH, step)

        @block.tensor
        def _(pe):
            def step(t):
                n2, n3, n4, n5 = (t.done(s) for s in range(2, 6))
                if t.live(2):
                    pe.wait_ge(weights_in, LOADED)
                    wait(pe, xn_done, n2)
                    wait(pe, xt_drained, n4)
                    for k in range(2):
                        last = nc.tensor.transpose(X[:, t.par(2), P * k:P * k + P], xn[:, t.par(2), k, :],
                                                   g.const[:, C_IDENT:C_IDENT + P])
                    last.then_inc(xt_filled, 1)
                if t.live(3):
                    pe.wait_ge(weights_in, LOADED)
                    wait(pe, xt_drained, n3)
                    wait(pe, l_drained, n5)
                    if b is not None:
                        nc.tensor.matmul(L[:, t.par(3), 0:16], g.const[0:1, C_ONES:C_ONES + P],
                                         b_s[:, :].unsqueeze(1).broadcast_to([1, 2, EXPERTS]), start=True, stop=False)
                    for k in range(2):
                        last = nc.tensor.matmul(L[:, t.par(3), 8 * k:8 * k + 8], xn_t[:, t.par(3), P * k:P * k + P], w_s[:, :],
                                                start=b is None, stop=b is None or k == 1)
                    last.then_inc(l_filled, 1)

            pipeline(pe, ITEMS, DEPTH, step)


def assign_slots(nc, g, name, kind, gate_col):
    T, E = TILES, EXPERTS
    ks = 2 if kind == "top2" else 1
    with ExitStack() as ctx:
        ph = Phase(nc, ctx, name)
        rest, cand = ph.sb("rest", [P, T, E]), ph.sb("cand", [P, T, E])
        hot = [ph.sb(f"hot{k}", [P, T, E]) for k in range(ks)]
        best = [ph.sb(f"best{k}", [P, T]) for k in range(ks)]
        topv = [ph.sb(f"topv{k}", [P, T]) for k in range(ks)]
        hot_bf = ph.sb("hot_bf", [P, T, E], BF16)
        soft, soft_sum, second = ph.sb("soft", [P, T, E]), ph.sb("soft_sum", [P, T]), ph.sb("second", [P, T])
        rev, zeros = ph.sb("rev", [P, E]), ph.sb("zeros", [P, T])
        per_tile, upto, pos = ph.sb("per_tile", [P, E, T]), ph.sb("upto", [P, E, T]), ph.sb("pos", [P, T, E])
        rank, keep, slot = ph.sb("rank", [P, T]), ph.sb("keep", [P, T]), ph.sb("slot", [P, T])
        blocks, base = ph.sb("blocks", [P, E, 16]), ph.sb("base", [P, E])
        nblk, blk_end = ph.sb("nblk", [P, E]), ph.sb("blk_end", [P, E])
        item_cmp = ph.sb("item_cmp", [P, TOP2_TILES, E - 1])
        INCL, TOT = ph.ps("INCL", [P, T, E]), ph.ps("TOT", [P, T, E])
        hot_ready, counted, shifted, soft_ready, diff_ready, diff_exp, chained, slots_done = ph.sems(
            "hot_ready counted shifted soft_ready diff_ready diff_exp chained slots_done")
        block = ctx.enter_context(nc.Block())
        V = nc.vector

        def over_experts(a):
            return a[:, :].unsqueeze(2).broadcast_to([P, T, E])

        def over_tiles(a):
            return a.unsqueeze(1).broadcast_to([P, T, E])

        @block.vector
        def _(dve):
            done = [0]

            def then(ins):
                done[0] += 1
                ins.then_inc(chained, 1)
                dve.wait_ge(chained, done[0])

            V.memset(zeros[:, :], 0.0)
            then(V.tensor_scalar(rev[:, :], g.const[:, C_ECOL:C_ECOL + E], -1.0, float(E), ALU.mult, ALU.add))
            src = g.logits
            for k in range(ks):
                then(V.tensor_reduce(topv[k][:, :], src[:, :, :], AX.X, ALU.max))
                then(V.tensor_tensor(cand[:, :, :], src[:, :, :], over_experts(topv[k]), ALU.is_equal))
                then(V.tensor_tensor(cand[:, :, :], cand[:, :, :], over_tiles(rev[:, :]), ALU.mult))
                then(V.tensor_reduce(best[k][:, :], cand[:, :, :], AX.X, ALU.max))
                then(V.tensor_tensor(hot[k][:, :, :], cand[:, :, :], over_experts(best[k]), ALU.is_equal))
                if k + 1 < ks:
                    then(V.scalar_tensor_tensor(rest[:, :, :].rearrange("p t e -> p (t e)"), hot[k][:, :, :].rearrange("p t e -> p (t e)"),
                                                -BIG, src[:, :, :].rearrange("p t e -> p (t e)"), ALU.mult, ALU.add))
                    src = rest
            if ks == 2:
                V.tensor_tensor(hot_bf[:, :, :], hot[0][:, :, :], hot[1][:, :, :], ALU.add).then_inc(hot_ready, 1)
            else:
                V.tensor_copy(hot_bf[:, :, :], hot[0][:, :, :]).then_inc(hot_ready, 1)
            V.tensor_tensor(soft[:, :, :], g.logits[:, :, :], over_experts(topv[0]), ALU.subtract).then_inc(shifted, 1)
            if ks == 2:
                V.tensor_tensor(second[:, :], topv[1][:, :], topv[0][:, :], ALU.subtract).then_inc(shifted, 1)
            dve.wait_ge(counted, 1)
            then(V.tensor_copy(per_tile[:, :, :], TOT[:, :, :].rearrange("p t e -> p e t")))
            for e in range(E):
                last = V.tensor_tensor_scan(upto[:, e, :], per_tile[:, e, :], zeros[:, :], 0.0, ALU.add, ALU.add)
            then(last)
            then(V.tensor_tensor(per_tile[:, :, :], upto[:, :, :], per_tile[:, :, :], ALU.subtract))
            then(V.tensor_tensor(pos[:, :, :], INCL[:, :, :], per_tile[:, :, :].rearrange("p e t -> p t e"), ALU.add))
            if ks == 2:
                then(V.tensor_tensor(blocks[:, :, :], upto[:, :, T - 1:T].broadcast_to([P, E, 16]),
                                     g.const[:, C_BLK:C_BLK + 16].unsqueeze(1).broadcast_to([P, E, 16]), ALU.is_gt))
                then(V.tensor_reduce(nblk[:, :], blocks[:, :, :], AX.X, ALU.add))
                then(V.tensor_tensor_scan(blk_end[:, :], nblk[:, :], zeros[:, 0:E], 0.0, ALU.add, ALU.add))
                then(V.tensor_tensor(nblk[:, :], blk_end[:, :], nblk[:, :], ALU.subtract))
                then(V.tensor_scalar(base[:, :], nblk[:, :], float(SLOTS), None, ALU.mult))
                then(V.tensor_tensor(pos[:, :, :], pos[:, :, :], over_tiles(base[:, :]), ALU.add))
                then(V.tensor_tensor(item_cmp[:, :, :],
                                     g.const[:, C_ITEM:C_ITEM + TOP2_TILES].unsqueeze(2).broadcast_to([P, TOP2_TILES, E - 1]),
                                     nblk[:, 1:E].unsqueeze(1).broadcast_to([P, TOP2_TILES, E - 1]), ALU.is_ge))
                then(V.tensor_reduce(slot[:, 0:TOP2_TILES], item_cmp[:, :, :], AX.X, ALU.add))
                then(V.tensor_copy(g.tile_expert[:, :], slot[:, 0:TOP2_TILES]))
            for k in range(ks):
                then(V.tensor_tensor(cand[:, :, :], hot[k][:, :, :], pos[:, :, :], ALU.mult))
                then(V.tensor_reduce(rank[:, :], cand[:, :, :], AX.X, ALU.add))
                if ks == 2:
                    then(V.tensor_scalar(slot[:, :], rank[:, :], -1.0, None, ALU.add))
                    then(V.tensor_copy(g.get[k][:, :], slot[:, :]))
                    then(V.tensor_copy(g.put[k][:, :], slot[:, :]))
                else:
                    then(V.tensor_scalar(keep[:, :], rank[:, :], float(CAP), None, ALU.is_le))
                    then(V.tensor_scalar(rank[:, :], rank[:, :], -1.0, float(CAP - 1), ALU.add, ALU.min))
                    then(V.tensor_scalar(slot[:, :], best[k][:, :], -float(CAP), float(E * CAP), ALU.mult, ALU.add))
                    then(V.tensor_tensor(slot[:, :], slot[:, :], rank[:, :], ALU.add))
                    then(V.tensor_copy(g.get[k][:, :], slot[:, :]))
                    then(V.tensor_scalar(rank[:, :], keep[:, :], -float(4 * TOKENS), float(4 * TOKENS), ALU.mult, ALU.add))
                    then(V.tensor_tensor(slot[:, :], slot[:, :], rank[:, :], ALU.add))
                    then(V.tensor_copy(g.put[k][:, :], slot[:, :]))
            gate = g.gate[:, gate_col:gate_col + 1]
            if kind == "first":
                then(V.tensor_scalar(g.weight[0][:, :], keep[:, :], gate, None, ALU.mult))
                then(V.tensor_scalar(g.weight[1][:, :], g.weight[0][:, :], -1.0, gate, ALU.mult, ALU.add))
            else:
                dve.wait_ge(soft_ready, ks)
                then(V.tensor_reduce(soft_sum[:, :], soft[:, :, :], AX.X, ALU.add))
                then(V.reciprocal(soft_sum[:, :], soft_sum[:, :]))
                if kind == "gated":
                    then(V.tensor_tensor(keep[:, :], keep[:, :], soft_sum[:, :], ALU.mult))
                    then(V.tensor_scalar(g.weight[0][:, :], keep[:, :], gate, None, ALU.mult))
                else:
                    then(V.tensor_tensor(second[:, :], second[:, :], soft_sum[:, :], ALU.mult))
                    V.tensor_tensor(second[:, :], second[:, :], soft_sum[:, :], ALU.subtract).then_inc(diff_ready, 1)
                    dve.wait_ge(diff_exp, 1)
                    then(V.tensor_scalar(rank[:, :], second[:, :], 1.0, None, ALU.add))
                    then(V.reciprocal(rank[:, :], rank[:, :]))
                    then(V.tensor_tensor(second[:, :], second[:, :], rank[:, :], ALU.mult))
                    then(V.tensor_scalar(g.weight[0][:, :], rank[:, :], gate, None, ALU.mult))
                    then(V.tensor_scalar(g.weight[1][:, :], second[:, :], gate, None, ALU.mult))

        @block.scalar
        def _(act):
            act.wait_ge(shifted, ks)
            nc.scalar.activation(soft[:, :, :], soft[:, :, :], ACT.Exp).then_inc(soft_ready, 1)
            if ks == 2:
                nc.scalar.activation(second[:, :], second[:, :], ACT.Exp).then_inc(soft_ready, 1)
                act.wait_ge(diff_ready, 1)
                nc.scalar.activation(second[:, :], second[:, :], ACT.Exp).then_inc(diff_exp, 1)

        @block.tensor
        def _(pe):
            pe.wait_ge(hot_ready, 1)
            rows = hot_bf[:, :, :].rearrange("p t e -> p (t e)")
            nc.tensor.matmul(INCL[:, :, :].rearrange("p t e -> p (t e)"), g.const_bf[:, C_TRI:C_TRI + P], rows, start=True, stop=True)
            nc.tensor.matmul(TOT[:, :, :].rearrange("p t e -> p (t e)"), g.const_bf[:, C_ONES:C_ONES + P], rows,
                             start=True, stop=True).then_inc(counted, 1)


def scatter_rows(nc, g, name, slots, ks):
    with ExitStack() as ctx:
        sent = Phase(nc, ctx, name).sem("sent")
        block = ctx.enter_context(nc.Block())

        @block.gpsimd
        def _(pool):
            for tile in range(TILES):
                for k in range(ks):
                    pool.indirect_dma_start(slots, bass.IndirectOffsetOnAxis(ap=g.put[k][:, tile:tile + 1], axis=0),
                                            g.xn[:, tile, :], None, bounds_check=slots.shape[0] - 1,
                                            oob_is_err=False).then_inc(sent, 16)
            pool.wait_ge(sent, 16 * TILES * ks)


def combine(nc, g, name, rows, ks, own):
    GROUP = 8
    GROUPS = TILES // GROUP
    with ExitStack() as ctx:
        ph = Phase(nc, ctx, name)
        got = ph.sb("got", [P, 2, GROUP, D])
        term = ph.sb("term", [P, GROUP, D])
        arrived = [ph.sem(f"arrived{k}") for k in range(2)]
        term_done, own_done, added = ph.sems("term_done own_done added")
        block = ctx.enter_context(nc.Block())

        @block.gpsimd
        def _(pool):
            for n in range(GROUPS * ks):
                grp, k = n // ks, n % ks
                if n >= 2:
                    pool.wait_ge(term_done, n - 1)
                for j in range(GROUP):
                    tile = grp * GROUP + j
                    pool.indirect_dma_start(got[:, n % 2, j, :], None, rows,
                                            bass.IndirectOffsetOnAxis(ap=g.get[k][:, tile:tile + 1], axis=0),
                                            bounds_check=rows.shape[0] - 1, oob_is_err=False).then_inc(arrived[n % 2], 16)

        @block.vector
        def _(dve):
            adds, terms = [0], [0]

            def add_term(src, weight, grp, sem, count):
                tiles = slice(grp * GROUP, grp * GROUP + GROUP)
                if adds[0]:
                    dve.wait_ge(added, adds[0])
                nc.vector.tensor_tensor(term[:, :, :], src, weight[:, tiles].unsqueeze(2).broadcast_to([P, GROUP, D]),
                                        ALU.mult).then_inc(sem, 1)
                dve.wait_ge(sem, count)
                nc.vector.tensor_tensor(g.x[:, tiles, :], g.x[:, tiles, :], term[:, :, :], ALU.add).then_inc(added, 1)
                adds[0] += 1

            if own:
                for grp in range(GROUPS):
                    add_term(g.xn[:, grp * GROUP:grp * GROUP + GROUP, :], g.weight[1], grp, own_done, grp + 1)
            for n in range(GROUPS * ks):
                grp, k = n // ks, n % ks
                dve.wait_ge(arrived[n % 2], 16 * GROUP * (n // 2 + 1))
                add_term(got[:, n % 2, :, :], g.weight[k], grp, term_done, n + 1)


def experts(nc, g, name, slots, rows, w1, b1, w2, b2, kind):
    dynamic = kind == "silu"
    ITEMS = TOP2_TILES if dynamic else SLOT_TILES
    DEPTH = 5
    FC = 2 if dynamic else 4
    C = ERF_C if kind == "gelu" else 1.0
    with ExitStack() as ctx:
        ph = Phase(nc, ctx, name)
        xs = ph.sb("xs", [P, 2, SUB, D])
        xs_t = ph.sb("xs_t", [P, 2, SLOTS])
        w1_s, w2_s = ph.sb("w1", [P, 2, 4, P]), ph.sb("w2", [P, 2, FC, D])
        b1_s, b1_scaled, b2_s = ph.sb("b1", [P, 2, 4]), ph.sb("b1_scaled", [P, 2, 4]), ph.sb("b2", [P, 2, D])
        hid = ph.sb("hid", [P, 2, FC, SLOTS])
        act_gate = ph.sb("act_gate", [P, FC, SLOTS])
        y = ph.sb("y", [P, 2, SUB, D])
        X, Y, H = ph.ps("X", [P, 512]), ph.ps("Y", [P, 512]), ph.ps("H", [P, 4, 512])
        go, xt_filled, xt_drained, y_filled, y_drained, b1_ready, hid_ready = ph.sems(
            "go xt_filled xt_drained y_filled y_drained b1_ready hid_ready")
        h_filled = [ph.sem(f"h_filled{c}") for c in range(4)]
        h_drained = [ph.sem(f"h_drained{c}") for c in range(4)]
        gate_ready = [ph.sem(f"gate_ready{c}") for c in range(2)]
        x_in, w1_in, w2_in, stored = ([ph.sem(f"{n}{k}") for k in range(2)] for n in ("x_in", "w1_in", "w2_in", "stored"))
        block = ctx.enter_context(nc.Block())
        src = slots.rearrange("(i s p) d -> i p s d", p=P, s=SUB)
        dst = rows.rearrange("(i s p) d -> i p s d", p=P, s=SUB)
        w1_v = w1.rearrange("e d (c f) -> e d c f", c=4)
        w2_v = w2.rearrange("e (c f) d -> e f c d", f=P)

        @block.sync
        def _(sp):
            def step(t):
                n2, n3, n4 = t.done(2), t.done(3), t.done(4)
                n5 = t.done(5)

                def expert(s):
                    if dynamic:
                        e = sp.value_load(g.tile_expert[0:1, bass.ds(t.item(s), 1)], min_val=0, max_val=EXPERTS - 1)
                        return [e]
                    return [(t.t - s) // 2 if t.i is None else t.i + (t.t - s) // 2]

                def at(a, e):
                    return a[bass.ds(e, 1)].rearrange("a p c d -> (a p) c d")

                if t.live(0):
                    wait(sp, xt_filled, t.done(2))
                    sp.dma_start(xs[:, t.par(0), :, :], at(src, t.item(0))).then_inc(x_in[t.par(0)], 16)
                if t.live(1):
                    e, = expert(1)
                    wait(sp, h_filled[3], n3)
                    if not dynamic:
                        wait(sp, h_drained[3], n3)
                    sp.dma_start(w1_s[:, t.par(1), :, :], at(w1_v, e)).then_inc(w1_in[t.par(1)], 16)
                    if not dynamic:
                        sp.dma_start(b1_s[:, t.par(1), :], b1[bass.ds(e, 1)].rearrange("a f c -> (a f) c")).then_inc(
                            w1_in[t.par(1)], 16)
                if t.live(2):
                    e, = expert(2)
                    wait(sp, y_drained, n4)
                    sp.dma_start(w2_s[:, t.par(2), :, :], at(w2_v, e)).then_inc(w2_in[t.par(2)], 16)
                    if not dynamic:
                        sp.dma_start(b2_s[:, t.par(2), :], b2[bass.ds(e, 1)].partition_broadcast(P)).then_inc(
                            w2_in[t.par(2)], 16)
                if t.live(4):
                    wait(sp, y_drained, n4)
                    sp.dma_start(at(dst, t.item(4)), y[:, t.par(4), :, :]).then_inc(stored[t.par(4)], 16)

            pipeline(sp, ITEMS, DEPTH, step)
            for k in range(2):
                sp.wait_ge(stored[k], 16 * ITEMS // 2)

        @block.vector
        def _(dve):
            nc.vector.memset(act_gate[:, :, :], 0.0).then_inc(go, 1)

            def step(t):
                n1, n2, n3 = t.done(1), t.done(2), t.done(3)
                bias_landed = t.landed(2, 1 if dynamic else 2)
                out_bias_landed = t.landed(3, 1 if dynamic else 2)
                kept = t.landed(5)
                if t.live(1):
                    dve.wait_ge(go, 1)
                    wait(dve, xt_filled, n1)
                    nc.vector.tensor_copy(xs_t[:, t.par(1), :], X[:, :]).then_inc(xt_drained, 1)
                if t.live(2) and not dynamic:
                    dve.wait_ge(go, 1)
                    wait(dve, w1_in[t.par(2)], bias_landed)
                    nc.vector.tensor_scalar(b1_scaled[:, t.par(2), :], b1_s[:, t.par(2), :], C, None, ALU.mult).then_inc(b1_ready, 1)
                if t.live(3):
                    dve.wait_ge(go, 1)
                    wait(dve, y_filled, n3)
                    wait(dve, stored[t.par(5)], kept)
                    yv = y[:, t.par(3), :, :]
                    if dynamic:
                        nc.vector.tensor_copy(yv, Y[:, :].rearrange("p (s d) -> p s d", s=SUB)).then_inc(y_drained, 1)
                    else:
                        wait(dve, w2_in[t.par(3)], out_bias_landed)
                        nc.vector.scalar_tensor_tensor(yv, Y[:, :].rearrange("p (s d) -> p s d", s=SUB), 1.0 / C,
                                                       b2_s[:, t.par(3), :].unsqueeze(1).broadcast_to([P, SUB, D]),
                                                       ALU.mult, ALU.add).then_inc(y_drained, 1)
                if t.live(2) and dynamic:
                    for c in range(FC):
                        dve.wait_ge(go, 1)
                        wait(dve, gate_ready[c], n2)
                        wait(dve, h_filled[c + 2], n2)
                        nc.vector.tensor_tensor(hid[:, t.par(2), c, :], act_gate[:, c, :], H[:, c + 2, :], ALU.mult).then_inc(
                            h_drained[c + 2], 1)

            pipeline(dve, ITEMS, DEPTH, step)

        @block.scalar
        def _(act):
            def step(t):
                n2, n3 = t.done(2), t.done(3)
                if t.live(2):
                    for c in range(FC):
                        act.wait_ge(go, 1)
                        wait(act, h_filled[c], n2)
                        if dynamic:
                            wait(act, h_drained[c + 2], n3)
                            nc.scalar.activation(act_gate[:, c, :], H[:, c, :], ACT.Silu).then_inc(gate_ready[c], 1)
                        else:
                            wait(act, b1_ready, n2)
                            nc.scalar.activation(hid[:, t.par(2), c, :], H[:, c, :], ACT.Gelu if kind == "gelu" else ACT.Relu,
                                                 bias=b1_scaled[:, t.par(2), c:c + 1], scale=C).then_inc(h_drained[c], 1)

            pipeline(act, ITEMS, DEPTH, step)

        @block.tensor
        def _(pe):
            def step(t):
                n1, n2, n3, n4 = (t.done(s) for s in range(1, 5))
                x_landed = t.landed(1)
                w1_landed = t.landed(2, 1 if dynamic else 2)
                w2_landed = t.landed(3, 1 if dynamic else 2)
                if t.live(2):
                    for c in range(4):
                        pe.wait_ge(go, 1)
                        if c == 0:
                            wait(pe, xt_drained, n2)
                            wait(pe, w1_in[t.par(2)], w1_landed)
                        wait(pe, gate_ready[c] if dynamic and c < 2 else h_drained[c], n3)
                        nc.tensor.matmul(H[:, c, :], w1_s[:, t.par(2), c, :], xs_t[:, t.par(2), :],
                                         start=True, stop=True).then_inc(h_filled[c], 1)
                if t.live(1):
                    pe.wait_ge(go, 1)
                    wait(pe, x_in[t.par(1)], x_landed)
                    wait(pe, xt_drained, n2)
                    for k in range(SUB):
                        last = nc.tensor.transpose(X[:, P * k:P * k + P], xs[:, t.par(1), k, :], g.const[:, C_IDENT:C_IDENT + P])
                    last.then_inc(xt_filled, 1)
                if t.live(3):
                    pe.wait_ge(go, 1)
                    for c in range(FC):
                        wait(pe, h_drained[c + (2 if dynamic else 0)], n3)
                    wait(pe, w2_in[t.par(3)], w2_landed)
                    wait(pe, y_drained, n4)
                    for k in range(SUB):
                        for c in range(FC):
                            last = nc.tensor.matmul(Y[:, P * k:P * k + P], hid[:, t.par(3), c, P * k:P * k + P],
                                                    w2_s[:, t.par(3), c, :], start=c == 0, stop=c == FC - 1)
                    last.then_inc(y_filled, 1)

            pipeline(pe, ITEMS, DEPTH, step)



def bitlinear_ffn(nc, g, t_in):
    ITEMS, DEPTH, UNROLL = TILES // 2, 11, 4
    gate_col = 5
    with ExitStack() as ctx:
        ph = Phase(nc, ctx, "bit")
        w_raw = [ph.sb("w1_raw", [P, FF]), ph.sb("w2_raw", [P, FF])]
        w_q = [ph.sb("w1_q", [P, FF], BF16), ph.sb("w2_q", [P, FF], BF16)]
        b1_s, b2_s = ph.sb("b1", [P, FF]), ph.sb("b2", [P, D])
        w_sum, w_scale, w_inv = ph.sb("w_sum", [P, 2]), ph.sb("w_scale", [P, 2, 2]), ph.sb("w_inv", [P, 2])
        w_round = ph.sb("w_round", [P, FF])
        neg_one, magic = ph.sb("neg_one", [P, 2]), ph.sb("magic", [P, 1])
        st, mv = ph.sb("st", [P, 2, 2, 6]), ph.sb("mv", [P, 2, 2, 2])
        var_eps, rstd = ph.sb("var_eps", [P, 2, 2]), ph.sb("rstd", [P, 2, 2])
        xn, hid = ph.sb("xn", [P, 4, 2, D]), ph.sb("hid", [P, 4, 2, FF])
        ssq, big = ph.sb("ssq", [P, 2, 4, 2]), ph.sb("big", [P, 2, 4, 2])
        root, unit, inv = ph.sb("root", [P, 2, 2]), ph.sb("unit", [P, 2, 2]), ph.sb("inv", [P, 2, 2])
        mult, deq = ph.sb("mult", [P, 2, 4, 2]), ph.sb("deq", [P, 2, 4, 2])
        x_square, h_square = ph.sb("x_square", [P, 2, D]), ph.sb("h_square", [P, 2, FF])
        x_round, h_round = ph.sb("x_round", [P, 2, D]), ph.sb("h_round", [P, 2, FF])
        xq, xq_t = ph.sb("xq", [P, 2, 2, D], BF16), ph.sb("xq_t", [P, 2, 2, P], BF16)
        hq, hq_t = ph.sb("hq", [P, 2, 2, FF], BF16), ph.sb("hq_t", [P, 2, 8, P], BF16)
        pre, term = ph.sb("pre", [P, 2, 2, FF]), ph.sb("term", [P, 2, D])
        XT, H = ph.ps("XT", [P, 1024], BF16), ph.ps("H", [P, 2, FF])
        HT, Y, W = ph.ps("HT", [P, 8, P], BF16), ph.ps("Y", [P, 512]), ph.ps("W", [P, 512])
        (weights_in, chained, w_summed, w_totalled, ready, stats_part, stats_done, eps_done, rstd_done, xn_done,
         x_big, x_ssq, pooled, x_scaled, x_rounded, xq_done, xt_filled, xt_drained, h_filled, h_read,
         hid_done, h_big, h_ssq, h_scaled, h_rounded, hq_done, ht_filled, ht_drained, y_filled, y_read, y_added) = ph.sems(
            "weights_in chained w_summed w_totalled ready stats_part stats_done eps_done rstd_done xn_done "
            "x_big x_ssq pooled x_scaled x_rounded xq_done xt_filled xt_drained h_filled h_read "
            "hid_done h_big h_ssq h_scaled h_rounded hq_done ht_filled ht_drained y_filled y_read y_added")
        block = ctx.enter_context(nc.Block())
        V = nc.vector

        @block.sync
        def _(sp):
            sp.dma_start(w_raw[0][:, :], t_in["B_w1"]).then_inc(weights_in, 16)
            sp.dma_start(w_raw[1][:, :].rearrange("p (c d) -> p c d", c=4), t_in["B_w2"].rearrange("(c p) d -> p c d", p=P)).then_inc(
                weights_in, 16)
            sp.dma_start(b1_s[:, :], t_in["B_b1"].partition_broadcast(P)).then_inc(weights_in, 16)
            sp.dma_start(b2_s[:, :], t_in["B_b2"].partition_broadcast(P)).then_inc(weights_in, 16)

        @block.gpsimd
        def _(pool):
            def step(t):
                n0 = t.done(0)
                if t.i is None:
                    links = 6 * (max(0, min(t.t - 2, ITEMS)) + max(0, min(t.t - 7, ITEMS)))

                def at(k):
                    if t.i is None:
                        return links + k
                    return pool.to_reg(t.i * (12 * UNROLL) + 6 * (t.t - 2 + t.t - 7) + k)

                marks = [at(k) for k in range(1, 13)]
                used = [0]

                def scales(n, s, width, sums, largest, finished, used_by):
                    b, before = t.par(s, 4), t.done(s + 4)
                    now = t.done(s)
                    pool.wait_ge(ready, 1)
                    wait(pool, sums, now)
                    wait(pool, largest, now)
                    wait(pool, used_by, before)

                    def then(ins):
                        ins.then_inc(pooled, 1)
                        pool.wait_ge(ready, 1)
                        pool.wait_ge(pooled, marks[used[0]])
                        used[0] += 1

                    G_ = nc.gpsimd
                    then(G_.tensor_scalar(root[:, n, :], ssq[:, n, b, :], 1.0 / width, LN_EPS, ALU.mult, ALU.add))
                    then(G_.tensor_tensor(root[:, n, :], root[:, n, :], g.neg_half[:, 0:2], ALU.pow))
                    then(G_.tensor_tensor(unit[:, n, :], big[:, n, b, :], root[:, n, :], ALU.mult))
                    then(G_.tensor_scalar(unit[:, n, :], unit[:, n, :], 1e-5, 1.0 / 127.0, ALU.max, ALU.mult))
                    then(G_.tensor_tensor(inv[:, n, :], unit[:, n, :], neg_one[:, :], ALU.pow))
                    then(G_.tensor_tensor(mult[:, n, b, :], root[:, n, :], inv[:, n, :], ALU.mult))
                    G_.tensor_tensor(deq[:, n, b, :], unit[:, n, :], w_scale[:, n, :], ALU.mult).then_inc(finished, 1)

                if t.live(2):
                    scales(0, 2, D, x_ssq, x_big, x_scaled, h_read)
                if t.live(7):
                    scales(1, 7, FF, h_ssq, h_big, h_scaled, y_read)
                if t.live(0):
                    pool.wait_ge(ready, 1)
                    wait(pool, stats_done, n0)
                    nc.gpsimd.tensor_tensor(var_eps[:, t.par(0), :], mv[:, t.par(0), :, 1], g.eps[:, 0:2], ALU.add).then_inc(eps_done, 1)
                    pool.wait_ge(ready, 1)
                    wait(pool, eps_done, n0)
                    nc.gpsimd.tensor_tensor(rstd[:, t.par(0), :], var_eps[:, t.par(0), :], g.neg_half[:, 0:2],
                                            ALU.pow).then_inc(rstd_done, 1)

            pipeline(pool, ITEMS, DEPTH, step, UNROLL)

        @block.vector
        def _(dve):
            done = [0]

            def then(ins):
                done[0] += 1
                ins.then_inc(chained, 1)
                dve.wait_ge(chained, done[0])

            V.memset(neg_one[:, :], -1.0)
            V.memset(magic[:, :], MAGIC)
            dve.wait_ge(weights_in, 64)
            for n in range(2):
                last = V.tensor_reduce(w_sum[:, n:n + 1], w_raw[n][:, :], AX.X, ALU.add, apply_absolute_value=True)
            last.then_inc(w_summed, 1)
            dve.wait_ge(w_totalled, 1)
            for k in range(2):
                last = V.tensor_scalar(w_scale[:, :, k], W[:, 0:2], 1.0 / (D * FF), 1e-5, ALU.mult, ALU.max)
            then(last)
            then(V.reciprocal(w_inv[:, :], w_scale[:, :, 0]))
            for n in range(2):
                then(V.tensor_scalar(w_round[:, :], w_raw[n][:, :], w_inv[:, n:n + 1], None, ALU.mult))
                then(V.tensor_scalar(w_round[:, :], w_round[:, :], MAGIC, -MAGIC, ALU.add, ALU.add))
                then(V.tensor_scalar(w_q[n][:, :], w_round[:, :], 1.0, -1.0, ALU.min, ALU.max))
            then(V.tensor_scalar(w_scale[:, 1, :], w_scale[:, 1, :], g.gate[:, gate_col:gate_col + 1], None, ALU.mult))
            V.tensor_scalar(b2_s[:, :], b2_s[:, :], g.gate[:, gate_col:gate_col + 1], None, ALU.mult).then_inc(ready, 1)
            dve.wait_ge(ready, 1)

            def step(t):
                n0, n1, n3, n4, n5, n7, n8, n10, n11 = (t.done(s) for s in (0, 1, 3, 4, 5, 7, 8, 10, 11))
                if t.live(1):
                    dve.wait_ge(ready, 1)
                    wait(dve, rstd_done, n1)
                    for k in range(2):
                        last = V.tensor_scalar(xn[:, t.par(1, 4), k, :].unsqueeze(1), g.x[:, bass.ds(t.item(1) * 2 + k, 1), :],
                                               mv[:, t.par(1), k, 0:1], rstd[:, t.par(1), k:k + 1], ALU.subtract, ALU.mult)
                    last.then_inc(xn_done, 1)
                if t.live(0):
                    for k in range(2):
                        last = V.bn_stats(st[:, t.par(0), k, :], g.x[:, bass.ds(t.item(0) * 2 + k, 1), :])
                    last.then_inc(stats_part, 1)
                if t.live(1):
                    dve.wait_ge(ready, 1)
                    wait(dve, xn_done, n1)
                    V.tensor_reduce(big[:, 0, t.par(1, 4), :], xn[:, t.par(1, 4), :, :], AX.X, ALU.max,
                                    apply_absolute_value=True).then_inc(x_big, 1)
                if t.live(0):
                    dve.wait_ge(ready, 1)
                    wait(dve, stats_part, n0)
                    for k in range(2):
                        last = V.bn_aggr(mv[:, t.par(0), k, :], st[:, t.par(0), k, :])
                    last.then_inc(stats_done, 1)
                if t.live(7):
                    dve.wait_ge(ready, 1)
                    wait(dve, hid_done, n7)
                    V.tensor_reduce(big[:, 1, t.par(7, 4), :], hid[:, t.par(7, 4), :, :], AX.X, ALU.max,
                                    apply_absolute_value=True).then_inc(h_big, 1)
                if t.live(3):
                    dve.wait_ge(ready, 1)
                    wait(dve, x_rounded, n3)
                    wait(dve, xt_filled, n5)
                    V.tensor_scalar(xq[:, t.par(3), :, :], x_round[:, :, :], -MAGIC, None, ALU.add).then_inc(xq_done, 1)
                if t.live(4):
                    dve.wait_ge(ready, 1)
                    wait(dve, xt_filled, n4)
                    V.tensor_copy(xq_t[:, t.par(4), :, :], XT[:, 0:256].rearrange("p (k n) -> p k n", k=2)).then_inc(xt_drained, 1)
                if t.live(10):
                    dve.wait_ge(ready, 1)
                    wait(dve, y_filled, n10)
                    wait(dve, y_added, n11)
                    for k in range(2):
                        last = V.scalar_tensor_tensor(term[:, k, :], Y[:, P * k:P * k + P], deq[:, 1, t.par(10, 4), k:k + 1],
                                                      b2_s[:, :], ALU.mult, ALU.add)
                    last.then_inc(y_read, 1)
                    dve.wait_ge(ready, 1)
                    wait(dve, y_read, n10)
                    xs = g.x[:, bass.ds(t.item(10) * 2, 2), :]
                    V.tensor_tensor(xs, xs, term[:, :, :], ALU.add).then_inc(y_added, 1)
                if t.live(8):
                    dve.wait_ge(ready, 1)
                    wait(dve, h_rounded, n8)
                    wait(dve, ht_filled, n10)
                    V.tensor_scalar(hq[:, t.par(8), :, :], h_round[:, :, :], -MAGIC, None, ALU.add).then_inc(hq_done, 1)
                if t.live(5):
                    dve.wait_ge(ready, 1)
                    wait(dve, h_filled, n5)
                    wait(dve, hid_done, n7)
                    for k in range(2):
                        last = V.scalar_tensor_tensor(pre[:, t.par(5), k, :], H[:, k, :], deq[:, 0, t.par(5, 4), k:k + 1],
                                                      b1_s[:, :], ALU.mult, ALU.add)
                    last.then_inc(h_read, 1)

            pipeline(dve, ITEMS, DEPTH, step, UNROLL)

        @block.scalar
        def _(act):
            def step(t):
                n2, n3, n4, n6, n7, n8, n9 = (t.done(s) for s in (2, 3, 4, 6, 7, 8, 9))
                if t.live(2):
                    act.wait_ge(ready, 1)
                    wait(act, xn_done, n2)
                    wait(act, x_ssq, n3)
                    for k in range(2):
                        last = nc.scalar.activation(x_square[:, k, :], xn[:, t.par(2, 4), k, :], ACT.Square,
                                                    accum_out=ssq[:, 0, t.par(2, 4), k:k + 1])
                    last.then_inc(x_ssq, 1)
                if t.live(6):
                    act.wait_ge(ready, 1)
                    wait(act, h_read, n6)
                    nc.scalar.activation(hid[:, t.par(6, 4), :, :], pre[:, t.par(6), :, :], ACT.Gelu).then_inc(hid_done, 1)
                if t.live(3):
                    act.wait_ge(ready, 1)
                    wait(act, x_scaled, n3)
                    wait(act, xq_done, n4)
                    for k in range(2):
                        last = nc.scalar.activation(x_round[:, k, :], xn[:, t.par(3, 4), k, :], ACT.Identity, bias=magic[:, :],
                                                    scale=mult[:, 0, t.par(3, 4), k:k + 1])
                    last.then_inc(x_rounded, 1)
                if t.live(9):
                    act.wait_ge(ready, 1)
                    wait(act, ht_filled, n9)
                    nc.scalar.copy(hq_t[:, t.par(9), :, :], HT[:, :, :]).then_inc(ht_drained, 1)
                if t.live(7):
                    act.wait_ge(ready, 1)
                    wait(act, hid_done, n7)
                    wait(act, h_ssq, n8)
                    for k in range(2):
                        last = nc.scalar.activation(h_square[:, k, :], hid[:, t.par(7, 4), k, :], ACT.Square,
                                                    accum_out=ssq[:, 1, t.par(7, 4), k:k + 1])
                    last.then_inc(h_ssq, 1)
                if t.live(8):
                    act.wait_ge(ready, 1)
                    wait(act, h_scaled, n8)
                    wait(act, hq_done, n9)
                    for k in range(2):
                        last = nc.scalar.activation(h_round[:, k, :], hid[:, t.par(8, 4), k, :], ACT.Identity, bias=magic[:, :],
                                                    scale=mult[:, 1, t.par(8, 4), k:k + 1])
                    last.then_inc(h_rounded, 1)

            pipeline(act, ITEMS, DEPTH, step, UNROLL)

        @block.tensor
        def _(pe):
            pe.wait_ge(w_summed, 1)
            nc.tensor.matmul(W[:, 0:2], g.const[:, C_ONES:C_ONES + P], w_sum[:, :], start=True, stop=True).then_inc(w_totalled, 1)
            ident = g.const_bf[:, C_IDENT:C_IDENT + P]

            def step(t):
                n4, n5, n6, n9, n10, n11 = (t.done(s) for s in (4, 5, 6, 9, 10, 11))
                if t.live(4):
                    pe.wait_ge(ready, 1)
                    wait(pe, xq_done, n4)
                    wait(pe, xt_drained, n5)
                    for k in range(2):
                        last = nc.tensor.transpose(XT[:, P * k:P * k + P], xq[:, t.par(4), k, :], ident)
                    last.then_inc(xt_filled, 1)
                if t.live(5):
                    pe.wait_ge(ready, 1)
                    wait(pe, xt_drained, n5)
                    wait(pe, h_read, n6)
                    for k in range(2):
                        last = nc.tensor.matmul(H[:, k, :], xq_t[:, t.par(5), k, :], w_q[0][:, :], start=True, stop=True)
                    last.then_inc(h_filled, 1)
                if t.live(9):
                    pe.wait_ge(ready, 1)
                    wait(pe, hq_done, n9)
                    wait(pe, ht_drained, n10)
                    for k in range(8):
                        last = nc.tensor.transpose(HT[:, k, :], hq[:, t.par(9), k // 4, P * (k % 4):P * (k % 4) + P], ident)
                    last.then_inc(ht_filled, 1)
                if t.live(10):
                    pe.wait_ge(ready, 1)
                    wait(pe, ht_drained, n10)
                    wait(pe, y_read, n11)
                    for k in range(8):
                        last = nc.tensor.matmul(Y[:, P * (k // 4):P * (k // 4) + P], hq_t[:, t.par(10), k, :],
                                                w_q[1][:, P * (k % 4):P * (k % 4) + P], start=k % 4 == 0, stop=k % 4 == 3)
                    last.then_inc(y_filled, 1)

            pipeline(pe, ITEMS, DEPTH, step, UNROLL)



class G:
    pass


def build(nc, t, out, stages):
    with ExitStack() as ctx:
        g = G()
        g.x = ctx.enter_context(nc.sbuf_tensor("x_stream", [P, TILES, D], F32))
        g.const = ctx.enter_context(nc.sbuf_tensor("const_table", [P, C_COLS], F32))
        g.const_bf = ctx.enter_context(nc.sbuf_tensor("const_bf", [P, 384], BF16))
        g.gate = ctx.enter_context(nc.sbuf_tensor("gates", [P, 8], F32))
        g.neg_half = ctx.enter_context(nc.sbuf_tensor("neg_half", [P, 8], F32))
        g.eps = ctx.enter_context(nc.sbuf_tensor("eps", [P, 8], F32))
        g.ctx_t = t["ctx_t"]
        g.scrap = nc.dram_tensor("scrap", [2, 8], F32).ap()
        g.slots0 = nc.dram_tensor("slots0", [TOKENS, D], F32).ap()
        g.slots3 = nc.dram_tensor("slots3", [TOKENS, D], F32).ap()
        g.slots2 = nc.dram_tensor("slots2", [TOP2_TILES * SLOTS, D], F32).ap()
        load_inputs(nc, g, t)
        def sb(name, shape, dt=F32):
            return ctx.enter_context(nc.sbuf_tensor(name, shape, dt))

        g.xn, g.logits = sb("xn_all", [P, TILES, D]), sb("logits", [P, TILES, EXPERTS])
        g.put = [sb(f"put{k}", [P, TILES], U32) for k in range(2)]
        g.get = [sb(f"get{k}", [P, TILES], U32) for k in range(2)]
        g.weight = [sb(f"weight{k}", [P, TILES]) for k in range(2)]
        g.tile_expert = sb("tile_expert", [P, TOP2_TILES], I32)

        def moe(n, slots, count, w, b, kind, act_kind, col, own):
            rows = nc.dram_tensor(f"rows{n}", [count, D], F32).ap()
            ks = 2 if kind == "top2" else 1
            route(nc, g, f"route{n}", w, b)
            assign_slots(nc, g, f"assign{n}", kind, col)
            scatter_rows(nc, g, f"scatter{n}", slots, ks)
            experts(nc, g, f"experts{n}", slots, rows, t[f"F{n}_w1"], t.get(f"F{n}_b1"), t[f"F{n}_w2"], t.get(f"F{n}_b2"), act_kind)
            combine(nc, g, f"combine{n}", rows, ks, own)

        if "a0" in stages:
            attention_wide(nc, g, t)
        if "f0" in stages:
            moe(0, g.slots0, TOKENS, t["F0_wg"], t["F0_bg"], "first", "gelu", 4, True)
        if "a1" in stages:
            attention_narrow(nc, g, "l1", 1, t["L1_wq"], t["L1_bq"], t["L1_wk"], t["L1_bk"], t["L1_wv"], t["L1_bv"],
                             t["L1_wo"], t["L1_bo"], "softmax")
        if "f1" in stages:
            bitlinear_ffn(nc, g, t)
        if "a2" in stages:
            attention_narrow(nc, g, "l2", 2, t["L2_wq"], t["L2_bq"], t["L2_wk"], t["L2_bk"], t["L2_wv"], t["L2_bv"],
                             t["L2_wo"], t["L2_bo"], "masked", t["mask"])
        if "f2" in stages:
            moe(2, g.slots2, TOP2_TILES * SLOTS, t["F2_wg"], None, "top2", "silu", 6, False)
        if "a3" in stages:
            attention_narrow(nc, g, "l3", 3, t["L3_wq"], t["L3_bq"], t["L3_wk"], t["L3_bk"], t["L3_wv"], t["L3_bv"],
                             t["L3_wo"], t["L3_bo"], "stable")
        if "f3" in stages:
            moe(3, g.slots3, TOKENS, t["F3_wg"], None, "gated", "relu", 7, False)
        with ExitStack() as c2:
            stored = c2.enter_context(nc.semaphore("stored"))
            block = c2.enter_context(nc.Block())

            @block.sync
            def _(sp):
                sp.dma_start(out.rearrange("(t p) d -> p t d", p=P), g.x[:, :, :]).then_inc(stored, 16)
                sp.wait_ge(stored, 16)


def lay_out(a):
    o = {"x": a["x"].reshape(TOKENS, D), "ctx_t": a["ctx_1024"].reshape(TOKENS, D).T,
         "g_xattn": a["g_xattn"], "g_ffn": a["g_ffn"], "consts": constants()}
    o["mask"] = a["mask_BxSxS2_bf1"].view(np.uint8).reshape(TILES, P, SEQ).transpose(1, 0, 2)

    def halves(w):
        r = w.reshape(w.shape[0], 8, 2, -1)
        return r.transpose(0, 2, 1, 3).reshape(w.shape[0], 2, -1)

    for n, p, tr in (("L1", "L1_xattn_w", True), ("L2", "L2_xattn_W", False), ("L3", "L3_xattn_W", True)):
        for m in "qkvo":
            w = a[p + m]
            w = w.T if tr else w
            o[f"{n}_w{m}"] = halves(w) if m == "v" else w
            b = a[f"{n}_xattn_b{m}"]
            o[f"{n}_b{m}"] = {"v": halves(b[None])[0], "o": b[None]}.get(m, b[:, None])
    o["L0_wq"], o["L0_wk"], o["L0_wo"] = a["L0_xattn_Wq"], a["L0_xattn_Wk"], a["L0_xattn_Wo"]
    o["L0_wv"] = halves(a["L0_xattn_Wv"])
    o["F0_wg"], o["F0_bg"] = a["L0_ffn_W_sw"], a["L0_ffn_b_sw"][None]
    o["F3_wg"], o["F2_wg"] = a["L3_ffn_Wg"], a["L2_ffn_router_kernel_DE"]
    for n in (0, 3):
        for m in ("W1", "b1", "W2", "b2"):
            o[f"F{n}_{m.lower()}"] = a[f"L{n}_ffn_{m}"]
        o[f"F{n}_b1"] = o[f"F{n}_b1"].reshape(EXPERTS, 4, P).transpose(0, 2, 1)
    o["F2_w1"] = np.concatenate([a["L2_ffn_kernel_gating_EDF"], a["L2_ffn_kernel_up_EDF"]], axis=2)
    o["F2_w2"] = a["L2_ffn_kernel_down_EFD"]
    o["B_w1"], o["B_w2"] = a["L1_ffn_w1"].T, a["L1_ffn_w2"].T
    o["B_b1"], o["B_b2"] = a["L1_ffn_b1"], a["L1_ffn_b2"]
    o["L2_wo"] = a["L2_xattn_Wo"].reshape(2, 64, D).transpose(1, 0, 2)
    return {k: np.ascontiguousarray(v) for k, v in o.items()}


STAGES = "a0 f0 a1 f1 a2 f2 a3 f3"


def kernel(**inputs):
    import numpy as _np
    import concourse.bacc as _bacc
    from concourse import mybir as _mybir
    from concourse.bass_utils import run_bass_kernel_spmd as _run

    nc = _bacc.Bacc("TRN2", target_bir_lowering=False, num_devices=1)
    arrays = lay_out({k: _np.asarray(v) for k, v in inputs.items()})
    t = {k: nc.dram_tensor("in_" + k, v.shape, _mybir.dt.from_np(v.dtype), kind="ExternalInput").ap()
         for k, v in arrays.items()}
    out = nc.dram_tensor("out", [TOKENS, D], F32, kind="ExternalOutput").ap()
    build(nc, t, out, STAGES.split())
    r = _run(nc, [{"in_" + k: v for k, v in arrays.items()}], core_ids=[0])
    return r.results[0]["out"].reshape(BATCH, SEQ, D)
```

```python
from contextlib import ExitStack

import numpy as np
import concourse.bass as bass
from concourse import mybir

P = 128
ALU = mybir.AluOpType
ACT = mybir.ActivationFunctionType
F32 = mybir.dt.float32
BF16 = mybir.dt.bfloat16
U8 = mybir.dt.uint8
I32 = mybir.dt.int32
U32 = mybir.dt.uint32
AX = mybir.AxisListType

BATCH, SEQ, D = 128, 64, 128
TOKENS = BATCH * SEQ
TILES = TOKENS // P
HEADS = 16
EXPERTS = 8
CAP = TOKENS // EXPERTS
FF = 512
FF2 = 256
SLOTS = 512
SUB = SLOTS // P
SLOT_TILES = TOKENS // SLOTS
REGION = TOKENS + SLOTS
TOP2_TILES = 2 * TOKENS // SLOTS + EXPERTS
PAD_ROWS = TOP2_TILES * SLOTS
BATCH_TILES = 8
LN_EPS = 1e-5
ERF_C = float(np.sqrt(2.0) / 1.41421)
MAGIC = 1.5 * 2.0 ** 23
BIG = 3.0e38

C_IDENT, C_TRI, C_ONES, C_JMASK, C_ECOL, C_BLK, C_ITEM = 0, 128, 256, 384, 388, 396, 412
C_COLS = C_ITEM + TOP2_TILES


def constants():
    c = np.zeros((P, C_COLS), np.float32)
    c[:, C_IDENT:C_IDENT + P] = np.eye(P)
    c[:, C_TRI:C_TRI + P] = np.triu(np.ones((P, P)))
    c[:, C_ONES:C_ONES + P] = 1.0
    for j in range(4):
        c[:, C_JMASK + j] = (np.arange(P) % 32) // 8 == j
    c[:, C_ECOL:C_ECOL + EXPERTS] = np.arange(EXPERTS)
    c[:, C_BLK:C_BLK + 16] = np.arange(16) * SLOTS
    c[:, C_ITEM:] = np.arange(TOP2_TILES)
    return c


class Step:

    def __init__(self, eng, items, t, i=None, unroll=2, depth=None):
        self.eng, self.items, self.t, self.i, self.unroll, self.depth = eng, items, t, i, unroll, depth
        self.counts = {}

    def live(self, s):
        return self.i is not None or 0 <= self.t - s < self.items

    def par(self, s, buffers=2):
        return (self.t - s) % buffers

    def item(self, s):
        return self.t - s if self.i is None else self.i * self.unroll + (self.t - s)

    def done(self, s):
        if self.i is None:
            return max(0, min(self.t - s + 1, self.items))
        if s not in self.counts:
            self.counts[s] = self.eng.to_reg(self.i * self.unroll + (self.t - s + 1))
        return self.counts[s]

    def batches(self, s, items):
        if self.i is None:
            return max(0, min(self.t - s + 1, self.items)) // items
        return self.eng.to_reg(self.i * (self.unroll // items) + (self.t - s + 1) // items)

    def landed(self, s, dmas=1):
        if self.i is None:
            return 16 * dmas * ((self.t - s) // 2 + 1) if self.t >= s else 0
        return self.eng.to_reg(self.i * (8 * dmas * self.unroll) + 16 * dmas * ((self.t - s) // 2 + 1))


def pipeline(eng, items, depth, emit, unroll=2):
    first = -(-depth // unroll) * unroll
    for t in range(first):
        emit(Step(eng, items, t))
    with eng.Fori(0, (items - first) // unroll) as i:
        for k in range(unroll):
            emit(Step(eng, items, first + k, i, unroll, depth))
    for t in range(items, items + depth - 1):
        emit(Step(eng, items, t))


def wait(eng, sem, count):
    if not (isinstance(count, int) and count <= 0):
        eng.wait_ge(sem, count)


class Phase:

    def __init__(self, nc, ctx, name):
        self.nc, self.ctx, self.name = nc, ctx, name
        self.held = []
        ctx.callback(self.clear)

    def clear(self):
        self.nc.clear_and_free_semaphores(self.held)
        self.nc.all_engine_barrier()

    def sb(self, name, shape, dt=F32):
        return self.ctx.enter_context(self.nc.sbuf_tensor(f"{self.name}_{name}", shape, dt))

    def ps(self, name, shape, dt=F32):
        return self.ctx.enter_context(self.nc.psum_tensor(f"{self.name}_{name}", shape, dt))

    def sem(self, name):
        self.held.append(self.nc.alloc_semaphore(f"{self.name}_{name}"))
        return self.held[-1]

    def sems(self, names):
        return [self.sem(n) for n in names.split()]



def load_inputs(nc, g, t):
    with ExitStack() as ctx:
        ph = Phase(nc, ctx, "setup")
        gates_raw = ph.sb("gates_raw", [P, 8])
        loaded, tanh_done, gates_in = ph.sems("loaded tanh_done gates_in")
        block = ctx.enter_context(nc.Block())

        @block.sync
        def _(sp):
            sp.dma_start(gates_raw[:, 0:4], t["g_xattn"].partition_broadcast(P)).then_inc(gates_in, 16)
            sp.dma_start(gates_raw[:, 4:8], t["g_ffn"].partition_broadcast(P)).then_inc(gates_in, 16)
            sp.dma_start(g.const[:, :], t["consts"]).then_inc(loaded, 16)
            sp.dma_start(g.x[:, :, :], t["x"].rearrange("(t p) d -> p t d", p=P)).then_inc(loaded, 16)
            sp.wait_ge(loaded, 32)

        @block.scalar
        def _(act):
            act.wait_ge(gates_in, 32)
            nc.scalar.activation(g.gate[:, :], gates_raw[:, :], ACT.Tanh).then_inc(tanh_done, 1)

        @block.vector
        def _(dve):
            nc.vector.memset(g.neg_half[:, :], -0.5).then_inc(tanh_done, 1)
            nc.vector.memset(g.eps[:, :], LN_EPS).then_inc(tanh_done, 1)
            dve.wait_ge(loaded, 32)
            nc.vector.tensor_copy(g.const_bf[:, :], g.const[:, 0:384]).then_inc(tanh_done, 1)



class Head:

    def __init__(self, ph, g, rows, ks, own):
        self.g, self.rows, self.ks, self.own = g, rows, ks, own
        self.index = ph.sb("index", [P, 2, ks, 2], U32)
        self.got = ph.sb("got", [P, 2, ks, 2, D])
        self.term = ph.sb("term", [P, ks + own, 2, D])
        self.arrived = [ph.sem(f"arrived{k}") for k in range(2)]
        self.index_done, self.terms_done, self.combined = ph.sems("index_done terms_done combined")
        self.partly = [ph.sem(f"partly{k}") for k in range(ks + own - 1)]

    def gather(self, nc, pool, t, s, ready, count):
        g, n0, n2 = self.g, t.done(s), t.done(s + 2)
        pool.wait_ge(ready, count)
        for k in range(self.ks):
            last = nc.gpsimd.tensor_copy(self.index[:, t.par(s), k, :], g.get[k][:, bass.ds(t.item(s) * 2, 2)])
        last.then_inc(self.index_done, 1)
        for k in range(self.ks):
            for tile in range(2):
                pool.wait_ge(ready, count)
                wait(pool, self.index_done, n0)
                wait(pool, self.terms_done, n2)
                pool.indirect_dma_start(self.got[:, t.par(s), k, tile, :], None, self.rows,
                                        bass.IndirectOffsetOnAxis(ap=self.index[:, t.par(s), k, tile:tile + 1], axis=0),
                                        bounds_check=self.rows.shape[0] - 1, oob_is_err=False).then_inc(self.arrived[t.par(s)], 16)

    def combine(self, nc, pool, t, s, ready, count):
        g, n1, n2 = self.g, t.done(s), t.done(s + 1)
        landed = t.landed(s, 2 * self.ks)
        tiles = bass.ds(t.item(s) * 2, 2)
        xs = g.x[:, tiles, :]
        pool.wait_ge(ready, count)
        wait(pool, self.arrived[t.par(s)], landed)
        wait(pool, self.combined, n2)
        for k in range(self.ks):
            last = nc.gpsimd.tensor_tensor(self.term[:, k, :, :], self.got[:, t.par(s), k, :, :],
                                           g.weight[k][:, tiles].unsqueeze(2).broadcast_to([P, 2, D]), ALU.mult)
        if self.own:
            last = nc.gpsimd.tensor_tensor(self.term[:, 1, :, :], g.xn[:, tiles, :],
                                           g.weight[1][:, tiles].unsqueeze(2).broadcast_to([P, 2, D]), ALU.mult)
        last.then_inc(self.terms_done, 1)
        pool.wait_ge(ready, count)
        wait(pool, self.terms_done, n1)
        nc.gpsimd.tensor_tensor(self.term[:, 0, :, :], self.term[:, 0, :, :], self.term[:, 1, :, :],
                                ALU.add).then_inc(self.partly[0], 1)
        pool.wait_ge(ready, count)
        wait(pool, self.partly[0], n1)
        nc.gpsimd.tensor_tensor(xs, xs, self.term[:, 0, :, :], ALU.add).then_inc(self.combined, 1)


class Tail:

    def __init__(self, ph, g, w, bias, kind, slots, tiles):
        self.g, self.w, self.bias, self.kind, self.slots, self.tiles = g, w, bias, kind, slots, tiles
        self.ks = 2 if kind == "top2" else 1
        self.nb = BATCH_TILES // tiles
        wide, narrow = [P, BATCH_TILES, EXPERTS], [P, BATCH_TILES]
        self.w_s, self.bias_s = ph.sb("router_w", [P, EXPERTS, D]), ph.sb("router_b", [P, EXPERTS])
        self.st, self.mv = ph.sb("tail_st", [P, 2, tiles, 6]), ph.sb("tail_mv", [P, 2, tiles, 2])
        self.var_eps, self.rstd = ph.sb("tail_var_eps", [P, 2, tiles]), ph.sb("tail_rstd", [P, 2, tiles])
        self.prod = ph.sb("products", [P, tiles, EXPERTS, D])
        self.rev, self.base = ph.sb("rev", [P, EXPERTS]), ph.sb("slot_base", [P, EXPERTS])
        self.rest, self.cand = ph.sb("rest", wide), ph.sb("cand", wide)
        self.topv, self.best = ph.sb("topv", narrow), ph.sb("best", narrow)
        self.hot = [ph.sb(f"hot{k}", wide) for k in range(self.ks)]
        self.chosen, self.before, self.of_batch = ph.sb("chosen", wide, BF16), ph.sb("before", [P, EXPERTS], BF16), ph.sb("of_batch", [P, EXPERTS])
        self.counts, self.ranked = ph.sb("counts", wide), ph.sb("ranked", wide)
        self.expert_base = ph.sb("expert_base", narrow)
        self.rank, self.slot, self.lost = (ph.sb(n, narrow) for n in ("rank", "slot", "lost"))
        self.put = ph.sb("put", [P, 2, self.ks, tiles], U32)
        self.rows = ph.sb("rows_out", [P, 2, tiles, D])
        (self.w_in, self.part, self.stats, self.eps, self.rstd_done, self.xn_done, self.multiplied, self.summed,
         self.chosen_done, self.counted, self.counts_read, self.put_done, self.rows_copied, self.chained, self.totalled) = ph.sems(
            "router_w_in tail_part tail_stats tail_eps tail_rstd_done tail_xn_done multiplied summed "
            "chosen_done counted counts_read put_done rows_copied chained totalled")
        self.sent = [ph.sem(f"sent{k}") for k in range(2)]
        self.slots_clear = None
        self.loads = 16 * (1 + (bias is not None))
        self.ph, self.steps = ph, {}

    def load(self, sp):
        sp.dma_start(self.w_s[:, :, :], self.w.partition_broadcast(P)).then_inc(self.w_in, 16)
        if self.bias is not None:
            sp.dma_start(self.bias_s[:, :], self.bias.partition_broadcast(P)).then_inc(self.w_in, 16)

    def prepare(self, nc, dve):
        g = self.g
        dve.wait_ge(self.w_in, self.loads)
        nc.vector.memset(self.chosen[:, :, :], 0.0)
        nc.vector.memset(self.before[:, :], 0.0)
        nc.vector.tensor_scalar(self.rev[:, :], g.const[:, C_ECOL:C_ECOL + EXPERTS], -1.0, float(EXPERTS), ALU.mult, ALU.add)
        nc.vector.tensor_scalar(self.base[:, :], g.const[:, C_ECOL:C_ECOL + EXPERTS], float(REGION), float(PAD_ROWS - 1),
                                ALU.mult, ALU.add).then_inc(self.chained, 1)
        dve.wait_ge(self.chained, 1)

    def batch(self, t, s):
        return t.live(s) and (t.t - s) % self.nb == self.nb - 1

    def on_dve(self, t, s):
        return t.i is None and t.item(s) >= t.items - 7

    def depth(self):
        return 5 + self.nb + 3

    def totals(self, nc, dve, items):
        dve.wait_ge(self.chosen_done, items // self.nb)
        nc.vector.tensor_reduce(self.of_batch[:, :], self.chosen[:, :, :].rearrange("p t e -> p e t"), AX.X, ALU.add).then_inc(
            self.totalled, 1)
        dve.wait_ge(self.totalled, 1)
        nc.vector.tensor_tensor(self.g.total_by_row[:, :], self.before[:, :], self.of_batch[:, :], ALU.add)

    def pool(self, nc, pool, t, s):
        g, par, k = self.g, t.par(s), self.tiles
        out = s + 5 + self.nb
        n0, n2, n3 = t.done(s), t.done(s + 2), t.done(s + 3)
        sent_before = t.landed(out + 2, k * self.ks)
        slotted = t.batches(out - self.nb + 1 + (t.t - out) % self.nb, self.nb) if t.live(out) else None
        if t.live(out) and t.i is None:
            if self.slots_clear and t.i is None and t.t == out:
                pool.wait_ge(*self.slots_clear)
            for tile in range(t.item(out) * k, t.item(out) * k + k):
                for c in range(self.ks):
                    pool.wait_ge(self.w_in, self.loads)
                    wait(pool, self.put_done, slotted)
                    wait(pool, self.sent[t.par(out)], sent_before)
                    pool.indirect_dma_start(
                        self.slots, bass.IndirectOffsetOnAxis(ap=g.put[c][:, tile:tile + 1], axis=0), g.xn[:, tile, :], None,
                        bounds_check=self.slots.shape[0] - 1, oob_is_err=False).then_inc(self.sent[t.par(out)], 16)
        elif t.live(out):
            tiles = bass.ds(t.item(out) * k, k)
            first = -(-t.depth // t.unroll) * t.unroll
            copied = pool.to_reg(t.i * t.unroll + (t.t - first + 1))
            pool.wait_ge(self.w_in, self.loads)
            wait(pool, self.put_done, slotted)
            wait(pool, self.sent[t.par(out)], sent_before)
            for c in range(self.ks):
                nc.gpsimd.tensor_copy(self.put[:, t.par(out), c, :], g.put[c][:, tiles])
            nc.gpsimd.tensor_copy(self.rows[:, t.par(out), :, :], g.xn[:, tiles, :]).then_inc(self.rows_copied, 1)
            for tile in range(k):
                for c in range(self.ks):
                    pool.wait_ge(self.w_in, self.loads)
                    wait(pool, self.rows_copied, copied)
                    pool.indirect_dma_start(
                        self.slots, bass.IndirectOffsetOnAxis(ap=self.put[:, t.par(out), c, tile:tile + 1], axis=0),
                        self.rows[:, t.par(out), tile, :], None, bounds_check=self.slots.shape[0] - 1,
                        oob_is_err=False).then_inc(self.sent[t.par(out)], 16)
        if t.live(s + 2) and not self.on_dve(t, s + 2):
            pool.wait_ge(self.w_in, self.loads)
            wait(pool, self.xn_done, n2)
            wait(pool, self.summed, n3)
            for tile in range(k):
                last = nc.gpsimd.tensor_tensor(self.prod[:, tile, :, :], self.w_s[:, :, :],
                                               g.xn[:, bass.ds(t.item(s + 2) * k + tile, 1), :].broadcast_to([P, EXPERTS, D]),
                                               ALU.mult)
            last.then_inc(self.multiplied, 1)
        if t.live(s):
            pool.wait_ge(self.w_in, self.loads)
            wait(pool, self.stats, n0)
            nc.gpsimd.tensor_tensor(self.var_eps[:, par, :], self.mv[:, par, :, 1], g.eps[:, 0:k], ALU.add).then_inc(self.eps, 1)
            pool.wait_ge(self.w_in, self.loads)
            wait(pool, self.eps, n0)
            nc.gpsimd.tensor_tensor(self.rstd[:, par, :], self.var_eps[:, par, :], g.neg_half[:, 0:k],
                                    ALU.pow).then_inc(self.rstd_done, 1)

    def finish(self, pool, items):
        for k in range(2):
            pool.wait_ge(self.sent[k], 16 * self.tiles * self.ks * items // 2)

    def count(self, nc, pe, t, s, bank):
        tri, ones = self.g.const_bf[:, C_TRI:C_TRI + P], self.g.const_bf[:, C_ONES:C_ONES + P]
        chosen = self.chosen[:, :, :].rearrange("p t e -> p (t e)")
        n = BATCH_TILES * EXPERTS
        nc.tensor.matmul(bank[:, 0:n], tri, chosen, start=True, stop=False)
        for shift in range(EXPERTS, n, EXPERTS):
            nc.tensor.matmul(bank[:, shift:n], ones, chosen[:, 0:n - shift], start=False, stop=False)
        nc.tensor.matmul(bank[:, 0:n], ones, self.before[:, :].unsqueeze(1).broadcast_to([P, BATCH_TILES, EXPERTS]),
                         start=False, stop=True).then_inc(self.counted, 1)

    def read_counts(self, nc, dve, t, s, bank, neighbour=None):
        if self.batch(t, s + 4):
            n4 = t.batches(s + 4, self.nb)
            dve.wait_ge(self.w_in, self.loads)
            wait(dve, self.counted, n4)
            if neighbour:
                wait(dve, *neighbour)
            nc.vector.tensor_copy(self.counts[:, :, :], bank[:, 0:BATCH_TILES * EXPERTS].rearrange("p (t e) -> p t e", e=EXPERTS)).then_inc(
                self.counts_read, 1)

    def dve(self, nc, dve, t, s, updated):
        g, k, V = self.g, self.tiles, nc.vector
        n0, n1, n3 = t.done(s), t.done(s + 1), t.done(s + 3)
        batch3, batch5 = self.batch(t, s + 3), self.batch(t, s + 5)
        choices = t.batches(s + 3, self.nb) if batch3 else None
        slotted = t.batches(s + 5, self.nb) if batch5 else None

        def tiles(s):
            return bass.ds(t.item(s) * k - (BATCH_TILES - k), BATCH_TILES)

        def over(a):
            return a.unsqueeze(1).broadcast_to([P, BATCH_TILES, EXPERTS])

        def over_experts(a):
            return a.unsqueeze(2).broadcast_to([P, BATCH_TILES, EXPERTS])

        def then(ins, sem, count):
            ins.then_inc(sem, 1)
            dve.wait_ge(self.w_in, self.loads)
            wait(dve, sem, count)

        if t.live(s):
            dve.wait_ge(self.w_in, self.loads)
            wait(dve, updated, n0)
            for tile in range(k):
                last = V.bn_stats(self.st[:, t.par(s), tile, :], g.x[:, bass.ds(t.item(s) * k + tile, 1), :])
            last.then_inc(self.part, 1)
        if batch5:
            link = self.chain(slotted, "slots")
            dve.wait_ge(self.w_in, self.loads)
            wait(dve, self.counts_read, slotted)
            if self.kind == "top2":
                then(V.tensor_tensor(self.ranked[:, :, :], self.counts[:, :, :], over(self.base[:, :]), ALU.add), *link())
            for c in range(self.ks):
                src = self.ranked if self.kind == "top2" else self.counts
                then(V.tensor_tensor(self.cand[:, :, :], self.hot[c][:, :, :], src[:, :, :], ALU.mult), *link())
                then(V.tensor_reduce(self.rank[:, :], self.cand[:, :, :], AX.X, ALU.add), *link())
                if self.kind == "top2":
                    V.tensor_copy(g.put_row[c][:, tiles(s + 5)], self.rank[:, :])
                else:
                    V.tensor_scalar(g.keep[:, tiles(s + 5)], self.rank[:, :], float(CAP), None, ALU.is_le)
                    V.tensor_scalar(self.lost[:, :], self.rank[:, :], float(CAP), float(4 * TOKENS), ALU.is_gt, ALU.mult)
                    then(V.scalar_tensor_tensor(self.slot[:, :], self.rank[:, :], float(CAP), self.expert_base[:, :],
                                                ALU.min, ALU.add), *link())
                    V.tensor_copy(g.get[0][:, tiles(s + 5)], self.slot[:, :])
                    then(V.tensor_tensor(self.rank[:, :], self.slot[:, :], self.lost[:, :], ALU.add), *link())
                last = V.tensor_copy(g.put[c][:, tiles(s + 5)], self.rank[:, :])
            last.then_inc(self.put_done, 1)
        if t.live(s + 3):
            if self.on_dve(t, s + 3):
                dve.wait_ge(self.w_in, self.loads)
                wait(dve, self.xn_done, n3)
                wait(dve, self.summed, t.done(s + 4))
                for tile in range(k):
                    last = V.tensor_tensor(self.prod[:, tile, :, :], self.w_s[:, :, :],
                                           g.xn[:, t.item(s + 3) * k + tile, :].unsqueeze(1).broadcast_to([P, EXPERTS, D]), ALU.mult)
                last.then_inc(self.multiplied, 1)
            dve.wait_ge(self.w_in, self.loads)
            wait(dve, self.multiplied, n3)
            V.tensor_reduce(g.logits[:, bass.ds(t.item(s + 3) * k, k), :], self.prod[:, :, :, :], AX.X, ALU.add).then_inc(self.summed, 1)
        if batch3:
            link = self.chain(choices, "choice")
            logits = g.logits[:, tiles(s + 3), :]
            dve.wait_ge(self.w_in, self.loads)
            wait(dve, self.summed, n3)
            V.tensor_reduce(self.of_batch[:, :], self.chosen[:, :, :].rearrange("p t e -> p e t"), AX.X, ALU.add)
            if self.bias is not None:
                then(V.tensor_tensor(logits, logits, over(self.bias_s[:, :]), ALU.add), *link())
            for c in range(self.ks):
                src = self.rest[:, :, :] if c else logits
                then(V.tensor_reduce(self.topv[:, :], src, AX.X, ALU.max), *link())
                if c == 0:
                    V.tensor_tensor(self.before[:, :], self.before[:, :], self.of_batch[:, :], ALU.add)
                then(V.tensor_tensor(self.cand[:, :, :], src, over_experts(self.topv[:, :]), ALU.is_equal), *link())
                then(V.tensor_tensor(self.cand[:, :, :], self.cand[:, :, :], over(self.rev[:, :]), ALU.mult), *link())
                then(V.tensor_reduce(self.best[:, :], self.cand[:, :, :], AX.X, ALU.max), *link())
                then(V.tensor_tensor(self.hot[c][:, :, :], self.cand[:, :, :], over_experts(self.best[:, :]), ALU.is_equal), *link())
                if c + 1 < self.ks:
                    then(V.tensor_scalar(self.rest[:, :, :], self.hot[c][:, :, :], -BIG, None, ALU.mult), *link())
                    then(V.tensor_tensor(self.rest[:, :, :], self.rest[:, :, :], logits, ALU.add), *link())
            if self.ks == 2:
                last = V.tensor_tensor(self.chosen[:, :, :], self.hot[0][:, :, :], self.hot[1][:, :, :], ALU.add)
            else:
                V.tensor_scalar(self.expert_base[:, :], self.best[:, :], -float(CAP), float(EXPERTS * CAP - 1), ALU.mult, ALU.add)
                last = V.tensor_copy(self.chosen[:, :, :], self.hot[0][:, :, :])
            last.then_inc(self.chosen_done, 1)
        if t.live(s):
            dve.wait_ge(self.w_in, self.loads)
            wait(dve, self.part, n0)
            for tile in range(k):
                last = V.bn_aggr(self.mv[:, t.par(s), tile, :], self.st[:, t.par(s), tile, :])
            last.then_inc(self.stats, 1)
        if t.live(s + 1):
            dve.wait_ge(self.w_in, self.loads)
            wait(dve, self.rstd_done, n1)
            for tile in range(k):
                last = V.tensor_scalar(
                    g.xn[:, bass.ds(t.item(s + 1) * k + tile, 1), :], g.x[:, bass.ds(t.item(s + 1) * k + tile, 1), :],
                    self.mv[:, t.par(s + 1), tile, 0:1], self.rstd[:, t.par(s + 1), tile:tile + 1], ALU.subtract, ALU.mult)
            last.then_inc(self.xn_done, 1)

    def chain(self, count, name):
        at = [0]

        def link():
            at[0] += 1
            key = (name, at[0])
            if key not in self.steps:
                self.steps[key] = self.ph.sem(f"{name}{at[0]}")
            return self.steps[key], count
        return link


def attention_narrow(nc, g, name, gate_col, wq, bq, wk, bk, wv, bv, wo, bo, kind, mask=None, head=None, tail=None):
    ITEMS, TPI = TILES // 2, 2
    SCALE = float(1.0 / np.sqrt(np.float32(8)))
    folded = kind == "masked"
    with ExitStack() as ctx:
        ph = Phase(nc, ctx, name)
        head = head and Head(ph, g, *head)
        tail = tail and Tail(ph, g, *tail, 2)
        wq_s, wk_s, wv_s = ph.sb("wq", [P, D]), ph.sb("wk", [P, D]), ph.sb("wv", [P, 2, 64])
        wo_s = ph.sb("wo", [P, 2, 2, D]) if folded else ph.sb("wo", [P, D])
        bq_s, bk_s = ph.sb("bq", [P, 1]), ph.sb("bk", [P, 1])
        bv_s, bo_s = ph.sb("bv", [P, 64]), ph.sb("bo", [1, D])
        bq_scaled, bk_masked = ph.sb("bq_scaled", [P, 1]), ph.sb("bk_masked", [P, 4])
        ctx_t = ph.sb("ctx_t", [P, 2, 256])
        st, mv = ph.sb("st", [P, 2, TPI, 6]), ph.sb("mv", [P, 2, TPI, 2])
        var_eps, rstd = ph.sb("var_eps", [P, 2, TPI]), ph.sb("rstd", [P, 2, TPI])
        xn, xn_t = ph.sb("xn", [P, 2, TPI, D]), ph.sb("xn_t", [P, 2, 256])
        q_t, k_t = ph.sb("q_t", [P, 2, 256]), ph.sb("k_t", [P, 2, 4, 256])
        val = ph.sb("val", [P, 2, 4, 8, 18])
        prob = ph.sb("prob", [P, 2, 4, TPI, 4, 64])
        top = ph.sb("top", [P, 4, TPI, 4])
        prob_t = ph.sb("prob_t", [P, 16, P])
        recip = ph.sb("recip", [P, TPI, 8, 2])
        ctx_out, ctx_out_t = ph.sb("ctx_out", [P, TPI, D]), ph.sb("ctx_out_t", [P, TPI, P])
        soft = ph.sb("soft", [P, 4, TPI, 4, 64]) if kind == "stable" else None
        if mask is not None:
            mask_raw, limit = ph.sb("mask_raw", [P, TILES, 64], U8), ph.sb("limit", [P, TILES, 64])
        S = ph.ps("S", [P, 4, TPI, 4, 64])
        PT = ph.ps("PT", [P, 2, 512])
        A, B = ph.ps("A", [P, 512]), ph.ps("B", [P, 512])

        weights_in, ready = ph.sem("weights_in"), ph.sem("ready")
        ctx_in = [ph.sem(f"ctx_in{k}") for k in range(2)]
        (stats_part, stats_done, eps_done, rstd_done, xn_done, xt_filled, xt_drained, qk_filled, qk_drained,
         v_filled, v_drained, s_filled, s_drained, s_limited, top_done, shifted, prob_ready, relu_done, log_done, soft_done,
         o_filled, recip_done, o_drained, ot_filled, ot_drained, wo_filled, wo_drained) = ph.sems(
            "stats_part stats_done eps_done rstd_done xn_done xt_filled xt_drained qk_filled qk_drained "
            "v_filled v_drained s_filled s_drained s_limited top_done shifted prob_ready relu_done log_done soft_done "
            "o_filled recip_done o_drained ot_filled ot_drained wo_filled wo_drained")
        pt_filled = [ph.sem(f"pt_filled{k}") for k in range(4)]
        pt_drained = [ph.sem(f"pt_drained{k}") for k in range(4)]
        block = ctx.enter_context(nc.Block())
        LOADED = 16 * (9 + (mask is not None) + folded)
        READY = 5 + (mask is not None)
        UNROLL = tail.nb if tail else 2
        DEPTH = 8
        ident = g.const[:, C_IDENT:C_IDENT + P]

        @block.sync
        def _(sp):
            sp.dma_start(wq_s[:, :], wq).then_inc(weights_in, 16)
            sp.dma_start(wk_s[:, :], wk).then_inc(weights_in, 16)
            sp.dma_start(wv_s[:, :, :], wv).then_inc(weights_in, 16)
            sp.dma_start(bq_s[:, :], bq).then_inc(weights_in, 16)
            sp.dma_start(bk_s[:, :], bk).then_inc(weights_in, 16)
            for h in range(2):
                sp.dma_start(bv_s[64 * h:64 * h + 64, :], bv[h].partition_broadcast(64)).then_inc(weights_in, 16)
            sp.dma_start(bo_s[:, :], bo).then_inc(weights_in, 16)
            if tail:
                tail.load(sp)
            if folded:
                sp.wait_ge(ready, 1)
                for b in range(2):
                    sp.dma_start(wo_s[64 * b:64 * b + 64, b, :, :], wo).then_inc(weights_in, 16)
                sp.dma_start(mask_raw[:, :, :], mask).then_inc(weights_in, 16)
            else:
                sp.dma_start(wo_s[:, :], wo).then_inc(weights_in, 16)
            for h in range(2):
                sp.dma_start(ctx_t[:, h, :], g.ctx_t[:, 256 * h:256 * h + 256]).then_inc(ctx_in[h], 16)

            def step(t):
                done_v = t.done(4)
                if t.live(2):
                    wait(sp, v_filled, done_v)
                    sp.dma_start(ctx_t[:, t.par(2), :], g.ctx_t[:, bass.ds(t.item(2) * 256, 256)]).then_inc(
                        ctx_in[t.par(2)], 16)

            for t in range(4, DEPTH):
                step(Step(sp, ITEMS, t))
            with sp.Fori(0, (ITEMS - DEPTH) // 2) as i:
                for k in range(2):
                    step(Step(sp, ITEMS, DEPTH + k, i))
            for t in range(ITEMS, ITEMS + 2):
                step(Step(sp, ITEMS, t))

        @block.gpsimd
        def _(pool):
            F = 2 if head else 0

            def step(t):
                n0 = t.done(F)
                if head and t.live(0):
                    head.gather(nc, pool, t, 0, ready, READY)
                if head and t.live(1):
                    head.combine(nc, pool, t, 1, ready, READY)
                if t.live(F):
                    pool.wait_ge(ready, READY)
                    wait(pool, stats_done, n0)
                    nc.gpsimd.tensor_tensor(var_eps[:, t.par(F), :], mv[:, t.par(F), :, 1], g.eps[:, 0:TPI],
                                            ALU.add).then_inc(eps_done, 1)
                    pool.wait_ge(ready, READY)
                    wait(pool, eps_done, n0)
                    nc.gpsimd.tensor_tensor(rstd[:, t.par(F), :], var_eps[:, t.par(F), :], g.neg_half[:, 0:TPI],
                                            ALU.pow).then_inc(rstd_done, 1)
                if tail:
                    tail.pool(nc, pool, t, F + 8)

            pipeline(pool, ITEMS, F + 8 + tail.depth() if tail else F + 1, step, UNROLL)
            if tail:
                tail.finish(pool, ITEMS)

        @block.vector
        def _(dve):
            n = nc.vector.memset(wo_s[:, :, :, :] if folded else bk_masked[:, :], 0.0).then_inc(ready, 1)
            nc.vector.memset(val[:, :, :, :, :], 0.0).then_inc(ready, 1)
            dve.wait_ge(ready, 2)
            for h in range(2):
                nc.vector.memset(val[64 * h:64 * h + 64, :, :, :, 16 + h:17 + h], 1.0).then_inc(s_limited, 1)
            dve.wait_ge(s_limited, 2)
            dve.wait_ge(weights_in, LOADED)
            nc.vector.tensor_scalar(bq_scaled[:, :], bq_s[:, :], SCALE, None, ALU.mult).then_inc(ready, 1)
            nc.vector.tensor_tensor(bk_masked[:, :], g.const[:, C_JMASK:C_JMASK + 4], bk_s[:, :].broadcast_to([P, 4]),
                                    ALU.mult).then_inc(ready, 1)
            if mask is not None:
                nc.vector.tensor_scalar(limit[:, :, :], mask_raw[:, :, :], BIG, -1.0e9, ALU.mult, ALU.add).then_inc(ready, 1)
            nc.vector.tensor_copy(recip[:, 0, 0, :], g.const[:, 0:2]).then_inc(ready, 1)
            if tail:
                tail.prepare(nc, dve)

            def flat_all(s, t):
                return prob[:, t.par(s), :, :, :, :].rearrange("p r t j k -> p (r t j k)")

            def step(t):
                n0, n1, n3, n4, n6, n7 = (t.done(s) for s in (0, 1, 3, 4, 6, 7))

                def add_to_stream():
                    dve.wait_ge(ready, READY)
                    wait(dve, wo_filled, n7)
                    src = (A if folded else B)[:, 0:256]
                    xs = g.x[:, bass.ds(t.item(7) * 2, 2), :]
                    nc.vector.scalar_tensor_tensor(xs, src.rearrange("p (t d) -> p t d", t=2), g.gate[:, gate_col:gate_col + 1],
                                                   xs, ALU.mult, ALU.add).then_inc(wo_drained, 1)

                def copy_counts():
                    if tail:
                        tail.read_counts(nc, dve, t, 8, A[:, 256:512], t.live(4) and (v_filled, n4))

                def copy_values():
                    copy_counts()
                    dve.wait_ge(ready, READY)
                    wait(dve, v_filled, n4)
                    for h in range(2):
                        rows = slice(64 * h, 64 * h + 64)
                        last = nc.vector.tensor_tensor(
                            val[rows, t.par(4), :, :, 8 * h:8 * h + 8],
                            A[rows, 0:256].rearrange("p (b h c) -> p b h c", b=4, h=8),
                            bv_s[rows, :].rearrange("p (h c) -> p h c", h=8).unsqueeze(1).broadcast_to([64, 4, 8, 8]),
                            ALU.add)
                    last.then_inc(v_drained, 1)

                if folded and t.live(7):
                    add_to_stream()
                if t.live(6):
                    o = B[:, 0:288].rearrange("p (t h c) -> p t h c", t=2, h=8)
                    dve.wait_ge(ready, READY)
                    wait(dve, o_filled, n6)
                    nc.vector.reciprocal(recip[:, :, :, :], o[:, :, :, 16:18]).then_inc(recip_done, 1)
                    dve.wait_ge(ready, READY)
                    wait(dve, recip_done, n6)
                    for tile in range(2):
                        last = nc.vector.tensor_tensor(
                            ctx_out[:, tile, :].rearrange("p (h two c) -> p h two c", h=8, two=2),
                            o[:, tile, :, 0:16].rearrange("p h (two c) -> p h two c", two=2),
                            recip[:, tile, :, :].unsqueeze(3).broadcast_to([P, 8, 2, 8]), ALU.mult)
                    last.then_inc(o_drained, 1)
                if t.live(4):
                    pr = prob[:, t.par(4), :, :, :, :]
                    flat = pr.rearrange("p r t j k -> p (r t j) k")
                    src = S[:, :, :, :, :].rearrange("p r t j k -> p (r t j) k")
                    topf = top[:, :, :, :].rearrange("p r t j -> p (r t j)")
                    if kind == "stable":
                        dve.wait_ge(ready, READY)
                        wait(dve, relu_done, n4)
                        nc.vector.tensor_scalar(pr.rearrange("p r t j k -> p (r t j k)"),
                                                S[:, :, :, :, :].rearrange("p r t j k -> p (r t j k)"),
                                                0.0, None, ALU.max).then_inc(s_drained, 1)
                    else:
                        dve.wait_ge(ready, READY)
                        wait(dve, s_filled, n4)
                        if mask is not None:
                            for tile in range(2):
                                last = nc.vector.tensor_tensor(
                                    pr[:, :, tile, :, :], S[:, :, tile, :, :],
                                    limit[:, bass.ds(t.item(4) * 2 + tile, 1), :].unsqueeze(1).broadcast_to([P, 4, 4, 64]),
                                    ALU.min)
                            last.then_inc(s_drained, 1)
                            copy_values()
                            src = flat
                            dve.wait_ge(ready, READY)
                            wait(dve, s_drained, n4)
                        nc.vector.tensor_reduce(topf, src, AX.X, ALU.max).then_inc(top_done, 1)
                        dve.wait_ge(ready, READY)
                        wait(dve, top_done, n4)
                        last = nc.vector.tensor_tensor(flat, src, topf.unsqueeze(2).broadcast_to([P, 32, 64]), ALU.subtract)
                        last.then_inc(shifted if mask is not None else s_drained, 1)
                if t.live(4) and mask is None:
                    copy_values()
                if not t.live(4):
                    copy_counts()
                if not folded and t.live(7):
                    add_to_stream()
                if tail and folded:
                    tail.dve(nc, dve, t, 8, wo_drained)
                if tail and not folded:
                    tail.dve(nc, dve, t, 8, wo_drained)
                if t.live(1):
                    dve.wait_ge(ready, READY)
                    wait(dve, rstd_done, n1)
                    wait(dve, xt_filled, n3)
                    for tile in range(2):
                        last = nc.vector.tensor_scalar(
                            xn[:, t.par(1), tile, :].unsqueeze(1), g.x[:, bass.ds(t.item(1) * 2 + tile, 1), :],
                            mv[:, t.par(1), tile, 0:1], rstd[:, t.par(1), tile:tile + 1], ALU.subtract, ALU.mult)
                    last.then_inc(xn_done, 1)
                if t.live(0):
                    if head:
                        dve.wait_ge(ready, READY)
                        wait(dve, head.combined, n0)
                    for tile in range(2):
                        last = nc.vector.bn_stats(st[:, t.par(0), tile, :], g.x[:, bass.ds(t.item(0) * 2 + tile, 1), :])
                    last.then_inc(stats_part, 1)
                    dve.wait_ge(ready, READY)
                    wait(dve, stats_part, n0)
                    for tile in range(2):
                        last = nc.vector.bn_aggr(mv[:, t.par(0), tile, :], st[:, t.par(0), tile, :])
                    last.then_inc(stats_done, 1)
                if t.live(4) and kind == "stable":
                    dve.wait_ge(ready, READY)
                    wait(dve, soft_done, n4)
                    nc.vector.tensor_tensor(flat_all(4, t), flat_all(4, t), soft[:, :, :, :, :].rearrange("p r t j k -> p (r t j k)"),
                                            ALU.add).then_inc(prob_ready, 1)

            pipeline(dve, ITEMS, DEPTH + 6 if tail else DEPTH, step, UNROLL)
            if tail:
                tail.totals(nc, dve, ITEMS)

        @block.scalar
        def _(act):
            if kind == "stable":
                nc.scalar.preload_act_table_set("natural_log_exp_and_others")
            def step(t):
                n2, n3, n4, n5, n6 = t.done(2), t.done(3), t.done(4), t.done(5), t.done(6)
                if kind == "stable" and t.live(4):
                    act.wait_ge(ready, READY)
                    wait(act, s_filled, n4)
                    wait(act, prob_ready, n5)
                    nc.scalar.activation(soft[:, :, :, :, :].rearrange("p r t j k -> p (r t j k)"),
                                         S[:, :, :, :, :].rearrange("p r t j k -> p (r t j k)"), ACT.Relu,
                                         scale=-1.0).then_inc(relu_done, 1)
                if t.live(2):
                    act.wait_ge(ready, READY)
                    wait(act, xt_filled, n2)
                    nc.scalar.copy(xn_t[:, t.par(2), :], A[:, 0:256]).then_inc(xt_drained, 1)
                if t.live(3):
                    act.wait_ge(ready, READY)
                    wait(act, qk_filled, n3)
                    nc.scalar.activation(q_t[:, t.par(3), :], B[:, 0:256], ACT.Identity, bias=bq_scaled[:, :], scale=SCALE)
                    for j in range(4):
                        last = nc.scalar.activation(k_t[:, t.par(3), j, :], B[:, 256:512], ACT.Identity,
                                                    bias=bk_masked[:, j:j + 1], scale=g.const[:, C_JMASK + j:C_JMASK + j + 1])
                    last.then_inc(qk_drained, 1)
                if t.live(5):
                    for c in range(4):
                        act.wait_ge(ready, READY)
                        wait(act, pt_filled[c], n5)
                        nc.scalar.copy(prob_t[:, 4 * c:4 * c + 4, :], PT[:, c % 2, :].rearrange("p (a q) -> p a q", a=4)).then_inc(
                            pt_drained[c], 1)
                if t.live(6) and not folded:
                    act.wait_ge(ready, READY)
                    wait(act, ot_filled, n6)
                    nc.scalar.copy(ctx_out_t[:, :, :], A[:, 0:256].rearrange("p (t q) -> p t q", t=2)).then_inc(ot_drained, 1)
                if t.live(4):
                    flat = prob[:, t.par(4), :, :, :, :].rearrange("p r t j k -> p (r t j k)")
                    if kind == "stable":
                        sf = soft[:, :, :, :, :].rearrange("p r t j k -> p (r t j k)")
                        act.wait_ge(ready, READY)
                        wait(act, relu_done, n4)
                        nc.scalar.activation(sf, sf, ACT.Ln, bias=g.const[:, C_ONES:C_ONES + 1]).then_inc(log_done, 1)
                        act.wait_ge(ready, READY)
                        wait(act, log_done, n4)
                        nc.scalar.activation(sf, sf, ACT.Exp, scale=-1.0).then_inc(soft_done, 1)
                    else:
                        act.wait_ge(ready, READY)
                        wait(act, shifted if mask is not None else s_drained, n4)
                        nc.scalar.activation(flat, flat, ACT.Exp).then_inc(prob_ready, 1)

            pipeline(act, ITEMS, DEPTH, step)

        @block.tensor
        def _(pe):
            def step(t):
                n2, n3, n4, n5, n6, n7 = (t.done(s) for s in range(2, 8))
                n8 = t.done(8) if t.i is None else None
                ranks_next = tail and tail.batch(t, 12)
                chosen = t.batches(12, tail.nb) if ranks_next else None
                counts_read = tail.counts_read if tail else v_drained
                ranks_before, ranks = (t.batches(13, tail.nb), t.batches(12, tail.nb)) if tail and t.i is None else (0, 0)
                context_landed = t.landed(3)
                def bank_read(*reads):
                    if t.i is None:
                        for sem, count in reads:
                            wait(pe, sem, count)

                if t.live(4):
                    pe.wait_ge(ready, READY)
                    wait(pe, qk_drained, n4)
                    wait(pe, s_drained, n5)
                    for tile in range(2):
                        for r in range(4):
                            for b in range(2):
                                rows = slice(32 * r, 32 * r + 32)
                                seq = slice(128 * tile + 64 * b, 128 * tile + 64 * b + 64)
                                last = nc.tensor.matmul(S[64 * b:64 * b + 64, r, tile, :, :], q_t[rows, t.par(4), seq],
                                                        k_t[rows, t.par(4), :, seq], start=True, stop=True)
                    last.then_inc(s_filled, 1)
                if t.live(2):
                    pe.wait_ge(ready, READY)
                    wait(pe, xn_done, n2)
                    wait(pe, wo_drained if folded else ot_drained, n7)
                    bank_read((xt_drained, n3), (v_drained, n5), (counts_read, ranks_before))
                    for tile in range(2):
                        last = nc.tensor.transpose(A[:, P * tile:P * tile + P], xn[:, t.par(2), tile, :], ident)
                    last.then_inc(xt_filled, 1)
                if t.live(3):
                    pe.wait_ge(ready, READY)
                    wait(pe, xt_drained, n3)
                    wait(pe, ctx_in[t.par(3)], context_landed)
                    wait(pe, o_drained, n6)
                    bank_read((qk_drained, n4), (wo_drained, n8))
                    nc.tensor.matmul(B[:, 0:256], wq_s[:, :], xn_t[:, t.par(3), :], start=True, stop=True)
                    nc.tensor.matmul(B[:, 256:512], wk_s[:, :], ctx_t[:, t.par(3), :], start=True, stop=True).then_inc(
                        qk_filled, 1)

                def transpose_probabilities(c):
                    pe.wait_ge(ready, READY)
                    wait(pe, prob_ready, n5)
                    wait(pe, pt_drained[(c + 2) % 4], n6 if c < 2 else n5)
                    for a in range(4):
                        last = nc.tensor.transpose(
                            PT[:, c % 2, P * a:P * a + P],
                            prob[:, t.par(5), c, a // 2, 2 * (a % 2):2 * (a % 2) + 2, :].rearrange("p j k -> p (j k)"), ident)
                    last.then_inc(pt_filled[c], 1)

                if t.live(5):
                    transpose_probabilities(0)
                    transpose_probabilities(1)
                if ranks_next:
                    pe.wait_ge(ready, READY)
                    wait(pe, tail.chosen_done, chosen)
                    wait(pe, xt_drained, n2)
                    bank_read((v_drained, n5), (wo_drained if folded else ot_drained, n7), (counts_read, ranks_before))
                    tail.count(nc, pe, t, 8, A[:, 256:512])
                if t.live(4):
                    pe.wait_ge(ready, READY)
                    wait(pe, xt_drained, n2)
                    bank_read((v_drained, n5), (wo_drained if folded else ot_drained, n7))
                    for b in range(4):
                        for h in range(2):
                            last = nc.tensor.matmul(A[64 * h:64 * h + 64, 64 * b:64 * b + 64],
                                                    ctx_t[:, t.par(4), 64 * b:64 * b + 64], wv_s[:, h, :],
                                                    start=True, stop=True)
                    last.then_inc(v_filled, 1)
                if t.live(7) and not folded:
                    pe.wait_ge(ready, READY)
                    wait(pe, ot_drained, n7)
                    wait(pe, qk_drained, n3)
                    bank_read((o_drained, n6), (wo_drained, n8))
                    nc.tensor.matmul(B[:, 0:256], g.const[0:1, C_ONES:C_ONES + P], bo_s[:, :].unsqueeze(1).broadcast_to([1, 2, D]),
                                     start=True, stop=False)
                    for tile in range(2):
                        last = nc.tensor.matmul(B[:, P * tile:P * tile + P], ctx_out_t[:, tile, :], wo_s[:, :],
                                                start=False, stop=tile == 1)
                    last.then_inc(wo_filled, 1)
                if t.live(5):
                    transpose_probabilities(2)
                    transpose_probabilities(3)
                if t.live(6):
                    pe.wait_ge(ready, READY)
                    wait(pe, o_drained, n6)
                    wait(pe, v_drained, n4)
                    bank_read((xt_drained, n2), (wo_drained if folded else ot_drained, n7), (counts_read, ranks))
                    if folded:
                        for b in range(2):
                            out = A[64 * b:64 * b + 64, 0:256]
                            nc.tensor.matmul(out, g.const[0:1, C_ONES:C_ONES + 64], bo_s[:, :].unsqueeze(1).broadcast_to([1, 2, D]),
                                             start=True, stop=False)
                            for tile in range(2):
                                for c in range(2):
                                    last = nc.tensor.matmul(out[:, P * tile:P * tile + P], ctx_out[:, tile, c:P:2],
                                                            wo_s[:, b, c, :], start=False, stop=(tile, c) == (1, 1))
                        last.then_inc(wo_filled, 1)
                    else:
                        for tile in range(2):
                            last = nc.tensor.transpose(A[:, P * tile:P * tile + P], ctx_out[:, tile, :], ident)
                        last.then_inc(ot_filled, 1)
                if t.live(5):
                    pe.wait_ge(ready, READY)
                    wait(pe, pt_drained[2], n5)
                    wait(pe, pt_drained[3], n5)
                    wait(pe, v_drained, n5)
                    if folded:
                        wait(pe, qk_drained, n3)
                    else:
                        wait(pe, wo_drained, n7)
                    bank_read((qk_drained, n3), (o_drained, n6))
                    for tile in range(2):
                        for b in range(2):
                            for hp in range(8):
                                col = 144 * tile + 18 * hp
                                last = nc.tensor.matmul(
                                    B[64 * b:64 * b + 64, col:col + 18],
                                    prob_t[:, 4 * (hp // 2) + 2 * tile + hp % 2, 64 * b:64 * b + 64],
                                    val[:, t.par(5), 2 * tile + b, hp, :], start=True, stop=True)
                    last.then_inc(o_filled, 1)

            pipeline(pe, ITEMS, DEPTH + 5 if tail else DEPTH, step, UNROLL)



def attention_wide(nc, g, t_in, router):
    ITEMS, DEPTH = TILES, 8
    SCALE = 1.0 / 8.0
    with ExitStack() as ctx:
        ph = Phase(nc, ctx, "l0")
        tail = Tail(ph, g, *router, 1)
        wq_s, wk_s = ph.sb("wq", [P, 8, P]), ph.sb("wk", [P, 8, P])
        wv_s, wo_s = ph.sb("wv", [P, 2, 512]), ph.sb("wo", [P, 8, D])
        ctx_t = ph.sb("ctx_t", [P, 2, P])
        st, mv = ph.sb("st", [P, 2, 6]), ph.sb("mv", [P, 2, 2])
        var_eps, rstd = ph.sb("var_eps", [P, 2]), ph.sb("rstd", [P, 2])
        xn, xn_t = ph.sb("xn", [P, 2, D]), ph.sb("xn_t", [P, 2, P])
        q_t, k_t = ph.sb("q_t", [P, 2, 8, P]), ph.sb("k_t", [P, 2, 8, P])
        val = ph.sb("val", [P, 2, 2, 8, 64])
        prob = ph.sb("prob", [P, 2, 8, 2, 64])
        top, total, recip = ph.sb("top", [P, 2, 8]), ph.sb("total", [P, 2, 8, 2]), ph.sb("recip", [P, 8, 2])
        prob_t = ph.sb("prob_t", [P, 8, P])
        ctx_out, ctx_out_t = ph.sb("ctx_out", [P, 8, 2, 64]), ph.sb("ctx_out_t", [P, 8, P])
        S, O = ph.ps("S", [P, 2, 8, 64]), ph.ps("O", [P, 2, 8, 64])
        R = ph.ps("R", [P, 4, 512])
        first_v = g.slots[0:TOKENS].rearrange("(n p a) d -> n p (a d)", n=DEPTH, p=P)
        slots_v = g.slots[TOKENS:PAD_ROWS].rearrange("r d -> (r d)").rearrange("(n p a) -> n p a", n=ITEMS, p=P)
        zeros = ph.sb("zeros", [P, first_v.shape[2]])
        weights_in, ready, zeroed, rows_zeroed, first_zeroed = ph.sems("weights_in ready zeroed rows_zeroed first_zeroed")
        UNROLL = tail.nb
        tail.slots_clear = (first_zeroed, 16 * DEPTH)
        ctx_in = [ph.sem(f"ctx_in{k}") for k in range(2)]
        (stats_part, stats_done, eps_done, rstd_done, xn_done, s_filled, s_drained, top_done, prob_ready,
         total_done, o_filled, recip_done, o_drained) = ph.sems(
            "stats_part stats_done eps_done rstd_done xn_done s_filled s_drained top_done prob_ready "
            "total_done o_filled recip_done o_drained")
        BANKS = [[("q0", 3), ("v0", 4), ("pt1", 5)], [("q1", 3), ("v1", 4), ("wo", 7)],
                 [("k0", 3), ("xt", 2), ("ot0", 6)], [("k1", 3), ("pt0", 5), ("ot1", 6)]]
        filled = {n: ph.sem(n + "_filled") for uses in BANKS for n, _ in uses}
        drained = {n: ph.sem(n + "_drained") for uses in BANKS for n, _ in uses}
        where = {n: b for b, uses in enumerate(BANKS) for n, _ in uses}
        ident = g.const[:, C_IDENT:C_IDENT + P]
        block = ctx.enter_context(nc.Block())

        @block.sync
        def _(sp):
            sp.dma_start(wq_s[:, :, :], t_in["L0_wq"].rearrange("d (c n) -> d c n", c=8)).then_inc(weights_in, 16)
            sp.dma_start(wk_s[:, :, :], t_in["L0_wk"].rearrange("d (c n) -> d c n", c=8)).then_inc(weights_in, 16)
            sp.dma_start(wv_s[:, :, :], t_in["L0_wv"]).then_inc(weights_in, 16)
            sp.dma_start(wo_s[:, :, :], t_in["L0_wo"].rearrange("(c p) d -> p c d", p=P)).then_inc(weights_in, 16)
            tail.load(sp)
            sp.wait_ge(zeroed, 1)

            def step(t):
                values = t.done(4)
                if t.live(2):
                    wait(sp, filled["v1"], values)
                    sp.dma_start(ctx_t[:, t.par(2), :], g.ctx_t[:, bass.ds(t.item(2) * P, P)]).then_inc(ctx_in[t.par(2)], 16)
                if t.i is None and t.t < DEPTH:
                    sp.dma_start(first_v[t.t], zeros[:, :]).then_inc(first_zeroed, 16)
                if t.live(0):
                    sp.dma_start(slots_v[bass.ds(t.item(0), 1)].rearrange("n p a -> (n p) a"), zeros[:, 0:slots_v.shape[2]]).then_inc(
                        rows_zeroed, 16)

            pipeline(sp, ITEMS, DEPTH, step)
            sp.wait_ge(rows_zeroed, 16 * ITEMS)

        @block.gpsimd
        def _(pool):
            def step(t):
                n0 = t.done(0)
                if t.live(0):
                    pool.wait_ge(ready, 1)
                    wait(pool, stats_done, n0)
                    nc.gpsimd.tensor_tensor(var_eps[:, t.par(0):t.par(0) + 1], mv[:, t.par(0), 1:2], g.eps[:, 0:1],
                                            ALU.add).then_inc(eps_done, 1)
                    pool.wait_ge(ready, 1)
                    wait(pool, eps_done, n0)
                    nc.gpsimd.tensor_tensor(rstd[:, t.par(0):t.par(0) + 1], var_eps[:, t.par(0):t.par(0) + 1],
                                            g.neg_half[:, 0:1], ALU.pow).then_inc(rstd_done, 1)
                tail.pool(nc, pool, t, 8)

            pipeline(pool, ITEMS, 8 + tail.depth(), step, UNROLL)
            tail.finish(pool, ITEMS)

        @block.vector
        def _(dve):
            nc.vector.memset(zeros[:, :], 0.0).then_inc(zeroed, 1)
            dve.wait_ge(weights_in, 64)
            nc.vector.tensor_copy(recip[:, 0, :], g.const[:, 0:2]).then_inc(ready, 1)
            tail.prepare(nc, dve)

            def step(t):
                n0, n1, n2, n3, n4, n5, n6, n7 = (t.done(s) for s in range(8))

                def copy_out(name, count, out):
                    dve.wait_ge(ready, 1)
                    wait(dve, filled[name], count)
                    nc.vector.tensor_copy(out, R[:, where[name], :].rearrange("p (c n) -> p c n", c=4)).then_inc(drained[name], 1)

                if t.live(6):
                    dve.wait_ge(ready, 1)
                    wait(dve, total_done, n6)
                    nc.vector.reciprocal(recip[:, :, :], total[:, t.par(6), :, :]).then_inc(recip_done, 1)
                    dve.wait_ge(ready, 1)
                    wait(dve, recip_done, n6)
                    wait(dve, o_filled, n6)
                    nc.vector.tensor_tensor(ctx_out[:, :, :, :], O[:, :, :, :].rearrange("p a h c -> p h a c"),
                                            recip[:, :, :].unsqueeze(3).broadcast_to([P, 8, 2, 64]), ALU.mult).then_inc(o_drained, 1)
                if t.live(1):
                    dve.wait_ge(ready, 1)
                    wait(dve, rstd_done, n1)
                    wait(dve, filled["xt"], n3)
                    nc.vector.tensor_scalar(xn[:, t.par(1), :].unsqueeze(1), g.x[:, bass.ds(t.item(1), 1), :],
                                            mv[:, t.par(1), 0:1], rstd[:, t.par(1):t.par(1) + 1],
                                            ALU.subtract, ALU.mult).then_inc(xn_done, 1)
                if t.live(0):
                    nc.vector.bn_stats(st[:, t.par(0), :], g.x[:, bass.ds(t.item(0), 1), :]).then_inc(stats_part, 1)
                    dve.wait_ge(ready, 1)
                    wait(dve, stats_part, n0)
                    nc.vector.bn_aggr(mv[:, t.par(0), :], st[:, t.par(0), :]).then_inc(stats_done, 1)
                if t.live(3):
                    copy_out("k1", n3, k_t[:, t.par(3), 4:8, :])
                tail.read_counts(nc, dve, t, 8, R[:, where["xt"], P:512], t.live(2) and (filled["xt"], n2))
                if t.live(2):
                    dve.wait_ge(ready, 1)
                    wait(dve, filled["xt"], n2)
                    nc.vector.tensor_copy(xn_t[:, t.par(2), :], R[:, where["xt"], 0:P]).then_inc(drained["xt"], 1)
                if t.live(5):
                    dve.wait_ge(ready, 1)
                    wait(dve, prob_ready, n5)
                    nc.vector.tensor_reduce(total[:, t.par(5), :, :], prob[:, t.par(5), :, :, :], AX.X, ALU.add).then_inc(total_done, 1)
                tail.dve(nc, dve, t, 8, drained["wo"])
                if t.live(7):
                    dve.wait_ge(ready, 1)
                    wait(dve, filled["wo"], n7)
                    xs = g.x[:, bass.ds(t.item(7), 1), :]
                    nc.vector.scalar_tensor_tensor(xs, R[:, where["wo"], 0:D].unsqueeze(1), g.gate[:, 0:1], xs,
                                                   ALU.mult, ALU.add).then_inc(drained["wo"], 1)
                if t.live(4):
                    dve.wait_ge(ready, 1)
                    wait(dve, s_filled, n4)
                    nc.vector.tensor_reduce(top[:, :, :], S[:, :, :, :], AX.X, ALU.max).then_inc(top_done, 1)
                    dve.wait_ge(ready, 1)
                    wait(dve, top_done, n4)
                    nc.vector.tensor_tensor(prob[:, t.par(4), :, :, :].rearrange("p h a k -> p a h k"), S[:, :, :, :],
                                            top[:, :, :].unsqueeze(3).broadcast_to([P, 2, 8, 64]), ALU.subtract).then_inc(s_drained, 1)
                if t.live(6):
                    copy_out("ot1", n6, ctx_out_t[:, 4:8, :])

            pipeline(dve, ITEMS, DEPTH + 6, step, UNROLL)

        @block.scalar
        def _(act):
            def step(t):
                n3, n4, n5, n6 = (t.done(s) for s in range(3, 7))

                def copy_out(name, count, out, scale=1.0):
                    act.wait_ge(ready, 1)
                    wait(act, filled[name], count)
                    nc.scalar.activation(out, R[:, where[name], :].rearrange("p (c n) -> p c n", c=out.shape[1]), ACT.Copy,
                                         scale=scale).then_inc(drained[name], 1)

                if t.live(3):
                    copy_out("q0", n3, q_t[:, t.par(3), 0:4, :], SCALE)
                    copy_out("q1", n3, q_t[:, t.par(3), 4:8, :], SCALE)
                    copy_out("k0", n3, k_t[:, t.par(3), 0:4, :])
                if t.live(4):
                    copy_out("v0", n4, val[:, t.par(4), 0, :, :])
                    copy_out("v1", n4, val[:, t.par(4), 1, :, :])
                if t.live(5):
                    copy_out("pt0", n5, prob_t[:, 0:4, :])
                    copy_out("pt1", n5, prob_t[:, 4:8, :])
                if t.live(6):
                    copy_out("ot0", n6, ctx_out_t[:, 0:4, :])
                if t.live(4):
                    flat = prob[:, t.par(4), :, :, :].rearrange("p h a k -> p (h a k)")
                    act.wait_ge(ready, 1)
                    wait(act, s_drained, n4)
                    nc.scalar.activation(flat, flat, ACT.Exp).then_inc(prob_ready, 1)

            pipeline(act, ITEMS, DEPTH, step)

        @block.tensor
        def _(pe):
            def step(t):
                n2, n3, n4, n5, n6, n7, n8 = (t.done(s) for s in range(2, 9))
                ranks_next = tail.batch(t, 12)
                chosen = t.batches(12, tail.nb) if ranks_next or t.i is None else None
                ranks_before = t.batches(13, tail.nb) if t.i is None else None
                context_landed = t.landed(3)

                def claim(name):
                    uses = BANKS[where[name]]
                    at = [n for n, _ in uses].index(name)
                    before = uses[at - 1:at] if at else uses[-1:]
                    for n, s in (before if t.i is not None else uses):
                        wait(pe, drained[n], t.done(s) if n in [m for m, _ in uses[:at]] else t.done(s + 1))
                    if t.i is None and where[name] == where["xt"]:
                        wait(pe, tail.counts_read, chosen if name == "ot0" else ranks_before)
                    return R[:, where[name], :]

                if t.live(3):
                    for c, (name, w, src) in enumerate((("q0", wq_s, xn_t), ("q1", wq_s, xn_t), ("k0", wk_s, ctx_t), ("k1", wk_s, ctx_t))):
                        pe.wait_ge(ready, 1)
                        if c == 0:
                            wait(pe, drained["xt"], n3)
                        if c == 2:
                            wait(pe, ctx_in[t.par(3)], context_landed)
                        bank = claim(name)
                        for k in range(4):
                            last = nc.tensor.matmul(bank[:, P * k:P * k + P], w[:, 4 * (c % 2) + k, :], src[:, t.par(3), :],
                                                    start=True, stop=True)
                        last.then_inc(filled[name], 1)
                if t.live(4):
                    for b in range(2):
                        pe.wait_ge(ready, 1)
                        bank = claim(f"v{b}")
                        for h in range(2):
                            last = nc.tensor.matmul(bank[64 * h:64 * h + 64, :], ctx_t[:, t.par(4), 64 * b:64 * b + 64],
                                                    wv_s[:, h, :], start=True, stop=True)
                        last.then_inc(filled[f"v{b}"], 1)
                if ranks_next:
                    pe.wait_ge(ready, 1)
                    wait(pe, tail.chosen_done, chosen)
                    bank = claim("xt")
                    tail.count(nc, pe, t, 8, bank[:, P:512])
                if t.live(2):
                    pe.wait_ge(ready, 1)
                    wait(pe, xn_done, n2)
                    bank = claim("xt")
                    nc.tensor.transpose(bank[:, 0:P], xn[:, t.par(2), :], ident).then_inc(filled["xt"], 1)
                if t.live(5):
                    for c in range(2):
                        pe.wait_ge(ready, 1)
                        wait(pe, prob_ready, n5)
                        bank = claim(f"pt{c}")
                        for k in range(4):
                            last = nc.tensor.transpose(bank[:, P * k:P * k + P],
                                                       prob[:, t.par(5), 4 * c + k, :, :].rearrange("p a k -> p (a k)"), ident)
                        last.then_inc(filled[f"pt{c}"], 1)
                if t.live(7):
                    pe.wait_ge(ready, 1)
                    wait(pe, drained["ot1"], n7)
                    wait(pe, drained["ot0"], n7)
                    bank = claim("wo")
                    for k in range(8):
                        last = nc.tensor.matmul(bank[:, 0:D], ctx_out_t[:, k, :], wo_s[:, k, :], start=k == 0, stop=k == 7)
                    last.then_inc(filled["wo"], 1)
                if t.live(4):
                    pe.wait_ge(ready, 1)
                    wait(pe, drained["q1"], n4)
                    wait(pe, drained["k0"], n4)
                    wait(pe, drained["k1"], n4)
                    wait(pe, s_drained, n5)
                    for k in range(8):
                        for b in range(2):
                            for h in range(2):
                                rows = slice(64 * h, 64 * h + 64)
                                last = nc.tensor.matmul(S[64 * b:64 * b + 64, h, k, :], q_t[rows, t.par(4), k, 64 * b:64 * b + 64],
                                                        k_t[rows, t.par(4), k, 64 * b:64 * b + 64], start=True, stop=True)
                    last.then_inc(s_filled, 1)
                if t.live(6):
                    for c in range(2):
                        pe.wait_ge(ready, 1)
                        wait(pe, o_drained, n6)
                        bank = claim(f"ot{c}")
                        for k in range(4):
                            last = nc.tensor.transpose(bank[:, P * k:P * k + P],
                                                       ctx_out[:, 4 * c + k, :, :].rearrange("p a c -> p (a c)"), ident)
                        last.then_inc(filled[f"ot{c}"], 1)
                if t.live(5):
                    pe.wait_ge(ready, 1)
                    wait(pe, drained["pt0"], n5)
                    wait(pe, drained["pt1"], n5)
                    wait(pe, drained["v1"], n5)
                    wait(pe, o_drained, n6)
                    for k in range(8):
                        for b in range(2):
                            for h in range(2):
                                rows = slice(64 * h, 64 * h + 64)
                                last = nc.tensor.matmul(O[64 * b:64 * b + 64, h, k, :], prob_t[rows, k, 64 * b:64 * b + 64],
                                                        val[rows, t.par(5), b, k, :], start=True, stop=True)
                    last.then_inc(o_filled, 1)

            pipeline(pe, ITEMS, DEPTH + 5, step, UNROLL)



def weigh(nc, g, name, kind, gate_col):
    T, E = TILES, EXPERTS
    ks = 2 if kind == "top2" else 1
    with ExitStack() as ctx:
        ph = Phase(nc, ctx, name)
        cand = ph.sb("cand", [P, T, E])
        topv, scaled = ph.sb("topv", [P, T]), ph.sb("scaled", [P, T])
        soft, soft_sum, second = ph.sb("soft", [P, T, E]), ph.sb("soft_sum", [P, T]), ph.sb("second", [P, T])
        zeros, zero_rows = ph.sb("zeros", [P, E]), ph.sb("zero_rows", [P, SUB, D])
        total, blocks = ph.sb("total", [P, E]), ph.sb("blocks", [P, E, 16])
        nblk, start, start_row = ph.sb("nblk", [P, E]), ph.sb("start", [P, E]), ph.sb("start_row", [P, E])
        item_cmp = ph.sb("item_cmp", [P, TOP2_TILES, E])
        shift, shift_step = ph.sb("shift", [P, E + 1]), ph.sb("shift_step", [P, E])
        expert, row, used = ph.sb("expert", [P, TOP2_TILES]), ph.sb("row", [P, TOP2_TILES]), ph.sb("used", [P, TOP2_TILES])
        end_row = ph.sb("end_row", [P, E], I32)
        TOT = ph.ps("TOT", [P, E])
        shifted, soft_ready, diff_ready, diff_exp, chained, counted, ends_known, rows_zeroed = ph.sems(
            "shifted soft_ready diff_ready diff_exp chained counted ends_known rows_zeroed")
        block = ctx.enter_context(nc.Block())
        V = nc.vector

        @block.sync
        def _(sp):
            if ks == 2:
                sp.wait_ge(ends_known, 1)
                for e in range(E):
                    end = sp.value_load(end_row[0:1, e:e + 1], min_val=PAD_ROWS, max_val=PAD_ROWS + E * REGION - SLOTS)
                    sp.dma_start(g.slots[bass.ds(end, SLOTS)].rearrange("(p s) d -> p s d", s=SUB), zero_rows[:, :, :]).then_inc(
                        rows_zeroed, 16)
                sp.wait_ge(rows_zeroed, 16 * E)

        @block.vector
        def _(dve):
            done = [0]

            def then(ins):
                done[0] += 1
                ins.then_inc(chained, 1)
                dve.wait_ge(chained, done[0])

            gate = g.gate[:, gate_col:gate_col + 1]
            if kind == "first":
                then(V.tensor_scalar(g.weight[0][:, :], g.keep[:, :], gate, None, ALU.mult))
                then(V.tensor_scalar(g.weight[1][:, :], g.weight[0][:, :], -1.0, gate, ALU.mult, ALU.add))
                return
            then(V.tensor_reduce(topv[:, :], g.logits[:, :, :], AX.X, ALU.max))
            V.tensor_tensor(soft[:, :, :], g.logits[:, :, :], topv[:, :].unsqueeze(2).broadcast_to([P, T, E]),
                            ALU.subtract).then_inc(shifted, 1)
            if ks == 2:
                V.memset(zeros[:, :], 0.0)
                V.memset(shift[:, 0:1], 0.0)
                then(V.memset(zero_rows[:, :, :], 0.0))
                dve.wait_ge(counted, 1)
                then(V.tensor_copy(total[:, :], TOT[:, :]))
                then(V.tensor_tensor(blocks[:, :, :], total[:, :].unsqueeze(2).broadcast_to([P, E, 16]),
                                     g.const[:, C_BLK:C_BLK + 16].unsqueeze(1).broadcast_to([P, E, 16]), ALU.is_gt))
                then(V.tensor_reduce(nblk[:, :], blocks[:, :, :], AX.X, ALU.add))
                then(V.tensor_scalar(start_row[:, :], g.const[:, C_ECOL:C_ECOL + E], float(REGION), float(PAD_ROWS),
                                     ALU.mult, ALU.add))
                then(V.tensor_tensor(total[:, :], total[:, :], start_row[:, :], ALU.add))
                V.tensor_copy(end_row[:, :], total[:, :]).then_inc(ends_known, 1)
                then(V.tensor_tensor_scan(start[:, :], nblk[:, :], zeros[:, :], 0.0, ALU.add, ALU.add))
                items = g.const[:, C_ITEM:C_ITEM + TOP2_TILES]
                then(V.tensor_tensor(item_cmp[:, :, :], items.unsqueeze(2).broadcast_to([P, TOP2_TILES, E]),
                                     start[:, :].unsqueeze(1).broadcast_to([P, TOP2_TILES, E]), ALU.is_ge))
                then(V.tensor_reduce(expert[:, :], item_cmp[:, :, :], AX.X, ALU.add))
                then(V.tensor_tensor(item_cmp[:, :, :], item_cmp[:, :, :], nblk[:, :].unsqueeze(1).broadcast_to([P, TOP2_TILES, E]),
                                     ALU.mult))
                then(V.tensor_reduce(row[:, :], item_cmp[:, :, :], AX.X, ALU.add))
                then(V.tensor_tensor(row[:, :], items, row[:, :], ALU.subtract))
                V.tensor_scalar(used[:, :], expert[:, :], float(E), None, ALU.is_lt)
                then(V.tensor_scalar(row[:, :], row[:, :], float(SLOTS), float(PAD_ROWS), ALU.mult, ALU.add))
                then(V.scalar_tensor_tensor(row[:, :], expert[:, :], float(REGION), row[:, :], ALU.mult, ALU.add))
                then(V.tensor_tensor(row[:, :], row[:, :], used[:, :], ALU.mult))
                V.tensor_scalar(expert[:, :], expert[:, :], float(E - 1), None, ALU.min)
                then(V.tensor_scalar(used[:, :], used[:, :], -float(SLOTS), float(SLOTS), ALU.mult, ALU.add))
                then(V.tensor_tensor(used[:, :], used[:, :], items, ALU.mult))
                then(V.tensor_tensor(row[:, :], row[:, :], used[:, :], ALU.add))
                then(V.tensor_tensor(shift[:, 1:E + 1], start[:, :], nblk[:, :], ALU.subtract))
                then(V.tensor_scalar(shift[:, 1:E + 1], shift[:, 1:E + 1], float(SLOTS), None, ALU.mult))
                then(V.tensor_tensor(shift[:, 1:E + 1], shift[:, 1:E + 1], start_row[:, :], ALU.subtract))
                then(V.tensor_tensor(shift_step[:, :], shift[:, 1:E + 1], shift[:, 0:E], ALU.subtract))
                for k in range(ks):
                    then(V.tensor_tensor(cand[:, :, :], g.put_row[k][:, :].unsqueeze(2).broadcast_to([P, T, E]),
                                         start_row[:, :].unsqueeze(1).broadcast_to([P, T, E]), ALU.is_ge))
                    then(V.tensor_tensor(cand[:, :, :], cand[:, :, :], shift_step[:, :].unsqueeze(1).broadcast_to([P, T, E]), ALU.mult))
                    then(V.tensor_reduce(scaled[:, :], cand[:, :, :], AX.X, ALU.add))
                    then(V.tensor_tensor(scaled[:, :], scaled[:, :], g.put_row[k][:, :], ALU.add))
                    then(V.tensor_copy(g.get[k][:, :], scaled[:, :]))
                V.tensor_copy(g.tile_row[:, :], row[:, :])
                then(V.tensor_copy(g.tile_expert[:, :], expert[:, :]))
                then(V.tensor_tensor(cand[:, :, :], g.logits[:, :, :], topv[:, :].unsqueeze(2).broadcast_to([P, T, E]), ALU.is_equal))
                then(V.tensor_reduce(second[:, :], cand[:, :, :], AX.X, ALU.add))
                then(V.scalar_tensor_tensor(cand[:, :, :].rearrange("p t e -> p (t e)"), cand[:, :, :].rearrange("p t e -> p (t e)"),
                                            -BIG, g.logits[:, :, :].rearrange("p t e -> p (t e)"), ALU.mult, ALU.add))
                then(V.tensor_reduce(scaled[:, :], cand[:, :, :], AX.X, ALU.max))
                then(V.tensor_tensor(scaled[:, :], scaled[:, :], topv[:, :], ALU.subtract))
                then(V.tensor_scalar(second[:, :], second[:, :], 1.0, None, ALU.is_le))
                V.tensor_tensor(second[:, :], scaled[:, :], second[:, :], ALU.mult).then_inc(shifted, 1)
            dve.wait_ge(soft_ready, ks)
            then(V.tensor_reduce(soft_sum[:, :], soft[:, :, :], AX.X, ALU.add))
            then(V.reciprocal(soft_sum[:, :], soft_sum[:, :]))
            if kind == "gated":
                then(V.tensor_tensor(scaled[:, :], g.keep[:, :], soft_sum[:, :], ALU.mult))
                then(V.tensor_scalar(g.weight[0][:, :], scaled[:, :], gate, None, ALU.mult))
            else:
                then(V.tensor_tensor(second[:, :], second[:, :], soft_sum[:, :], ALU.mult))
                V.tensor_tensor(second[:, :], second[:, :], soft_sum[:, :], ALU.subtract).then_inc(diff_ready, 1)
                dve.wait_ge(diff_exp, 1)
                then(V.tensor_scalar(scaled[:, :], second[:, :], 1.0, None, ALU.add))
                then(V.reciprocal(scaled[:, :], scaled[:, :]))
                then(V.tensor_tensor(second[:, :], second[:, :], scaled[:, :], ALU.mult))
                then(V.tensor_scalar(g.weight[0][:, :], scaled[:, :], gate, None, ALU.mult))
                then(V.tensor_scalar(g.weight[1][:, :], second[:, :], gate, None, ALU.mult))

        @block.scalar
        def _(act):
            if kind == "first":
                return
            act.wait_ge(shifted, 1)
            nc.scalar.activation(soft[:, :, :], soft[:, :, :], ACT.Exp).then_inc(soft_ready, 1)
            if ks == 2:
                act.wait_ge(shifted, 2)
                nc.scalar.activation(second[:, :], second[:, :], ACT.Exp).then_inc(soft_ready, 1)
                act.wait_ge(diff_ready, 1)
                nc.scalar.activation(second[:, :], second[:, :], ACT.Exp).then_inc(diff_exp, 1)

        @block.tensor
        def _(pe):
            if ks == 2:
                ones = g.const_bf[:, C_ONES:C_ONES + P]
                nc.tensor.matmul(TOT[:, :], ones, g.total_by_row[:, :], start=True, stop=True).then_inc(counted, 1)


def combine_and_store(nc, g, rows, out):
    GROUP = 4
    GROUPS = TILES // GROUP
    with ExitStack() as ctx:
        ph = Phase(nc, ctx, "combine")
        got, term = ph.sb("got", [P, 4, GROUP, D]), ph.sb("term", [P, 2, GROUP, D])
        arrived = [ph.sem(f"arrived{k}") for k in range(4)]
        term_done, added, stored = ph.sems("term_done added stored")
        block = ctx.enter_context(nc.Block())
        out_v = out.rearrange("(t p) d -> p t d", p=P)

        def tiles(n):
            return slice(n * GROUP, n * GROUP + GROUP)

        @block.gpsimd
        def _(pool):
            for n in range(GROUPS):
                if n >= 4:
                    pool.wait_ge(term_done, n - 3)
                for tile in range(n * GROUP, n * GROUP + GROUP):
                    pool.indirect_dma_start(got[:, n % 4, tile % GROUP, :], None, rows,
                                            bass.IndirectOffsetOnAxis(ap=g.get[0][:, tile:tile + 1], axis=0),
                                            bounds_check=rows.shape[0] - 1, oob_is_err=False).then_inc(arrived[n % 4], 16)

        @block.vector
        def _(dve):
            for n in range(GROUPS):
                dve.wait_ge(arrived[n % 4], 16 * GROUP * (n // 4 + 1))
                if n >= 2:
                    dve.wait_ge(added, n - 1)
                nc.vector.tensor_tensor(term[:, n % 2, :, :], got[:, n % 4, :, :],
                                        g.weight[0][:, tiles(n)].unsqueeze(2).broadcast_to([P, GROUP, D]), ALU.mult).then_inc(term_done, 1)
                dve.wait_ge(term_done, n + 1)
                nc.vector.tensor_tensor(g.x[:, tiles(n), :], g.x[:, tiles(n), :], term[:, n % 2, :, :], ALU.add).then_inc(added, 1)

        @block.sync
        def _(sp):
            for n in range(GROUPS):
                sp.wait_ge(added, n + 1)
                sp.dma_start(out_v[:, tiles(n), :], g.x[:, tiles(n), :]).then_inc(stored, 16)
            sp.wait_ge(stored, 16 * GROUPS)


def experts(nc, g, name, slots, rows, w1, b1, w2, b2, kind):
    dynamic = kind == "silu"
    ITEMS = TOP2_TILES if dynamic else SLOT_TILES
    DEPTH = 5
    FC = 2 if dynamic else 4
    C = ERF_C if kind == "gelu" else 1.0
    with ExitStack() as ctx:
        ph = Phase(nc, ctx, name)
        xs = ph.sb("xs", [P, 2, SUB, D])
        xs_t = ph.sb("xs_t", [P, 2, SLOTS])
        w1_s, w2_s = ph.sb("w1", [P, 2, 4, P]), ph.sb("w2", [P, 2, FC, D])
        b1_s, b1_scaled, b2_s = ph.sb("b1", [P, 2, 4]), ph.sb("b1_scaled", [P, 2, 4]), ph.sb("b2", [P, 2, D])
        hid = ph.sb("hid", [P, 2, FC, SLOTS])
        act_gate = ph.sb("act_gate", [P, FC, SLOTS])
        y = ph.sb("y", [P, 2, SUB, D])
        X, Y, H = ph.ps("X", [P, 512]), ph.ps("Y", [P, 512]), ph.ps("H", [P, 4, 512])
        go, xt_filled, xt_drained, y_filled, y_drained, b1_ready, hid_ready = ph.sems(
            "go xt_filled xt_drained y_filled y_drained b1_ready hid_ready")
        h_filled = [ph.sem(f"h_filled{c}") for c in range(4)]
        h_drained = [ph.sem(f"h_drained{c}") for c in range(4)]
        gate_ready = [ph.sem(f"gate_ready{c}") for c in range(2)]
        x_in, w1_in, w2_in, stored = ([ph.sem(f"{n}{k}") for k in range(2)] for n in ("x_in", "w1_in", "w2_in", "stored"))
        block = ctx.enter_context(nc.Block())
        w1_v = w1.rearrange("e d (c f) -> e d c f", c=4)
        w2_v = w2.rearrange("e (c f) d -> e f c d", f=P)

        @block.sync
        def _(sp):
            def step(t):
                n2, n3, n4 = t.done(2), t.done(3), t.done(4)
                n5 = t.done(5)

                def expert(s):
                    if dynamic:
                        e = sp.value_load(g.tile_expert[0:1, bass.ds(t.item(s), 1)], min_val=0, max_val=EXPERTS - 1)
                        return [e]
                    return [(t.t - s) // 2 if t.i is None else t.i + (t.t - s) // 2]

                def rows_of(a, s):
                    if dynamic and a is slots:
                        r = sp.value_load(g.tile_row[0:1, bass.ds(t.item(s), 1)], min_val=0, max_val=a.shape[0] - SLOTS)
                        return a[bass.ds(r, SLOTS)].rearrange("(s p) d -> p s d", p=P)
                    return at(a.rearrange("(i s p) d -> i p s d", p=P, s=SUB), t.item(s))

                def at(a, e):
                    return a[bass.ds(e, 1)].rearrange("a p c d -> (a p) c d")

                if t.live(0):
                    src = rows_of(slots, 0)
                    wait(sp, xt_filled, n2)
                    sp.dma_start(xs[:, t.par(0), :, :], src).then_inc(x_in[t.par(0)], 16)
                if t.live(1):
                    e, = expert(1)
                    wait(sp, h_filled[3], n3)
                    if not dynamic:
                        wait(sp, h_drained[3], n3)
                    sp.dma_start(w1_s[:, t.par(1), :, :], at(w1_v, e)).then_inc(w1_in[t.par(1)], 16)
                    if not dynamic:
                        sp.dma_start(b1_s[:, t.par(1), :], b1[bass.ds(e, 1)].rearrange("a f c -> (a f) c")).then_inc(
                            w1_in[t.par(1)], 16)
                if t.live(2):
                    e, = expert(2)
                    wait(sp, y_drained, n4)
                    sp.dma_start(w2_s[:, t.par(2), :, :], at(w2_v, e)).then_inc(w2_in[t.par(2)], 16)
                    if not dynamic:
                        sp.dma_start(b2_s[:, t.par(2), :], b2[bass.ds(e, 1)].partition_broadcast(P)).then_inc(
                            w2_in[t.par(2)], 16)
                if t.live(4):
                    dst = rows_of(rows, 4)
                    wait(sp, y_drained, n4)
                    sp.dma_start(dst, y[:, t.par(4), :, :]).then_inc(stored[t.par(4)], 16)

            pipeline(sp, ITEMS, DEPTH, step)
            for k in range(2):
                sp.wait_ge(stored[k], 16 * ITEMS // 2)

        @block.vector
        def _(dve):
            nc.vector.memset(act_gate[:, :, :], 0.0).then_inc(go, 1)

            def step(t):
                n1, n2, n3 = t.done(1), t.done(2), t.done(3)
                bias_landed = t.landed(2, 1 if dynamic else 2)
                out_bias_landed = t.landed(3, 1 if dynamic else 2)
                kept = t.landed(5)
                if t.live(1):
                    dve.wait_ge(go, 1)
                    wait(dve, xt_filled, n1)
                    nc.vector.tensor_copy(xs_t[:, t.par(1), :], X[:, :]).then_inc(xt_drained, 1)
                if t.live(2) and not dynamic:
                    dve.wait_ge(go, 1)
                    wait(dve, w1_in[t.par(2)], bias_landed)
                    nc.vector.tensor_scalar(b1_scaled[:, t.par(2), :], b1_s[:, t.par(2), :], C, None, ALU.mult).then_inc(b1_ready, 1)
                if t.live(3):
                    dve.wait_ge(go, 1)
                    wait(dve, y_filled, n3)
                    wait(dve, stored[t.par(5)], kept)
                    yv = y[:, t.par(3), :, :]
                    if dynamic:
                        nc.vector.tensor_copy(yv, Y[:, :].rearrange("p (s d) -> p s d", s=SUB)).then_inc(y_drained, 1)
                    else:
                        wait(dve, w2_in[t.par(3)], out_bias_landed)
                        nc.vector.scalar_tensor_tensor(yv, Y[:, :].rearrange("p (s d) -> p s d", s=SUB), 1.0 / C,
                                                       b2_s[:, t.par(3), :].unsqueeze(1).broadcast_to([P, SUB, D]),
                                                       ALU.mult, ALU.add).then_inc(y_drained, 1)
                if t.live(2) and dynamic:
                    for c in range(FC):
                        dve.wait_ge(go, 1)
                        wait(dve, gate_ready[c], n2)
                        wait(dve, h_filled[c + 2], n2)
                        nc.vector.tensor_tensor(hid[:, t.par(2), c, :], act_gate[:, c, :], H[:, c + 2, :], ALU.mult).then_inc(
                            h_drained[c + 2], 1)

            pipeline(dve, ITEMS, DEPTH, step)

        @block.scalar
        def _(act):
            def step(t):
                n2, n3 = t.done(2), t.done(3)
                if t.live(2):
                    for c in range(FC):
                        act.wait_ge(go, 1)
                        wait(act, h_filled[c], n2)
                        if dynamic:
                            wait(act, h_drained[c + 2], n3)
                            nc.scalar.activation(act_gate[:, c, :], H[:, c, :], ACT.Silu).then_inc(gate_ready[c], 1)
                        else:
                            wait(act, b1_ready, n2)
                            nc.scalar.activation(hid[:, t.par(2), c, :], H[:, c, :], ACT.Gelu if kind == "gelu" else ACT.Relu,
                                                 bias=b1_scaled[:, t.par(2), c:c + 1], scale=C).then_inc(h_drained[c], 1)

            pipeline(act, ITEMS, DEPTH, step)

        @block.tensor
        def _(pe):
            def step(t):
                n1, n2, n3, n4 = (t.done(s) for s in range(1, 5))
                x_landed = t.landed(1)
                w1_landed = t.landed(2, 1 if dynamic else 2)
                w2_landed = t.landed(3, 1 if dynamic else 2)
                if t.live(2):
                    for c in range(4):
                        pe.wait_ge(go, 1)
                        if c == 0:
                            wait(pe, xt_drained, n2)
                            wait(pe, w1_in[t.par(2)], w1_landed)
                        wait(pe, gate_ready[c] if dynamic and c < 2 else h_drained[c], n3)
                        nc.tensor.matmul(H[:, c, :], w1_s[:, t.par(2), c, :], xs_t[:, t.par(2), :],
                                         start=True, stop=True).then_inc(h_filled[c], 1)
                if t.live(1):
                    pe.wait_ge(go, 1)
                    wait(pe, x_in[t.par(1)], x_landed)
                    wait(pe, xt_drained, n2)
                    for k in range(SUB):
                        last = nc.tensor.transpose(X[:, P * k:P * k + P], xs[:, t.par(1), k, :], g.const[:, C_IDENT:C_IDENT + P])
                    last.then_inc(xt_filled, 1)
                if t.live(3):
                    pe.wait_ge(go, 1)
                    for c in range(FC):
                        wait(pe, h_drained[c + (2 if dynamic else 0)], n3)
                    wait(pe, w2_in[t.par(3)], w2_landed)
                    wait(pe, y_drained, n4)
                    for k in range(SUB):
                        for c in range(FC):
                            last = nc.tensor.matmul(Y[:, P * k:P * k + P], hid[:, t.par(3), c, P * k:P * k + P],
                                                    w2_s[:, t.par(3), c, :], start=c == 0, stop=c == FC - 1)
                    last.then_inc(y_filled, 1)

            pipeline(pe, ITEMS, DEPTH, step)



def bitlinear_ffn(nc, g, t_in):
    ITEMS, DEPTH, UNROLL = TILES // 2, 11, 4
    gate_col = 5
    with ExitStack() as ctx:
        ph = Phase(nc, ctx, "bit")
        w_raw = [ph.sb("w1_raw", [P, FF]), ph.sb("w2_raw", [P, FF])]
        w_q = [ph.sb("w1_q", [P, FF], BF16), ph.sb("w2_q", [P, FF], BF16)]
        b1_s, b2_s = ph.sb("b1", [P, FF]), ph.sb("b2", [P, D])
        w_sum, w_scale, w_inv = ph.sb("w_sum", [P, 2]), ph.sb("w_scale", [P, 2, 2]), ph.sb("w_inv", [P, 2])
        w_round = ph.sb("w_round", [P, FF])
        neg_one, magic = ph.sb("neg_one", [P, 2]), ph.sb("magic", [P, 1])
        st, mv = ph.sb("st", [P, 2, 2, 6]), ph.sb("mv", [P, 2, 2, 2])
        var_eps, rstd = ph.sb("var_eps", [P, 2, 2]), ph.sb("rstd", [P, 2, 2])
        xn, hid = ph.sb("xn", [P, 4, 2, D]), ph.sb("hid", [P, 4, 2, FF])
        ssq, big = ph.sb("ssq", [P, 2, 4, 2]), ph.sb("big", [P, 2, 4, 2])
        root, unit, inv = ph.sb("root", [P, 2, 2]), ph.sb("unit", [P, 2, 2]), ph.sb("inv", [P, 2, 2])
        mult, deq = ph.sb("mult", [P, 2, 4, 2]), ph.sb("deq", [P, 2, 4, 2])
        x_square, h_square = ph.sb("x_square", [P, 2, D]), ph.sb("h_square", [P, 2, FF])
        x_round, h_round = ph.sb("x_round", [P, 2, D]), ph.sb("h_round", [P, 2, FF])
        xq, xq_t = ph.sb("xq", [P, 2, 2, D], BF16), ph.sb("xq_t", [P, 2, 2, P], BF16)
        hq, hq_t = ph.sb("hq", [P, 2, 2, FF], BF16), ph.sb("hq_t", [P, 2, 8, P], BF16)
        pre, term = ph.sb("pre", [P, 2, 2, FF]), ph.sb("term", [P, 2, D])
        XT, H = ph.ps("XT", [P, 1024], BF16), ph.ps("H", [P, 2, FF])
        HT, Y, W = ph.ps("HT", [P, 8, P], BF16), ph.ps("Y", [P, 512]), ph.ps("W", [P, 512])
        (weights_in, chained, w_summed, w_totalled, ready, stats_part, stats_done, eps_done, rstd_done, xn_done,
         x_big, x_ssq, pooled, x_scaled, x_rounded, xq_done, xt_filled, xt_drained, h_filled, h_read,
         hid_done, h_big, h_ssq, h_scaled, h_rounded, hq_done, ht_filled, ht_drained, y_filled, y_read, y_added) = ph.sems(
            "weights_in chained w_summed w_totalled ready stats_part stats_done eps_done rstd_done xn_done "
            "x_big x_ssq pooled x_scaled x_rounded xq_done xt_filled xt_drained h_filled h_read "
            "hid_done h_big h_ssq h_scaled h_rounded hq_done ht_filled ht_drained y_filled y_read y_added")
        block = ctx.enter_context(nc.Block())
        V = nc.vector

        @block.sync
        def _(sp):
            sp.dma_start(w_raw[0][:, :], t_in["B_w1"]).then_inc(weights_in, 16)
            sp.dma_start(w_raw[1][:, :].rearrange("p (c d) -> p c d", c=4), t_in["B_w2"].rearrange("(c p) d -> p c d", p=P)).then_inc(
                weights_in, 16)
            sp.dma_start(b1_s[:, :], t_in["B_b1"].partition_broadcast(P)).then_inc(weights_in, 16)
            sp.dma_start(b2_s[:, :], t_in["B_b2"].partition_broadcast(P)).then_inc(weights_in, 16)

        @block.gpsimd
        def _(pool):
            def step(t):
                n0 = t.done(0)
                if t.i is None:
                    links = 6 * (max(0, min(t.t - 2, ITEMS)) + max(0, min(t.t - 7, ITEMS)))

                def at(k):
                    if t.i is None:
                        return links + k
                    return pool.to_reg(t.i * (12 * UNROLL) + 6 * (t.t - 2 + t.t - 7) + k)

                marks = [at(k) for k in range(1, 13)]
                used = [0]

                def scales(n, s, width, sums, largest, finished, used_by):
                    b, before = t.par(s, 4), t.done(s + 4)
                    now = t.done(s)
                    pool.wait_ge(ready, 1)
                    wait(pool, sums, now)
                    wait(pool, largest, now)
                    wait(pool, used_by, before)

                    def then(ins):
                        ins.then_inc(pooled, 1)
                        pool.wait_ge(ready, 1)
                        pool.wait_ge(pooled, marks[used[0]])
                        used[0] += 1

                    G_ = nc.gpsimd
                    then(G_.tensor_scalar(root[:, n, :], ssq[:, n, b, :], 1.0 / width, LN_EPS, ALU.mult, ALU.add))
                    then(G_.tensor_tensor(root[:, n, :], root[:, n, :], g.neg_half[:, 0:2], ALU.pow))
                    then(G_.tensor_tensor(unit[:, n, :], big[:, n, b, :], root[:, n, :], ALU.mult))
                    then(G_.tensor_scalar(unit[:, n, :], unit[:, n, :], 1e-5, 1.0 / 127.0, ALU.max, ALU.mult))
                    then(G_.tensor_tensor(inv[:, n, :], unit[:, n, :], neg_one[:, :], ALU.pow))
                    then(G_.tensor_tensor(mult[:, n, b, :], root[:, n, :], inv[:, n, :], ALU.mult))
                    G_.tensor_tensor(deq[:, n, b, :], unit[:, n, :], w_scale[:, n, :], ALU.mult).then_inc(finished, 1)

                if t.live(2):
                    scales(0, 2, D, x_ssq, x_big, x_scaled, h_read)
                if t.live(7):
                    scales(1, 7, FF, h_ssq, h_big, h_scaled, y_read)
                if t.live(0):
                    pool.wait_ge(ready, 1)
                    wait(pool, stats_done, n0)
                    nc.gpsimd.tensor_tensor(var_eps[:, t.par(0), :], mv[:, t.par(0), :, 1], g.eps[:, 0:2], ALU.add).then_inc(eps_done, 1)
                    pool.wait_ge(ready, 1)
                    wait(pool, eps_done, n0)
                    nc.gpsimd.tensor_tensor(rstd[:, t.par(0), :], var_eps[:, t.par(0), :], g.neg_half[:, 0:2],
                                            ALU.pow).then_inc(rstd_done, 1)

            pipeline(pool, ITEMS, DEPTH, step, UNROLL)

        @block.vector
        def _(dve):
            done = [0]

            def then(ins):
                done[0] += 1
                ins.then_inc(chained, 1)
                dve.wait_ge(chained, done[0])

            V.memset(neg_one[:, :], -1.0)
            V.memset(magic[:, :], MAGIC)
            dve.wait_ge(weights_in, 64)
            for n in range(2):
                last = V.tensor_reduce(w_sum[:, n:n + 1], w_raw[n][:, :], AX.X, ALU.add, apply_absolute_value=True)
            last.then_inc(w_summed, 1)
            dve.wait_ge(w_totalled, 1)
            for k in range(2):
                last = V.tensor_scalar(w_scale[:, :, k], W[:, 0:2], 1.0 / (D * FF), 1e-5, ALU.mult, ALU.max)
            then(last)
            then(V.reciprocal(w_inv[:, :], w_scale[:, :, 0]))
            for n in range(2):
                then(V.tensor_scalar(w_round[:, :], w_raw[n][:, :], w_inv[:, n:n + 1], None, ALU.mult))
                then(V.tensor_scalar(w_round[:, :], w_round[:, :], MAGIC, -MAGIC, ALU.add, ALU.add))
                then(V.tensor_scalar(w_q[n][:, :], w_round[:, :], 1.0, -1.0, ALU.min, ALU.max))
            then(V.tensor_scalar(w_scale[:, 1, :], w_scale[:, 1, :], g.gate[:, gate_col:gate_col + 1], None, ALU.mult))
            V.tensor_scalar(b2_s[:, :], b2_s[:, :], g.gate[:, gate_col:gate_col + 1], None, ALU.mult).then_inc(ready, 1)
            dve.wait_ge(ready, 1)

            def step(t):
                n0, n1, n3, n4, n5, n7, n8, n10, n11 = (t.done(s) for s in (0, 1, 3, 4, 5, 7, 8, 10, 11))
                if t.live(1):
                    dve.wait_ge(ready, 1)
                    wait(dve, rstd_done, n1)
                    for k in range(2):
                        last = V.tensor_scalar(xn[:, t.par(1, 4), k, :].unsqueeze(1), g.x[:, bass.ds(t.item(1) * 2 + k, 1), :],
                                               mv[:, t.par(1), k, 0:1], rstd[:, t.par(1), k:k + 1], ALU.subtract, ALU.mult)
                    last.then_inc(xn_done, 1)
                if t.live(0):
                    for k in range(2):
                        last = V.bn_stats(st[:, t.par(0), k, :], g.x[:, bass.ds(t.item(0) * 2 + k, 1), :])
                    last.then_inc(stats_part, 1)
                if t.live(1):
                    dve.wait_ge(ready, 1)
                    wait(dve, xn_done, n1)
                    V.tensor_reduce(big[:, 0, t.par(1, 4), :], xn[:, t.par(1, 4), :, :], AX.X, ALU.max,
                                    apply_absolute_value=True).then_inc(x_big, 1)
                if t.live(0):
                    dve.wait_ge(ready, 1)
                    wait(dve, stats_part, n0)
                    for k in range(2):
                        last = V.bn_aggr(mv[:, t.par(0), k, :], st[:, t.par(0), k, :])
                    last.then_inc(stats_done, 1)
                if t.live(7):
                    dve.wait_ge(ready, 1)
                    wait(dve, hid_done, n7)
                    V.tensor_reduce(big[:, 1, t.par(7, 4), :], hid[:, t.par(7, 4), :, :], AX.X, ALU.max,
                                    apply_absolute_value=True).then_inc(h_big, 1)
                if t.live(3):
                    dve.wait_ge(ready, 1)
                    wait(dve, x_rounded, n3)
                    wait(dve, xt_filled, n5)
                    V.tensor_scalar(xq[:, t.par(3), :, :], x_round[:, :, :], -MAGIC, None, ALU.add).then_inc(xq_done, 1)
                if t.live(4):
                    dve.wait_ge(ready, 1)
                    wait(dve, xt_filled, n4)
                    V.tensor_copy(xq_t[:, t.par(4), :, :], XT[:, 0:256].rearrange("p (k n) -> p k n", k=2)).then_inc(xt_drained, 1)
                if t.live(10):
                    dve.wait_ge(ready, 1)
                    wait(dve, y_filled, n10)
                    wait(dve, y_added, n11)
                    for k in range(2):
                        last = V.scalar_tensor_tensor(term[:, k, :], Y[:, P * k:P * k + P], deq[:, 1, t.par(10, 4), k:k + 1],
                                                      b2_s[:, :], ALU.mult, ALU.add)
                    last.then_inc(y_read, 1)
                    dve.wait_ge(ready, 1)
                    wait(dve, y_read, n10)
                    xs = g.x[:, bass.ds(t.item(10) * 2, 2), :]
                    V.tensor_tensor(xs, xs, term[:, :, :], ALU.add).then_inc(y_added, 1)
                if t.live(8):
                    dve.wait_ge(ready, 1)
                    wait(dve, h_rounded, n8)
                    wait(dve, ht_filled, n10)
                    V.tensor_scalar(hq[:, t.par(8), :, :], h_round[:, :, :], -MAGIC, None, ALU.add).then_inc(hq_done, 1)
                if t.live(5):
                    dve.wait_ge(ready, 1)
                    wait(dve, h_filled, n5)
                    wait(dve, hid_done, n7)
                    for k in range(2):
                        last = V.scalar_tensor_tensor(pre[:, t.par(5), k, :], H[:, k, :], deq[:, 0, t.par(5, 4), k:k + 1],
                                                      b1_s[:, :], ALU.mult, ALU.add)
                    last.then_inc(h_read, 1)

            pipeline(dve, ITEMS, DEPTH, step, UNROLL)

        @block.scalar
        def _(act):
            def step(t):
                n2, n3, n4, n6, n7, n8, n9 = (t.done(s) for s in (2, 3, 4, 6, 7, 8, 9))
                if t.live(2):
                    act.wait_ge(ready, 1)
                    wait(act, xn_done, n2)
                    wait(act, x_ssq, n3)
                    for k in range(2):
                        last = nc.scalar.activation(x_square[:, k, :], xn[:, t.par(2, 4), k, :], ACT.Square,
                                                    accum_out=ssq[:, 0, t.par(2, 4), k:k + 1])
                    last.then_inc(x_ssq, 1)
                if t.live(6):
                    act.wait_ge(ready, 1)
                    wait(act, h_read, n6)
                    nc.scalar.activation(hid[:, t.par(6, 4), :, :], pre[:, t.par(6), :, :], ACT.Gelu).then_inc(hid_done, 1)
                if t.live(3):
                    act.wait_ge(ready, 1)
                    wait(act, x_scaled, n3)
                    wait(act, xq_done, n4)
                    for k in range(2):
                        last = nc.scalar.activation(x_round[:, k, :], xn[:, t.par(3, 4), k, :], ACT.Identity, bias=magic[:, :],
                                                    scale=mult[:, 0, t.par(3, 4), k:k + 1])
                    last.then_inc(x_rounded, 1)
                if t.live(9):
                    act.wait_ge(ready, 1)
                    wait(act, ht_filled, n9)
                    nc.scalar.copy(hq_t[:, t.par(9), :, :], HT[:, :, :]).then_inc(ht_drained, 1)
                if t.live(7):
                    act.wait_ge(ready, 1)
                    wait(act, hid_done, n7)
                    wait(act, h_ssq, n8)
                    for k in range(2):
                        last = nc.scalar.activation(h_square[:, k, :], hid[:, t.par(7, 4), k, :], ACT.Square,
                                                    accum_out=ssq[:, 1, t.par(7, 4), k:k + 1])
                    last.then_inc(h_ssq, 1)
                if t.live(8):
                    act.wait_ge(ready, 1)
                    wait(act, h_scaled, n8)
                    wait(act, hq_done, n9)
                    for k in range(2):
                        last = nc.scalar.activation(h_round[:, k, :], hid[:, t.par(8, 4), k, :], ACT.Identity, bias=magic[:, :],
                                                    scale=mult[:, 1, t.par(8, 4), k:k + 1])
                    last.then_inc(h_rounded, 1)

            pipeline(act, ITEMS, DEPTH, step, UNROLL)

        @block.tensor
        def _(pe):
            pe.wait_ge(w_summed, 1)
            nc.tensor.matmul(W[:, 0:2], g.const[:, C_ONES:C_ONES + P], w_sum[:, :], start=True, stop=True).then_inc(w_totalled, 1)
            ident = g.const_bf[:, C_IDENT:C_IDENT + P]

            def step(t):
                n4, n5, n6, n9, n10, n11 = (t.done(s) for s in (4, 5, 6, 9, 10, 11))
                if t.live(4):
                    pe.wait_ge(ready, 1)
                    wait(pe, xq_done, n4)
                    wait(pe, xt_drained, n5)
                    for k in range(2):
                        last = nc.tensor.transpose(XT[:, P * k:P * k + P], xq[:, t.par(4), k, :], ident)
                    last.then_inc(xt_filled, 1)
                if t.live(5):
                    pe.wait_ge(ready, 1)
                    wait(pe, xt_drained, n5)
                    wait(pe, h_read, n6)
                    for k in range(2):
                        last = nc.tensor.matmul(H[:, k, :], xq_t[:, t.par(5), k, :], w_q[0][:, :], start=True, stop=True)
                    last.then_inc(h_filled, 1)
                if t.live(9):
                    pe.wait_ge(ready, 1)
                    wait(pe, hq_done, n9)
                    wait(pe, ht_drained, n10)
                    for k in range(8):
                        last = nc.tensor.transpose(HT[:, k, :], hq[:, t.par(9), k // 4, P * (k % 4):P * (k % 4) + P], ident)
                    last.then_inc(ht_filled, 1)
                if t.live(10):
                    pe.wait_ge(ready, 1)
                    wait(pe, ht_drained, n10)
                    wait(pe, y_read, n11)
                    for k in range(8):
                        last = nc.tensor.matmul(Y[:, P * (k // 4):P * (k // 4) + P], hq_t[:, t.par(10), k, :],
                                                w_q[1][:, P * (k % 4):P * (k % 4) + P], start=k % 4 == 0, stop=k % 4 == 3)
                    last.then_inc(y_filled, 1)

            pipeline(pe, ITEMS, DEPTH, step, UNROLL)



class G:
    pass


def build(nc, t, out):
    with ExitStack() as ctx:
        g = G()
        g.x = ctx.enter_context(nc.sbuf_tensor("x_stream", [P, TILES, D], F32))
        g.const = ctx.enter_context(nc.sbuf_tensor("const_table", [P, C_COLS], F32))
        g.const_bf = ctx.enter_context(nc.sbuf_tensor("const_bf", [P, 384], BF16))
        g.gate = ctx.enter_context(nc.sbuf_tensor("gates", [P, 8], F32))
        g.neg_half = ctx.enter_context(nc.sbuf_tensor("neg_half", [P, 8], F32))
        g.eps = ctx.enter_context(nc.sbuf_tensor("eps", [P, 8], F32))
        g.ctx_t = t["ctx_t"]
        g.slots = nc.dram_tensor("slots", [PAD_ROWS + EXPERTS * REGION, D], F32).ap()
        load_inputs(nc, g, t)
        def sb(name, shape, dt=F32):
            return ctx.enter_context(nc.sbuf_tensor(name, shape, dt))

        g.xn, g.logits = sb("xn_all", [P, TILES, D]), sb("logits", [P, TILES, EXPERTS])
        g.get = [sb(f"get{k}", [P, TILES], U32) for k in range(2)]
        g.weight = [sb(f"weight{k}", [P, TILES]) for k in range(2)]
        g.put = [sb(f"put{k}", [P, TILES], U32) for k in range(2)]
        g.keep, g.put_row = sb("keep", [P, TILES]), [sb(f"put_row{k}", [P, TILES]) for k in range(2)]
        g.tile_expert, g.tile_row = sb("tile_expert", [P, TOP2_TILES], I32), sb("tile_row", [P, TOP2_TILES], I32)
        g.total_by_row = sb("total_by_row", [P, EXPERTS], BF16)

        def moe(n, slots, kind, act_kind, col):
            rows = nc.dram_tensor(f"rows{n}", [PAD_ROWS if kind == "top2" else TOKENS, D], F32).ap()
            weigh(nc, g, f"weigh{n}", kind, col)
            experts(nc, g, f"experts{n}", slots, rows, t[f"F{n}_w1"], t.get(f"F{n}_b1"), t[f"F{n}_w2"], t.get(f"F{n}_b2"), act_kind)
            return rows

        first_rows = g.slots[0:TOKENS]
        attention_wide(nc, g, t, (t["F0_wg"], t["F0_bg"], "first", first_rows))
        rows0 = moe(0, first_rows, "first", "gelu", 4)
        attention_narrow(nc, g, "l1", 1, t["L1_wq"], t["L1_bq"], t["L1_wk"], t["L1_bk"], t["L1_wv"], t["L1_bv"],
                         t["L1_wo"], t["L1_bo"], "softmax", head=(rows0, 1, True))
        bitlinear_ffn(nc, g, t)
        attention_narrow(nc, g, "l2", 2, t["L2_wq"], t["L2_bq"], t["L2_wk"], t["L2_bk"], t["L2_wv"], t["L2_bv"],
                         t["L2_wo"], t["L2_bo"], "masked", t["mask"], tail=(t["F2_wg"], None, "top2", g.slots))
        rows2 = moe(2, g.slots, "top2", "silu", 6)
        attention_narrow(nc, g, "l3", 3, t["L3_wq"], t["L3_bq"], t["L3_wk"], t["L3_bk"], t["L3_wv"], t["L3_bv"],
                         t["L3_wo"], t["L3_bo"], "stable", head=(rows2, 2, False), tail=(t["F3_wg"], None, "gated", first_rows))
        rows3 = moe(3, first_rows, "gated", "relu", 7)
        combine_and_store(nc, g, rows3, out)


def lay_out(a):
    o = {"x": a["x"].reshape(TOKENS, D), "ctx_t": a["ctx_1024"].reshape(TOKENS, D).T,
         "g_xattn": a["g_xattn"], "g_ffn": a["g_ffn"], "consts": constants()}
    o["mask"] = a["mask_BxSxS2_bf1"].view(np.uint8).reshape(TILES, P, SEQ).transpose(1, 0, 2)

    def halves(w):
        r = w.reshape(w.shape[0], 8, 2, -1)
        return r.transpose(0, 2, 1, 3).reshape(w.shape[0], 2, -1)

    for n, p, tr in (("L1", "L1_xattn_w", True), ("L2", "L2_xattn_W", False), ("L3", "L3_xattn_W", True)):
        for m in "qkvo":
            w = a[p + m]
            w = w.T if tr else w
            o[f"{n}_w{m}"] = halves(w) if m == "v" else w
            b = a[f"{n}_xattn_b{m}"]
            o[f"{n}_b{m}"] = {"v": halves(b[None])[0], "o": b[None]}.get(m, b[:, None])
    o["L0_wq"], o["L0_wk"], o["L0_wo"] = a["L0_xattn_Wq"], a["L0_xattn_Wk"], a["L0_xattn_Wo"]
    o["L0_wv"] = halves(a["L0_xattn_Wv"])
    o["F0_wg"], o["F0_bg"] = a["L0_ffn_W_sw"].T, a["L0_ffn_b_sw"]
    o["F3_wg"], o["F2_wg"] = a["L3_ffn_Wg"].T, a["L2_ffn_router_kernel_DE"].T
    for n in (0, 3):
        for m in ("W1", "b1", "W2", "b2"):
            o[f"F{n}_{m.lower()}"] = a[f"L{n}_ffn_{m}"]
        o[f"F{n}_b1"] = o[f"F{n}_b1"].reshape(EXPERTS, 4, P).transpose(0, 2, 1)
    o["F2_w1"] = np.concatenate([a["L2_ffn_kernel_gating_EDF"], a["L2_ffn_kernel_up_EDF"]], axis=2)
    o["F2_w2"] = a["L2_ffn_kernel_down_EFD"]
    o["B_w1"], o["B_w2"] = a["L1_ffn_w1"].T, a["L1_ffn_w2"].T
    o["B_b1"], o["B_b2"] = a["L1_ffn_b1"], a["L1_ffn_b2"]
    o["L2_wo"] = a["L2_xattn_Wo"].reshape(2, 64, D).transpose(1, 0, 2)
    return {k: np.ascontiguousarray(v) for k, v in o.items()}


def kernel(**inputs):
    import numpy as _np
    import concourse.bacc as _bacc
    from concourse import mybir as _mybir
    from concourse.bass_utils import run_bass_kernel_spmd as _run

    nc = _bacc.Bacc("TRN2", target_bir_lowering=False, num_devices=1)
    arrays = lay_out({k: _np.asarray(v) for k, v in inputs.items()})
    t = {k: nc.dram_tensor("in_" + k, v.shape, _mybir.dt.from_np(v.dtype), kind="ExternalInput").ap()
         for k, v in arrays.items()}
    out = nc.dram_tensor("out", [TOKENS, D], F32, kind="ExternalOutput").ap()
    build(nc, t, out)
    r = _run(nc, [{"in_" + k: v for k, v in arrays.items()}], core_ids=[0])
    return r.results[0]["out"].reshape(BATCH, SEQ, D)
```
